# Optimizing a Trainium2 kernel written in Bass

```python
import numpy as np
import jax
import jax.numpy as jnp

def _softmax(x, axis=-1):
    return jax.nn.softmax(x, axis=axis)

def _gelu(x):
    return jax.nn.gelu(x, approximate=True)

def _silu(x):
    return jax.nn.silu(x)

def _sigmoid(x):
    return jax.nn.sigmoid(x)

def _layernorm(x, axis=-1, eps=1e-05):
    m = jnp.mean(x, axis=axis, keepdims=True)
    v = jnp.var(x, axis=axis, keepdims=True)
    return (x - m) / jnp.sqrt(v + eps)

def _scatter_add(tgt, idx, src, axis=0):
    return tgt.at[idx].add(src)

def _segment_sum(src, seg, n):
    return jax.ops.segment_sum(src, seg, n)
kernel_name = 'mk_hybrid_d1_jaxref_r8_ef56fd'

def setup_inputs(seed: int=0):
    np.random.seed(seed)
    _w = jnp.asarray

    def _L0_attn_a_setup():
        import jax, jax.numpy as jnp
        import numpy as np
        import math
        B, T, C, H, K = (2, 512, 256, 16, 4)
        D = C // H

        def _ln(t, g, b, eps=1e-05):
            m = t.mean(-1, keepdims=True)
            v = t.var(-1, keepdims=True)
            return (t - m) / jnp.sqrt(v + eps) * g + b

        def _l2n(t, eps=1e-12):
            return t / jnp.maximum(jnp.linalg.norm(t, axis=-1, keepdims=True), eps)
        key = jax.random.key(seed)
        ks = jax.random.split(key, 16)
        s = 0.02
        target = 1.0 - np.exp(np.linspace(math.log(1 - 0.9), math.log(1 - 0.999), H))
        gamma_b = jnp.asarray(np.log(target / (1 - target)), dtype=jnp.float32)
        inp = {'x': jax.random.normal(ks[0], (B, T, C), jnp.float32), 'Wq': jax.random.normal(ks[1], (C, C), jnp.float32) * s, 'Wk': jax.random.normal(ks[2], (C, C), jnp.float32) * s, 'Wv': jax.random.normal(ks[3], (C, C), jnp.float32) * s, 'Wo': jax.random.normal(ks[4], (C, C), jnp.float32) * s, 'conv_w': jax.random.normal(ks[5], (C, 1, K), jnp.float32) * s, 'conv_b': jnp.zeros((C,), jnp.float32), 'ig_w': jax.random.normal(ks[6], (C, C), jnp.float32) * s, 'ig_b': jnp.full((C,), -3.0, jnp.float32), 'og_w': jax.random.normal(ks[7], (C, C), jnp.float32) * s, 'og_b': jnp.zeros((C,), jnp.float32), 'gamma_w': jax.random.normal(ks[8], (H, C), jnp.float32) * (s * 0.1), 'gamma_b': gamma_b, 'vn_g': jnp.ones((D,), jnp.float32), 'vn_b': jnp.zeros((D,), jnp.float32), 'gn_g': jnp.ones((C,), jnp.float32), 'gn_b': jnp.zeros((C,), jnp.float32), 'mn_g': jnp.ones((D,), jnp.float32), 'mn_b': jnp.zeros((D,), jnp.float32)}
        return inp
    _L0_attn_a_in = _L0_attn_a_setup()

    def _L0_attn_b_setup():
        import jax, jax.numpy as jnp
        import numpy as np
        import math
        N_Q = 128
        N_K = 128
        N_V = 128
        D_MODEL = 256
        N_HEADS = 16
        B, T = (8, 512)
        key = jax.random.key(seed)
        ks = jax.random.split(key, 9)
        s = 0.02
        return {'x': jax.random.normal(ks[0], (B, T, D_MODEL), dtype=jnp.float32), 'Wq': jax.random.normal(ks[1], (D_MODEL, N_Q * N_HEADS), dtype=jnp.float32) * s, 'bq': jnp.zeros((N_Q * N_HEADS,), dtype=jnp.float32), 'Wk': jax.random.normal(ks[2], (D_MODEL, N_K * N_HEADS), dtype=jnp.float32) * s, 'bk': jnp.zeros((N_K * N_HEADS,), dtype=jnp.float32), 'Wv': jax.random.normal(ks[3], (D_MODEL, N_V * N_HEADS), dtype=jnp.float32) * s, 'bv': jnp.zeros((N_V * N_HEADS,), dtype=jnp.float32), 'Wo': jax.random.normal(ks[4], (N_V * N_HEADS, D_MODEL), dtype=jnp.float32) * s, 'bo': jnp.zeros((D_MODEL,), dtype=jnp.float32)}
    _L0_attn_b_in = _L0_attn_b_setup()

    def _L0_ffn_setup():
        import jax, jax.numpy as jnp
        import numpy as np
        HIDDEN = 256
        INTER = 704
        B, S = (2, 256)

        def _ternary(key, shape):
            return jax.random.randint(key, shape, -1, 2).astype(jnp.float32)
        key = jax.random.key(seed)
        ks = jax.random.split(key, 7)
        x = jax.random.normal(ks[0], (B, S, HIDDEN), dtype=jnp.float32)
        gate_w = _ternary(ks[1], (INTER, HIDDEN))
        up_w = _ternary(ks[2], (INTER, HIDDEN))
        down_w = _ternary(ks[3], (HIDDEN, INTER))
        gate_s = jax.random.uniform(ks[4], (INTER,), minval=0.01, maxval=0.1, dtype=jnp.float32)
        up_s = jax.random.uniform(ks[5], (INTER,), minval=0.01, maxval=0.1, dtype=jnp.float32)
        down_s = jax.random.uniform(ks[6], (HIDDEN,), minval=0.01, maxval=0.1, dtype=jnp.float32)
        return {'x': x, 'gate_w': gate_w, 'up_w': up_w, 'down_w': down_w, 'gate_s': gate_s, 'up_s': up_s, 'down_s': down_s}
    _L0_ffn_in = _L0_ffn_setup()
    _d = {'L0_attn_a_x': _L0_attn_a_in['x'], 'L0_attn_a_Wq': _L0_attn_a_in['Wq'], 'L0_attn_a_Wk': _L0_attn_a_in['Wk'], 'L0_attn_a_Wv': _L0_attn_a_in['Wv'], 'L0_attn_a_Wo': _L0_attn_a_in['Wo'], 'L0_attn_a_conv_w': _L0_attn_a_in['conv_w'], 'L0_attn_a_conv_b': _L0_attn_a_in['conv_b'], 'L0_attn_a_ig_w': _L0_attn_a_in['ig_w'], 'L0_attn_a_ig_b': _L0_attn_a_in['ig_b'], 'L0_attn_a_og_w': _L0_attn_a_in['og_w'], 'L0_attn_a_og_b': _L0_attn_a_in['og_b'], 'L0_attn_a_gamma_w': _L0_attn_a_in['gamma_w'], 'L0_attn_a_gamma_b': _L0_attn_a_in['gamma_b'], 'L0_attn_a_vn_g': _L0_attn_a_in['vn_g'], 'L0_attn_a_vn_b': _L0_attn_a_in['vn_b'], 'L0_attn_a_gn_g': _L0_attn_a_in['gn_g'], 'L0_attn_a_gn_b': _L0_attn_a_in['gn_b'], 'L0_attn_a_mn_g': _L0_attn_a_in['mn_g'], 'L0_attn_a_mn_b': _L0_attn_a_in['mn_b'], 'L0_attn_b_Wq': _L0_attn_b_in['Wq'], 'L0_attn_b_bq': _L0_attn_b_in['bq'], 'L0_attn_b_Wk': _L0_attn_b_in['Wk'], 'L0_attn_b_bk': _L0_attn_b_in['bk'], 'L0_attn_b_Wv': _L0_attn_b_in['Wv'], 'L0_attn_b_bv': _L0_attn_b_in['bv'], 'L0_attn_b_Wo': _L0_attn_b_in['Wo'], 'L0_attn_b_bo': _L0_attn_b_in['bo'], 'L0_ffn_gate_w': _L0_ffn_in['gate_w'], 'L0_ffn_up_w': _L0_ffn_in['up_w'], 'L0_ffn_down_w': _L0_ffn_in['down_w'], 'L0_ffn_gate_s': _L0_ffn_in['gate_s'], 'L0_ffn_up_s': _L0_ffn_in['up_s'], 'L0_ffn_down_s': _L0_ffn_in['down_s']}
    _x0 = _d['L0_attn_a_x']
    _d['L0_attn_a_x'] = jax.random.normal(jax.random.fold_in(jax.random.key(seed), 1), (4, 256, 256), dtype=_x0.dtype)
    del _x0
    return _d

def reference(L0_attn_a_x, L0_attn_a_Wq, L0_attn_a_Wk, L0_attn_a_Wv, L0_attn_a_Wo, L0_attn_a_conv_w, L0_attn_a_conv_b, L0_attn_a_ig_w, L0_attn_a_ig_b, L0_attn_a_og_w, L0_attn_a_og_b, L0_attn_a_gamma_w, L0_attn_a_gamma_b, L0_attn_a_vn_g, L0_attn_a_vn_b, L0_attn_a_gn_g, L0_attn_a_gn_b, L0_attn_a_mn_g, L0_attn_a_mn_b, L0_attn_b_Wq, L0_attn_b_bq, L0_attn_b_Wk, L0_attn_b_bk, L0_attn_b_Wv, L0_attn_b_bv, L0_attn_b_Wo, L0_attn_b_bo, L0_ffn_gate_w, L0_ffn_up_w, L0_ffn_down_w, L0_ffn_gate_s, L0_ffn_up_s, L0_ffn_down_s):

    def _L0_attn_a_ref(x, Wq, Wk, Wv, Wo, conv_w, conv_b, ig_w, ig_b, og_w, og_b, gamma_w, gamma_b, vn_g, vn_b, gn_g, gn_b, mn_g, mn_b):
        import jax, jax.numpy as jnp
        import numpy as np
        import math
        B, T, C, H, K = (2, 512, 256, 16, 4)
        D = C // H

        def _ln(t, g, b, eps=1e-05):
            m = t.mean(-1, keepdims=True)
            v = t.var(-1, keepdims=True)
            return (t - m) / jnp.sqrt(v + eps) * g + b

        def _l2n(t, eps=1e-12):
            return t / jnp.maximum(jnp.linalg.norm(t, axis=-1, keepdims=True), eps)
        Bs, Ts, Cs = x.shape
        Hs = gamma_w.shape[0]
        Ds = Cs // Hs
        Ks = conv_w.shape[-1]
        xt = jnp.transpose(x, (0, 2, 1))
        xc = jax.lax.conv_general_dilated(xt, conv_w, window_strides=(1,), padding=[(Ks - 1, 0)], dimension_numbers=('NCH', 'OIH', 'NCH'), feature_group_count=Cs)
        xc = jax.nn.silu(jnp.transpose(xc + conv_b[None, :, None], (0, 2, 1)))
        q = _l2n((x @ Wq.T).reshape(Bs, Ts, Hs, Ds))
        k = _l2n((x @ Wk.T).reshape(Bs, Ts, Hs, Ds))
        v = _ln((x @ Wv.T).reshape(Bs, Ts, Hs, Ds), vn_g, vn_b)
        i_gate = jax.nn.sigmoid(xc @ ig_w.T + ig_b).reshape(Bs, Ts, Hs, Ds)
        gamma = jax.nn.sigmoid(xc @ gamma_w.T + gamma_b)[..., None]
        a = jnp.broadcast_to(gamma, (Bs, Ts, Hs, Ds))
        b = i_gate * k * v

        def comb(left, right):
            aL, bL = left
            aR, bR = right
            return (aL * aR, bL * aR + bR)
        _, mem = jax.lax.associative_scan(comb, (a, b), axis=1)
        out = _ln(mem, mn_g, mn_b) * q
        o = out.reshape(Bs * Ts, Hs, Ds)
        m = o.mean(-1, keepdims=True)
        var = o.var(-1, keepdims=True)
        o = (o - m) / jnp.sqrt(var + 1e-05)
        o = o.reshape(Bs * Ts, Cs) * gn_g + gn_b
        o = o.reshape(Bs, Ts, Cs)
        o = o * jax.nn.sigmoid(xc @ og_w.T + og_b)
        return o @ Wo.T

    def _L0_attn_b_ref(x, Wq, bq, Wk, bk, Wv, bv, Wo, bo):
        import jax, jax.numpy as jnp
        import numpy as np
        import math
        N_Q = 128
        N_K = 128
        N_V = 128
        D_MODEL = 256
        N_HEADS = 16
        B, T = (8, 512)
        Bx, Tx, _ = x.shape
        q = (x @ Wq + bq).reshape(Bx, Tx, N_Q, N_HEADS)
        k = (x @ Wk + bk).reshape(Bx, Tx, N_K, N_HEADS)
        v = (x @ Wv + bv).reshape(Bx, Tx, N_V, N_HEADS)
        q = jnp.transpose(q, (0, 3, 2, 1))
        k = jnp.transpose(k, (0, 3, 1, 2))
        v = jnp.transpose(v, (0, 3, 2, 1))
        att = jax.nn.softmax(q @ k / math.sqrt(N_K), axis=-1)
        y = att @ v
        y = jnp.transpose(y, (0, 2, 1, 3)).reshape(Bx, -1, N_V * N_HEADS)
        return y @ Wo + bo

    def _L0_ffn_ref(x, gate_w, up_w, down_w, gate_s, up_s, down_s):
        import jax, jax.numpy as jnp
        import numpy as np
        HIDDEN = 256
        INTER = 704
        B, S = (2, 256)

        def _ternary(key, shape):
            return jax.random.randint(key, shape, -1, 2).astype(jnp.float32)
        b, s, h = x.shape
        xf = x.reshape(b * s, h)
        g = jnp.einsum('th,ih->ti', xf, gate_w) * gate_s
        u = jnp.einsum('th,ih->ti', xf, up_w) * up_s
        hdn = jax.nn.silu(g) * u
        out = jnp.einsum('ti,hi->th', hdn, down_w) * down_s
        return out.reshape(b, s, -1)
    x = L0_attn_a_x
    x = x + _L0_attn_a_ref(_layernorm(x, axis=-1), L0_attn_a_Wq, L0_attn_a_Wk, L0_attn_a_Wv, L0_attn_a_Wo, L0_attn_a_conv_w, L0_attn_a_conv_b, L0_attn_a_ig_w, L0_attn_a_ig_b, L0_attn_a_og_w, L0_attn_a_og_b, L0_attn_a_gamma_w, L0_attn_a_gamma_b, L0_attn_a_vn_g, L0_attn_a_vn_b, L0_attn_a_gn_g, L0_attn_a_gn_b, L0_attn_a_mn_g, L0_attn_a_mn_b)
    x = x + _L0_ffn_ref(_layernorm(x, axis=-1), L0_ffn_gate_w, L0_ffn_up_w, L0_ffn_down_w, L0_ffn_gate_s, L0_ffn_up_s, L0_ffn_down_s)
    x = x + _L0_attn_b_ref(_layernorm(x, axis=-1), L0_attn_b_Wq, L0_attn_b_bq, L0_attn_b_Wk, L0_attn_b_bk, L0_attn_b_Wv, L0_attn_b_bv, L0_attn_b_Wo, L0_attn_b_bo)
    x = x + _L0_ffn_ref(_layernorm(x, axis=-1), L0_ffn_gate_w, L0_ffn_up_w, L0_ffn_down_w, L0_ffn_gate_s, L0_ffn_up_s, L0_ffn_down_s)
    return x

_drawn_inputs = setup_inputs


def setup_inputs(seed=0):
    import zlib

    import numpy as np

    out = dict(_drawn_inputs(seed))
    spreads = {'L0_attn_a_conv_b': (0.0, 0.8),
     'L0_attn_a_ig_b': (-3.0, 0.2),
     'L0_attn_a_og_b': (0.0, 0.765),
     'L0_attn_a_vn_g': (1.0, 0.2),
     'L0_attn_a_vn_b': (0.0, 0.343),
     'L0_attn_a_gn_g': (1.0, 0.2),
     'L0_attn_a_gn_b': (0.0, 0.405),
     'L0_attn_a_mn_g': (1.0, 0.561),
     'L0_attn_a_mn_b': (0.0, 0.345),
     'L0_attn_b_bq': (0.0, 0.8),
     'L0_attn_b_bk': (0.0, 0.8),
     'L0_attn_b_bv': (0.0, 0.8),
     'L0_attn_b_bo': (0.0, 0.1)}
    factors = {'L0_attn_a_conv_w': 8.0,
     'L0_attn_a_ig_w': 8.0,
     'L0_attn_a_og_w': 8.0,
     'L0_attn_a_gamma_w': 33.305,
     'L0_attn_b_Wq': 8.0,
     'L0_attn_b_Wk': 8.0}
    for name, (base, spread) in spreads.items():
        noise = np.random.default_rng([zlib.crc32(name.encode()), seed]).standard_normal(out[name].shape)
        drawn = base * np.exp(spread * noise) if base else spread * noise
        out[name] = jnp.asarray(drawn.astype(out[name].dtype))
    for name, factor in factors.items():
        out[name] = (out[name] * factor).astype(out[name].dtype)
    return out
```

```python
from contextlib import ExitStack

import concourse.bass as bass
from concourse import mybir

F32 = mybir.dt.float32
F32R = mybir.dt.float32r
ACT = mybir.ActivationFunctionType
ALU = mybir.AluOpType
AX = mybir.AxisListType

P = 128
B, T, C = 4, 256, 256
H, D = 16, 16
TAPS = 4
NH, NQ = 16, 128
INTER = 704
R = T // P
NT = B * R
KC = C // P
HALF = B * T // 2
HT = NT // 2
HB = B // 2
EPS = 1e-5
FULL = INTER // P
REST = INTER - FULL * P
FCH = FULL + 1
NG = 4
STEPS = NH // NG
HL = NG // 2
Y_BLOCKS = NH // 2
SCALE = float(NQ) ** -0.5
BANK = 512

V_TAP, V_CONV_B, V_IG_B, V_GAMMA_B, V_OG_B, V_VN_G, V_VN_B, V_MN_G, V_MN_B, V_GN_G, V_GN_B = 0, 4, 5, 6, 7, 8, 9, 10, 11, 12, 13
N_VEC = 14
W_Q, W_K, W_V, W_IG, W_OG, W_GAMMA = range(6)

ORDER = [("project", 0), ("norms", 0), ("project", 1), ("memory", 0), ("norms", 1), ("group", 0),
         ("memory", 1), ("out", 0), ("group", 1), ("ffn", 0), ("out", 1), ("ffn", 1)]

STAGE_SLOTS = {"project": ["xt", "q", "k", "v", "ig", "og", "gamma"], "norms": ["nq", "nk", "nv"],
               "memory": ["mc", "mv"], "group": ["oc", "ov"], "out": ["wo"],
               "ffn": ["ft"] + [f"gu{n}" for n in range(FCH)] + ["dn"]}


class FfnBuffers:

    def __init__(self, sb, suffix, scope):
        self.XTf = sb("XTf" + suffix, [P, KC, HALF], F32, scope)
        self.XTh = sb("XTh" + suffix, [P, KC, HALF], F32R, scope)
        self.XTl = sb("XTl" + suffix, [P, KC, HALF], F32R, scope)
        self.HD = sb("HD" + suffix, [P, FCH, HALF], F32, scope)
        self.SG = sb("SG" + suffix, [P, 2, HALF], F32, scope)


def pair_plan():
    pair, before, held = {}, {}, [None] * 4
    n = 0
    for stage, h in ORDER:
        for name in STAGE_SLOTS[stage]:
            pair[name, h], before[name, h] = n % 4, held[n % 4]
            held[n % 4] = (name, h)
            n += 1
    return pair, before


def loop_value(i, per_step, nth):
    return (i + 1) * per_step + nth


def hybrid_block(nc, x, w_rec, w_gamma, w_rec_out, vec, w_gu, w_dn, ffn_scale, down_s,
                 wk, wv, wq, wo, bk, bq, bv, bo, out):
    pair, before = pair_plan()
    with ExitStack() as ctx:
        def sem(name):
            return ctx.enter_context(nc.semaphore(name))

        def sb(name, shape, dt=F32, scope=ctx):
            return scope.enter_context(nc.sbuf_tensor(name, shape, dt))

        s = {n: sem(n) for n in """
            x_in w_rec_in w_gamma_in w_out_in vec_in w_gu_in w_dn_in gu_again_in scale_in down_s_in
            wk_in wv_in wq_in wo_in bk_in bq_in bv_in bo_in x_out
            consts_pool consts_dve vec_half rec_split gu_raw_free gu_split dn_scaled
            ln_stat ln_agg ln_eps ln_rstd ln_done
            xt_ps xt_f xt_hi xt_lo conv_m0 conv_m1 silu_done xc_hi xc_lo
            q_ps k_ps v_ps ig_ps og_ps gamma_ps q_cp k_cp v_cp q_sq k_sq v_sq ti_done to_done tg_done gamma_done
            nq_ps nk_ps nv_ps nq_max nk_max nq_ln nk_ln nv_ln rq_done rk_done rv_done
            qn_done k_n k_g v_n v_a0 v_a1 b_done mem_done
            mc_ps mc_sq mv_ps mv_ln r1_done y_n y_a0 y_a1 o_done
            oc_ps oc_sq ov_ps ov_ln r2_done z_n z_a0 z_a1 z_done wo_ps rec_added
            ft_ps ft_f ft_hi ft_lo gu_ps silu_g hd_done dn_ps ffn_added
            bo_added x_hi x_lo g_ps g_hi g_lo s_cp s_rep s_rep_hi s_rep_lo ones_r_done
            raw_k_free raw_o_free raw_v_free wk_split wo_split wv_split bq_split bq_raw_free
            r_ps r_sum r_mask r_hi r_lo z_ps z_added w_ps w_cp s_ps negmax bias_done exp_done rsum
            e_norm p_ps p_hi p_lo t_ps t_cp u_ps u_added a_ps a_added""".split()}

        ps = ctx.enter_context(nc.psum_tensor("ps", [P, 4, 2, BANK], F32))

        X = sb("X", [P, NT, C])
        XN = sb("XN", [P, NT, C + 2])
        gu_hi = sb("gu_hi", [P, KC, 2 * INTER], F32R)
        gu_lo = sb("gu_lo", [P, KC, 2 * INTER], F32R)
        w_down = sb("w_down", [P, FCH, C])
        f_scale = sb("f_scale", [P, 2 * FCH])
        ident = sb("ident", [P, P])
        heads_ones = sb("heads_ones", [P, P])
        centre = sb("centre", [P, P])
        eps_col = sb("eps_col", [P, 1])
        minus_half = sb("minus_half", [P, NT])
        stats = sb("stats", [P, NT, 6])
        agg = sb("agg", [P, NT, 2])
        var_eps = sb("var_eps", [P, NT])
        rstd = sb("rstd", [P, NT])

        one = ctx.enter_context(ExitStack())
        w_hi = sb("w_hi", [P, KC, 6, C], F32R, one)
        w_lo = sb("w_lo", [P, KC, 6, C], F32R, one)
        w_out = sb("w_out", [P, KC, C], F32, one)
        down_b = sb("down_b", [P, C], F32, one)
        vecs = sb("vecs", [P, KC, N_VEC], F32, one)
        gam = sb("gam", [P, KC, H], F32, one)
        msum = sb("msum", [P, KC, H], F32, one)
        XCf = sb("XCf", [P, KC, HALF], F32, one)
        XCh = sb("XCh", [P, KC, HALF], F32R, one)
        XCl = sb("XCl", [P, KC, HALF], F32R, one)
        q_t, k_t, v_t, sq_q, sq_k, sq_v, t_ig, t_og, t_ga, mem = (
            sb(n, [P, 2, KC, HALF], F32, one)
            for n in ("q_t", "k_t", "v_t", "sq_q", "sq_k", "sq_v", "t_ig", "t_og", "t_ga", "mem"))
        ffn1 = FfnBuffers(sb, "1", one)
        w_raw = ffn1.HD[:].rearrange("p a b -> p (a b)").rearrange("p (k w c) -> p k w c", k=KC, w=6)
        one.close()

        two = ctx.enter_context(ExitStack())
        raw_k = sb("raw_k", [P, KC, NG * NQ], F32, two)
        raw_v = sb("raw_v", [P, KC, NG * NQ], F32, two)
        raw_o = sb("raw_o", [P, R, HL * C], F32, two)
        raw_q = sb("raw_q", [P, KC, NG * NQ], F32, two)
        wk_hi = sb("wk_hi", [P, KC, NG * NQ], F32R, two)
        wk_lo = sb("wk_lo", [P, KC, NG * NQ], F32R, two)
        wv_hi = sb("wv_hi", [P, KC, NG * NQ], F32R, two)
        wv_lo = sb("wv_lo", [P, KC, NG * NQ], F32R, two)
        wo_hi = sb("wo_hi", [P, R, HL * C], F32R, two)
        wo_lo = sb("wo_lo", [P, R, HL * C], F32R, two)
        bk_b = sb("bk_b", [P, NG * NQ], F32, two)
        bq_b = sb("bq_b", [96, NG * NQ], F32, two)
        bq_s = sb("bq_s", [96, NG * NQ], F32R, two)
        bv_c = sb("bv_c", [P, NH], F32, two)
        bo_b = sb("bo_b", [P, C], F32, two)
        XH = sb("XH", [P, NT, C], F32R, two)
        XL = sb("XL", [P, NT, C], F32R, two)
        G_hi = sb("G_hi", [P, B, KC, C], F32R, two)
        G_lo = sb("G_lo", [P, B, KC, C], F32R, two)
        S_col = sb("S_col", [P, KC, B], F32, two)
        S_hi = sb("S_hi", [P, KC, P], F32R, two)
        S_lo = sb("S_lo", [P, KC, P], F32R, two)
        ones_r = sb("ones_r", [P, P], F32R, two)
        mask = sb("mask", [96, B], F32, two)
        Z = sb("Z", [P, KC, B, NG * NQ], F32, two)
        r_row = sb("r_row", [P, NG * NQ], F32, two)
        r_s = sb("r_s", [96, NG, B, NQ], F32R, two)
        r_masked = XN[:].rearrange("p a b -> p (a b)")[0:96, 0:NG * B * NQ].rearrange(
            "p (g b n) -> p g b n", g=NG, b=B)
        w_sum = sb("w_sum", [P, HL, C], F32, two)
        E = sb("E", [P, 2, B, NQ], F32, two)
        neg = sb("neg", [P, 2, B], F32, two)
        e_bias = sb("e_bias", [P, 2, B], F32, two)
        e_sum = sb("e_sum", [P, 2, B], F32, two)
        e_inv = sb("e_inv", [P, 2, B], F32, two)
        ET = sb("ET", [P, NG, B, NQ], F32, two)
        S_rep = ET[:, 0, 0:KC]
        P_hi = sb("P_hi", [P, KC, B, HL, C], F32R, two)
        P_lo = sb("P_lo", [P, KC, B, HL, C], F32R, two)
        U = sb("U", [P, HL, B, C], F32, two)
        two.close()

        ffn2 = FfnBuffers(sb, "2", ctx)
        ffn = [ffn1, ffn2]

        freed = {}
        for h in range(2):
            freed.update({
                ("xt", h): (s["xt_f"], h + 1), ("q", h): (s["q_sq"], h + 1), ("k", h): (s["k_sq"], h + 1),
                ("v", h): (s["v_sq"], h + 1), ("ig", h): (s["ti_done"], 2 * h + 2), ("og", h): (s["to_done"], 2 * h + 2),
                ("gamma", h): (s["tg_done"], 2 * h + 2), ("nq", h): (s["nq_max"], h + 1), ("nk", h): (s["nk_max"], h + 1),
                ("nv", h): (s["nv_ln"], h + 1), ("mc", h): (s["y_n"], h + 1), ("mv", h): (s["mv_ln"], h + 1),
                ("oc", h): (s["z_n"], h + 1), ("ov", h): (s["ov_ln"], h + 1), ("wo", h): (s["rec_added"], h + 1),
                ("ft", h): (s["ft_f"], h + 1), ("dn", h): (s["ffn_added"], h + 1),
                **{(f"gu{n}", h): (s["hd_done"], h * FCH + n + 1) for n in range(FCH)}})

        def bank_pair(name, h):
            return ps[:, pair[name, h]]

        def token_cols(t):
            b, r = t // R, t % R
            return slice(b * T + r, (b + 1) * T, R)

        block = ctx.enter_context(nc.Block())

        @block.sync
        def _(sp):
            sp.dma_start(X[:].rearrange("p (b r) c -> p b (r c)", r=R),
                         x.rearrange("b (p r) c -> p b (r c)", r=R)).then_inc(s["x_in"], 16)
            sp.dma_start(vecs[:], vec.rearrange("(k p) v -> p k v", p=P)).then_inc(s["vec_in"], 16)
            sp.dma_start(gam[:], w_gamma.rearrange("(k p) h -> p k h", p=P)).then_inc(s["w_gamma_in"], 16)
            sp.dma_start(w_raw[:, :, 0:5, :], w_rec.rearrange("(k p) w c -> p k w c", p=P)).then_inc(s["w_rec_in"], 16)
            sp.dma_start(w_out[:], w_rec_out.rearrange("(k p) c -> p k c", p=P)).then_inc(s["w_out_in"], 16)
            sp.dma_start(w_down[:, 0:FULL, :], w_dn[0:FULL * P].rearrange("(n p) c -> p n c", p=P)).then_inc(s["w_dn_in"], 16)
            sp.dma_start(w_down[0:REST, FULL, :], w_dn[FULL * P:INTER]).then_inc(s["w_dn_in"], 16)
            sp.dma_start(f_scale[:], ffn_scale).then_inc(s["scale_in"], 16)
            sp.dma_start(down_b[:], down_s.partition_broadcast(P)).then_inc(s["down_s_in"], 16)
            sp.wait_ge(s["rec_split"], 2 * KC)
            sp.dma_start(ffn1.HD[:].rearrange("p a b -> p (a b)")[:, 0:KC * 2 * INTER].rearrange("p (k n) -> p k n", k=KC),
                         w_gu.rearrange("(k p) n -> p k n", p=P)).then_inc(s["w_gu_in"], 16)

            def load_step(i):
                sp.dma_start(raw_k[:], wk[i].rearrange("(k p) n -> p k n", p=P)).then_inc(s["wk_in"], 16)
                sp.dma_start(bk_b[:], bk[i].partition_broadcast(P)).then_inc(s["bk_in"], 16)
                sp.dma_start(raw_o[:], wo[i].rearrange("(p r) n -> p r n", r=R)).then_inc(s["wo_in"], 16)
                sp.dma_start(raw_v[:], wv[i].rearrange("(k p) n -> p k n", p=P)).then_inc(s["wv_in"], 16)
                sp.dma_start(bq_b[:], bq[i].partition_broadcast(96)).then_inc(s["bq_in"], 16)
                sp.dma_start(raw_q[:], wq[i].rearrange("(k p) n -> p k n", p=P)).then_inc(s["wq_in"], 16)

            sp.wait_ge(s["ffn_added"], 2)
            sp.dma_start(bv_c[:], bv).then_inc(s["bv_in"], 16)
            sp.dma_start(bo_b[:], bo.partition_broadcast(P)).then_inc(s["bo_in"], 16)
            load_step(0)
            with sp.Fori(1, STEPS) as i:
                sp.wait_ge(s["raw_k_free"], loop_value(i - 1, 1, 1))
                sp.dma_start(raw_k[:], wk[bass.ds(i, 1)].rearrange("o (k p) n -> p (o k) n", p=P)).then_inc(s["wk_in"], 16)
                sp.wait_ge(s["z_added"], loop_value(i - 1, 2 * B, 2 * B))
                sp.wait_ge(s["r_sum"], loop_value(i - 1, 1, 1))
                sp.dma_start(bk_b[:], bk[bass.ds(i, 1)].rearrange("o n -> (o n)").partition_broadcast(P)).then_inc(s["bk_in"], 16)
                sp.wait_ge(s["raw_o_free"], loop_value(i - 1, 1, 1))
                sp.dma_start(raw_o[:], wo[bass.ds(i, 1)].rearrange("o (p r) n -> p (o r) n", r=R)).then_inc(s["wo_in"], 16)
                sp.wait_ge(s["raw_v_free"], loop_value(i - 1, 1, 1))
                sp.dma_start(raw_v[:], wv[bass.ds(i, 1)].rearrange("o (k p) n -> p (o k) n", p=P)).then_inc(s["wv_in"], 16)
                sp.wait_ge(s["bq_raw_free"], loop_value(i - 1, 1, 1))
                sp.dma_start(bq_b[:], bq[bass.ds(i, 1)].rearrange("o n -> (o n)").partition_broadcast(96)).then_inc(s["bq_in"], 16)
                sp.wait_ge(s["s_ps"], loop_value(i - 1, NG, NG))
                sp.dma_start(raw_q[:], wq[bass.ds(i, 1)].rearrange("o (k p) n -> p (o k) n", p=P)).then_inc(s["wq_in"], 16)

            x_view = X[:].rearrange("p (b r) c -> p b (r c)", r=R)
            o_view = out.rearrange("b (p r) c -> p b (r c)", r=R)
            for h in range(2):
                sp.wait_ge(s["ffn_added"], 3 + h)
                sp.dma_start(o_view[:, h * HB:(h + 1) * HB], x_view[:, h * HB:(h + 1) * HB]).then_inc(s["x_out"], 16)
            sp.wait_ge(s["x_out"], 32)

        @block.gpsimd
        def _(pool):
            pool.memset(ident[:], 0.0).then_inc(s["consts_pool"], 1)
            pool.memset(heads_ones[:], 1.0).then_inc(s["consts_pool"], 1)
            pool.memset(eps_col[:], EPS).then_inc(s["consts_pool"], 1)
            pool.memset(minus_half[:], -0.5).then_inc(s["consts_pool"], 1)
            pool.wait_ge(s["consts_pool"], 4)
            pool.affine_select(out=ident[:], in_=ident[:], compare_op=ALU.not_equal, fill=1.0, base=0,
                               pattern=[[-1, P]], channel_multiplier=1).then_inc(s["consts_pool"], 1)
            blocks = heads_ones[:].rearrange("p (h d) -> p h d", d=D)
            pool.affine_select(out=blocks, in_=blocks, compare_op=ALU.is_ge, fill=0.0, base=0,
                               pattern=[[-D, P // D], [0, D]], channel_multiplier=1).then_inc(s["consts_pool"], 1)
            pool.wait_ge(s["consts_pool"], 6)
            pool.affine_select(out=blocks, in_=blocks, compare_op=ALU.is_ge, fill=0.0, base=D - 1,
                               pattern=[[D, P // D], [0, D]], channel_multiplier=-1).then_inc(s["consts_pool"], 1)

            def layer_norm(n, t0, nt):
                pool.wait_ge(s["ln_eps"], n + 1)
                pool.tensor_tensor(rstd[:, t0:t0 + nt], var_eps[:, t0:t0 + nt], minus_half[:, 0:nt],
                                   ALU.pow).then_inc(s["ln_rstd"], 1)

            def rec_project(h):
                pool.wait_ge(s["xt_f"], h + 1)
                if h:
                    pool.wait_ge(s["gamma_ps"], h)
                pool.tensor_scalar(ffn1.XTh[:], ffn1.XTf[:], 1.0, 0.0, ALU.mult, ALU.add).then_inc(s["xt_hi"], 1)
                pool.wait_ge(s["silu_done"], 2 * h + 2)
                if h:
                    pool.wait_ge(s["gamma_ps"], h)
                pool.tensor_scalar(XCh[:], XCf[:], 1.0, 0.0, ALU.mult, ALU.add).then_inc(s["xc_hi"], 1)

            def rec_norms(h):
                pool.wait_ge(s["rk_done"], h + 1)
                pool.wait_ge(s["k_cp"], h + 1)
                pool.tensor_tensor(k_t[:, h], k_t[:, h], sq_k[:, h], ALU.mult).then_inc(s["k_n"], 1)
                pool.wait_ge(s["rq_done"], h + 1)
                pool.wait_ge(s["q_cp"], h + 1)
                pool.tensor_tensor(q_t[:, h], q_t[:, h], sq_q[:, h], ALU.mult).then_inc(s["qn_done"], 1)

            def ffn_half(f, h):
                n = 2 * f + h
                w = ffn[f]
                layer_norm(1 + h if f == 0 else 4 + h, h * HT, HT)
                pool.wait_ge(s["ft_f"], n + 1)
                if f == 0 and h == 0:
                    pool.wait_ge(s["gamma_ps"], 2)
                elif h:
                    pool.wait_ge(s["gu_ps"], n * FCH)
                pool.tensor_scalar(w.XTh[:], w.XTf[:], 1.0, 0.0, ALU.mult, ALU.add).then_inc(s["ft_hi"], 1)

            layer_norm(0, 0, NT)
            for stage, h in ORDER:
                if stage == "project":
                    rec_project(h)
                elif stage == "norms":
                    rec_norms(h)
                elif stage == "ffn":
                    ffn_half(0, h)

            layer_norm(3, 0, NT)
            pool.sem_inc(s["r_mask"], 1)
            pool.sem_inc(s["r_lo"], 1)
            with pool.Fori(0, STEPS) as i:
                pool.wait_ge(s["r_sum"], loop_value(i, 1, 1))
                pool.wait_ge(s["r_lo"], loop_value(i - 1, 1, 1))
                for g in range(NG):
                    rm = pool.tensor_tensor(
                        r_masked[:, g],
                        r_row[0:96, g * NQ:(g + 1) * NQ].unsqueeze(1).to_broadcast([96, B, NQ]),
                        mask[:].unsqueeze(2).to_broadcast([96, B, NQ]), ALU.mult)
                rm.then_inc(s["r_mask"], 1)
                pool.wait_ge(s["r_hi"], loop_value(i, 1, 1))
                pool.wait_ge(s["r_mask"], loop_value(i, 1, 1))
                pool.tensor_tensor(r_s[32:64], r_masked[32:64], r_s[32:64].bitcast(F32),
                                   ALU.subtract).then_inc(s["r_lo"], 1)
            for h in range(2):
                ffn_half(1, h)

        @block.scalar
        def _(act):
            def to_channel_major(src, dst):
                for m in range(KC):
                    op = act.copy(dst[:, m, :].rearrange("p (b n r) -> p b r n", b=HB, r=R),
                                  src[:, m, :].rearrange("p (b r n) -> p b r n", b=HB, r=R))
                return op

            def rsqrt_of(src, dst, scale, bias, ln_sem, done_sem, h):
                act.activation(dst, src, ACT.Ln, scale=scale, bias=bias).then_inc(ln_sem, 1)
                act.wait_ge(ln_sem, h + 1)
                act.activation(dst, dst, ACT.Exp, scale=-0.5).then_inc(done_sem, 1)

            def rec_project(h):
                act.wait_ge(s["xt_ps"], h + 1)
                if h:
                    act.wait_ge(s["conv_m0"], TAPS)
                    act.wait_ge(s["conv_m1"], TAPS)
                    act.wait_ge(s["xt_hi"], 1)
                    act.wait_ge(s["xt_lo"], 1)
                to_channel_major(bank_pair("xt", h), ffn1.XTf).then_inc(s["xt_f"], 1)
                for m, conv in enumerate((s["conv_m0"], s["conv_m1"])):
                    act.wait_ge(conv, TAPS * (h + 1))
                    act.activation(XCf[:, m], XCf[:, m], ACT.Silu,
                                   bias=vecs[:, m, V_CONV_B:V_CONV_B + 1]).then_inc(s["silu_done"], 1)
                for name, got, dst, cp, sq, sq_sem in (("q", s["q_ps"], q_t, s["q_cp"], sq_q, s["q_sq"]),
                                                       ("k", s["k_ps"], k_t, s["k_cp"], sq_k, s["k_sq"]),
                                                       ("v", s["v_ps"], v_t, s["v_cp"], sq_v, s["v_sq"])):
                    act.wait_ge(got, h + 1)
                    act.copy(dst[:, h], bank_pair(name, h)).then_inc(cp, 1)
                    act.activation(sq[:, h], bank_pair(name, h), ACT.Square).then_inc(sq_sem, 1)
                act.wait_ge(s["vec_half"], 1)
                for name, got, dst, done, col in (("ig", s["ig_ps"], t_ig, s["ti_done"], V_IG_B),
                                                  ("og", s["og_ps"], t_og, s["to_done"], V_OG_B),
                                                  ("gamma", s["gamma_ps"], t_ga, s["tg_done"], V_GAMMA_B)):
                    act.wait_ge(got, h + 1)
                    for m in range(KC):
                        act.activation(dst[:, h, m], bank_pair(name, h)[:, m], ACT.Tanh, scale=0.5,
                                       bias=vecs[:, m, col:col + 1]).then_inc(done, 1)

            def rec_norms(h):
                act.wait_ge(s["nk_max"], h + 1)
                rsqrt_of(sq_k[:, h], sq_k[:, h], 1.0, 0.0, s["nk_ln"], s["rk_done"], h)
                act.wait_ge(s["nv_ps"], h + 1)
                rsqrt_of(bank_pair("nv", h), sq_v[:, h], 1.0 / D, eps_col[:], s["nv_ln"], s["rv_done"], h)
                act.wait_ge(s["nq_max"], h + 1)
                rsqrt_of(sq_q[:, h], sq_q[:, h], 1.0, 0.0, s["nq_ln"], s["rq_done"], h)

            def rec_memory(h):
                act.wait_ge(s["mc_ps"], h + 1)
                act.wait_ge(s["v_n"], h + 1)
                act.activation(sq_v[:, h], bank_pair("mc", h), ACT.Square).then_inc(s["mc_sq"], 1)
                act.wait_ge(s["mv_ps"], h + 1)
                rsqrt_of(bank_pair("mv", h), sq_v[:, h], 1.0 / D, eps_col[:], s["mv_ln"], s["r1_done"], h)

            def rec_group(h):
                act.wait_ge(s["oc_ps"], h + 1)
                act.wait_ge(s["qn_done"], h + 1)
                act.activation(sq_q[:, h], bank_pair("oc", h), ACT.Square).then_inc(s["oc_sq"], 1)
                act.wait_ge(s["ov_ps"], h + 1)
                rsqrt_of(bank_pair("ov", h), sq_q[:, h], 1.0 / D, eps_col[:], s["ov_ln"], s["r2_done"], h)

            def ffn_half(f, h, psum):
                n, w = 2 * f + h, ffn[f]
                act.wait_ge(s["ft_ps"], n + 1)
                if f == 0 and h == 0:
                    act.wait_ge(s["conv_m1"], 2 * TAPS)
                    act.wait_ge(s["xt_lo"], 2)
                    act.wait_ge(s["xt_hi"], 2)
                elif h:
                    act.wait_ge(s["ft_hi"], n)
                    act.wait_ge(s["ft_lo"], n)
                to_channel_major(psum("ft"), w.XTf).then_inc(s["ft_f"], 1)
                for c in range(FCH):
                    rows = P if c < FULL else REST
                    act.wait_ge(s["gu_ps"], n * FCH + c + 1)
                    if c >= 2 or h:
                        act.wait_ge(s["hd_done"], n * FCH + c - 1)
                    act.activation(w.SG[0:rows, c % 2], psum(f"gu{c}")[0:rows, 0], ACT.Silu,
                                   scale=f_scale[0:rows, c:c + 1]).then_inc(s["silu_g"], 1)

            act.wait_ge(s["consts_pool"], 7)
            act.wait_ge(s["vec_in"], 16)
            for stage, h in ORDER:
                if stage == "project":
                    rec_project(h)
                elif stage == "norms":
                    rec_norms(h)
                elif stage == "memory":
                    rec_memory(h)
                elif stage == "group":
                    rec_group(h)
                elif stage == "ffn":
                    if h == 0:
                        act.wait_ge(s["scale_in"], 16)
                    ffn_half(0, h, lambda name: bank_pair(name, h))

            act.wait_ge(s["ffn_added"], 2)
            for b in range(B):
                act.wait_ge(s["g_ps"], b + 1)
                act.copy(G_hi[:, b], ps[:, b, :, 0:C]).then_inc(s["g_hi"], 1)
            for sm, per in ((s["r_hi"], 1), (s["w_cp"], 1), (s["exp_done"], NG * B), (s["p_hi"], B), (s["t_cp"], 2)):
                act.sem_inc(sm, per)
            with act.Fori(0, STEPS) as i:
                act.wait_ge(s["r_mask"], loop_value(i, 1, 1))
                act.wait_ge(s["s_ps"], loop_value(i - 1, NG, NG))
                act.copy(r_s[:], r_masked).then_inc(s["r_hi"], 1)
                act.wait_ge(s["w_ps"], loop_value(i, 1, 1))
                act.wait_ge(s["u_added"], loop_value(i - 1, 2 * NG, 2 * NG))
                act.copy(w_sum[:].rearrange("p a c -> p (a c)"), ps[:, 1, 0, :]).then_inc(s["w_cp"], 1)

                def exps(g):
                    j = g % 2
                    act.wait_ge(s["bias_done"], loop_value(i, NG, g + 1))
                    act.wait_ge(s["t_ps"], loop_value(i, 2, g // 2))
                    act.wait_ge(s["e_norm"], loop_value(i, NG, g - 1))
                    for b in range(B):
                        act.activation(E[:, j, b], ps[:, S_PAIR[g // 2], j, b * NQ:(b + 1) * NQ], ACT.Exp,
                                       scale=SCALE, bias=e_bias[:, j, b:b + 1],
                                       accum_out=e_sum[:, j, b:b + 1]).then_inc(s["exp_done"], 1)

                def transposed(j):
                    act.wait_ge(s["t_ps"], loop_value(i, 2, j + 1))
                    act.wait_ge(s["a_ps"], loop_value(i - 1, 2, j + 1))
                    act.copy(ET[:, 2 * j:2 * j + 2].rearrange("p g b n -> p g (b n)"),
                             ps[:, T_PAIR[j]]).then_inc(s["t_cp"], 1)

                exps(0)
                exps(1)
                for b in range(B):
                    act.wait_ge(s["p_ps"], loop_value(i, B, b + 1))
                    act.wait_ge(s["u_ps"], loop_value(i - 1, NG, NG))
                    act.copy(P_hi[:, :, b].rearrange("p m l c -> p m (l c)"), ps[:, P_PAIR[b]]).then_inc(s["p_hi"], 1)
                    if b == 0:
                        transposed(0)
                exps(2)
                exps(3)
                transposed(1)
            for h in range(2):
                ffn_half(1, h, lambda name: ps[:, F2_PAIR[name, h]])

        @block.tensor
        def _(pe):
            def claim(name, h):
                if before[name, h] is not None:
                    pe.wait_ge(*freed[before[name, h]])
                return bank_pair(name, h)

            def split_product(outs, left, right):
                terms = [(a, b) for (lh, ll), (rh, rl) in zip(left, right)
                         for a, b in ((lh, rh), (lh, rl), (ll, rh))]
                for n, (a, b) in enumerate(terms):
                    mm = pe.matmul(outs, a, b, start=(n == 0), stop=(n == len(terms) - 1))
                return mm

            def transposes(dst, h, done):
                for t in range(HT):
                    for m in range(KC):
                        tr = pe.transpose(dst[:, m, t * P:(t + 1) * P], XN[:, h * HT + t, m * P:(m + 1) * P], ident[:])
                tr.then_inc(done, 1)

            def projection(name, block_, h, xh, xl, done):
                dst = claim(name, h)
                for m in range(KC):
                    mm = split_product(dst[:, m],
                                       [(w_hi[:, k, block_, m * P:(m + 1) * P], w_lo[:, k, block_, m * P:(m + 1) * P]) for k in range(KC)],
                                       [(xh[:, k], xl[:, k]) for k in range(KC)])
                mm.then_inc(done, 1)

            def rec_project(h):
                dst = claim("xt", h)
                pe.wait_ge(s["ln_done"], 1)
                transposes(dst, h, s["xt_ps"])
                pe.wait_ge(s["rec_split"], 2 * KC)
                pe.wait_ge(s["xt_hi"], h + 1)
                pe.wait_ge(s["xt_lo"], h + 1)
                for name, w, done in (("q", W_Q, s["q_ps"]), ("k", W_K, s["k_ps"]), ("v", W_V, s["v_ps"])):
                    projection(name, w, h, ffn1.XTh, ffn1.XTl, done)
                pe.wait_ge(s["xc_hi"], h + 1)
                pe.wait_ge(s["xc_lo"], h + 1)
                for name, w, done in (("ig", W_IG, s["ig_ps"]), ("og", W_OG, s["og_ps"]), ("gamma", W_GAMMA, s["gamma_ps"])):
                    projection(name, w, h, XCh, XCl, done)

            def by_head(name, h, matrix, src, done):
                dst = claim(name, h)
                for m in range(KC):
                    mm = pe.matmul(dst[:, m], matrix[:], src[:, h, m], start=True, stop=True)
                mm.then_inc(done, 1)

            def rec_norms(h):
                pe.wait_ge(s["q_sq"], h + 1)
                by_head("nq", h, heads_ones, sq_q, s["nq_ps"])
                pe.wait_ge(s["k_sq"], h + 1)
                by_head("nk", h, heads_ones, sq_k, s["nk_ps"])
                pe.wait_ge(s["v_sq"], h + 1)
                by_head("nv", h, heads_ones, sq_v, s["nv_ps"])

            def rec_memory(h):
                pe.wait_ge(s["mem_done"], 2 * HB * (h + 1))
                by_head("mc", h, centre, mem, s["mc_ps"])
                pe.wait_ge(s["mc_sq"], h + 1)
                by_head("mv", h, heads_ones, sq_v, s["mv_ps"])

            def rec_group(h):
                pe.wait_ge(s["o_done"], h + 1)
                by_head("oc", h, centre, v_t, s["oc_ps"])
                pe.wait_ge(s["oc_sq"], h + 1)
                by_head("ov", h, heads_ones, sq_q, s["ov_ps"])

            def rec_out(h):
                dst = claim("wo", h).rearrange("p a (t c) -> p (a t) c", c=C)
                pe.wait_ge(s["w_out_in"], 16)
                pe.wait_ge(s["z_done"], h + 1)
                for t in range(HT):
                    for k in range(KC):
                        mm = pe.matmul(dst[:, t], k_t[:, h, k, token_cols(t)], w_out[:, k], start=(k == 0), stop=(k == KC - 1))
                mm.then_inc(s["wo_ps"], 1)

            def ffn_half(f, h, psum):
                n, w = 2 * f + h, ffn[f]
                dst = psum("ft")
                pe.wait_ge(s["ln_done"], 2 + h if f == 0 else 5 + h)
                transposes(dst, h, s["ft_ps"])
                pe.wait_ge(s["gu_split"], 2)
                pe.wait_ge(s["ft_hi"], n + 1)
                pe.wait_ge(s["ft_lo"], n + 1)
                right = [(w.XTh[:, k], w.XTl[:, k]) for k in range(KC)]
                for c in range(FCH):
                    dst = psum(f"gu{c}")
                    for j in range(2 if c < FULL else 1):
                        cols = slice((2 * c + j) * P, (2 * c + j + 1) * P)
                        mm = split_product(dst[:, j], [(gu_hi[:, k, cols], gu_lo[:, k, cols]) for k in range(KC)], right)
                    mm.then_inc(s["gu_ps"], 1)
                dst = psum("dn").rearrange("p a (t c) -> p (a t) c", c=C)
                pe.wait_ge(s["dn_scaled"], 2)
                pe.wait_ge(s["hd_done"], (n + 1) * FCH)
                for t in range(HT):
                    for c in range(FCH):
                        rows = P if c < FULL else REST
                        mm = pe.matmul(dst[:, t], w.HD[0:rows, c, token_cols(t)], w_down[0:rows, c],
                                       start=(c == 0), stop=(c == FCH - 1))
                mm.then_inc(s["dn_ps"], 1)

            pe.wait_ge(s["consts_pool"], 7)
            pe.wait_ge(s["consts_dve"], 1)
            for stage, h in ORDER:
                if stage == "project":
                    rec_project(h)
                elif stage == "norms":
                    rec_norms(h)
                elif stage == "memory":
                    rec_memory(h)
                elif stage == "group":
                    rec_group(h)
                elif stage == "out":
                    rec_out(h)
                elif stage == "ffn":
                    ffn_half(0, h, lambda name: claim(name, h))

            pe.wait_ge(s["ln_done"], 4)
            pe.wait_ge(s["ffn_added"], 2)
            for b in range(B):
                for m in range(KC):
                    for k in range(R):
                        mm = pe.matmul(ps[:, b, m, 0:C + 1], XN[:, b * R + k, m * P:(m + 1) * P],
                                       XN[:, b * R + k, 0:C + 1], start=(k == 0), stop=(k == R - 1))
                mm.then_inc(s["g_ps"], 1)
            for sm, per in ((s["r_ps"], 1), (s["z_ps"], B), (s["w_ps"], 1), (s["s_ps"], NG), (s["p_ps"], B), (s["t_ps"], 2),
                            (s["u_ps"], NG), (s["a_ps"], 2)):
                pe.sem_inc(sm, per)
            pe.wait_ge(s["g_lo"], B)
            pe.wait_ge(s["g_hi"], B)
            pe.wait_ge(s["s_rep_hi"], 1)
            pe.wait_ge(s["s_rep_lo"], 1)
            pe.wait_ge(s["x_lo"], 1)
            pe.wait_ge(s["ones_r_done"], 1)
            with pe.Fori(0, STEPS) as i:
                def scores(g):
                    dst = ps[:, S_PAIR[g // 2], g % 2]
                    cols = slice(g * NQ, (g + 1) * NQ)
                    if g == 0:
                        pe.wait_ge(s["wq_in"], 16 * (i + 1))
                        pe.wait_ge(s["z_added"], loop_value(i, 2 * B, 2 * B))
                    for k in range(KC):
                        pe.matmul(dst, raw_q[:, k, cols], Z[:, k, :, cols], start=(k == 0), stop=False)
                    if g == 0:
                        pe.wait_ge(s["bq_split"], loop_value(i, 2, 2))
                        pe.wait_ge(s["r_lo"], loop_value(i, 1, 1))
                    pe.matmul(dst, bq_s[:, cols], r_s[:, g].rearrange("p b n -> p (b n)"), start=False,
                              stop=True).then_inc(s["s_ps"], 1)

                def transpose_pair(j):
                    pe.wait_ge(s["e_norm"], loop_value(i, NG, 2 * j + 2))
                    for g in range(2):
                        for b in range(B):
                            tr = pe.transpose(ps[:, T_PAIR[j], g, b * NQ:(b + 1) * NQ], E[:, g, b], ident[:])
                    tr.then_inc(s["t_ps"], 1)

                def project_wo(b):
                    for m in range(KC):
                        mm = split_product(ps[:, P_PAIR[b], m],
                                           [(XH[:, b * R + k, m * P:(m + 1) * P], XL[:, b * R + k, m * P:(m + 1) * P]) for k in range(R)],
                                           [(wo_hi[:, k], wo_lo[:, k]) for k in range(R)])
                    mm.then_inc(s["p_ps"], 1)

                def values(g):
                    cols = slice(g * NQ, (g + 1) * NQ)
                    for j in range(2):
                        right = [(P_hi[:, k, 2 * j:2 * j + 2, g % HL], P_lo[:, k, 2 * j:2 * j + 2, g % HL]) for k in range(KC)]
                        mm = split_product(ps[:, U_PAIR[g], j], [(wv_hi[:, k, cols], wv_lo[:, k, cols]) for k in range(KC)], right)
                    mm.then_inc(s["u_ps"], 1)

                def attend(j):
                    dst = ps[:, A_PAIR[j]].rearrange("p a (b c) -> p (a b) c", c=C)
                    for b in range(B):
                        for l in range(HL):
                            mm = pe.matmul(dst[:, b], ET[:, 2 * j + l, b], U[:, l, b], start=(l == 0), stop=(l == HL - 1))
                    mm.then_inc(s["a_ps"], 1)

                pe.wait_ge(s["wk_split"], loop_value(i, 2, 2))
                pe.wait_ge(s["u_added"], loop_value(i - 1, 2 * NG, 6))
                split_product(ps[:, 0, 0], [(S_hi[:, k], S_lo[:, k]) for k in range(KC)],
                              [(wk_hi[:, k], wk_lo[:, k]) for k in range(KC)]).then_inc(s["r_ps"], 1)
                for b in range(B):
                    if b == 0:
                        pe.wait_ge(s["u_added"], loop_value(i - 1, 2 * NG, 8))
                    if b == 1:
                        pe.wait_ge(s["a_added"], loop_value(i - 1, 2, 2))
                    if b == 3:
                        pe.wait_ge(s["r_sum"], loop_value(i, 1, 1))
                    for m in range(KC):
                        mm = split_product(ps[:, Z_PAIR[b], m],
                                           [(G_hi[:, b, k, m * P:(m + 1) * P], G_lo[:, b, k, m * P:(m + 1) * P]) for k in range(KC)],
                                           [(wk_hi[:, k], wk_lo[:, k]) for k in range(KC)])
                    mm.then_inc(s["z_ps"], 1)
                pe.wait_ge(s["wo_split"], loop_value(i, 2, 2))
                pe.wait_ge(s["z_added"], loop_value(i, 2 * B, 2))
                for k in range(R):
                    for part, w in enumerate((wo_hi, wo_lo)):
                        mm = pe.matmul(ps[:, 1, 0], ones_r[:], w[:, k], start=(k == 0 and part == 0),
                                       stop=(k == R - 1 and part == 1))
                mm.then_inc(s["w_ps"], 1)
                scores(0)
                scores(1)
                project_wo(0)
                project_wo(1)
                pe.wait_ge(s["w_cp"], loop_value(i, 1, 1))
                project_wo(2)
                pe.wait_ge(s["exp_done"], loop_value(i, NG * B, 2 * B))
                project_wo(3)
                pe.wait_ge(s["p_lo"], loop_value(i, B, 1))
                transpose_pair(0)
                pe.wait_ge(s["p_lo"], loop_value(i, B, 2))
                scores(2)
                scores(3)
                pe.wait_ge(s["wv_split"], loop_value(i, 2, 2))
                pe.wait_ge(s["p_lo"], loop_value(i, B, B))
                values(0)
                values(1)
                pe.wait_ge(s["t_cp"], loop_value(i, 2, 1))
                pe.wait_ge(s["u_added"], loop_value(i, 2 * NG, 4))
                attend(0)
                transpose_pair(1)
                values(2)
                values(3)
                pe.wait_ge(s["t_cp"], loop_value(i, 2, 2))
                pe.wait_ge(s["u_added"], loop_value(i, 2 * NG, 8))
                pe.wait_ge(s["a_added"], loop_value(i, 2, 1))
                attend(1)

            for h in range(2):
                def claim2(name, h=h):
                    order = [(f"{n}", hh) for hh in range(2) for n in STAGE_SLOTS["ffn"]]
                    at = order.index((name, h))
                    if at < 4:
                        pe.wait_ge(s["a_added"], loop_value(STEPS - 1, 2, 2))
                    else:
                        was, hh = order[at - 4]
                        value = {"ft": (s["ft_f"], 3 + hh), "dn": (s["ffn_added"], 3 + hh)}.get(was)
                        if value is None:
                            value = (s["hd_done"], (2 + hh) * FCH + int(was[2:]) + 1)
                        pe.wait_ge(*value)
                    return ps[:, F2_PAIR[name, h]]
                ffn_half(1, h, claim2)

        @block.vector
        def _(dve):
            def layer_norm(n, t0, nt, augmented=False):
                first = sum(k for _, k in LN_RUNS[:n])
                for t in range(nt):
                    dve.bn_stats(stats[:, t0 + t], X[:, t0 + t]).then_inc(s["ln_stat"], 1)
                for t in range(nt):
                    dve.wait_ge(s["ln_stat"], first + t + 1)
                    dve.bn_aggr(agg[:, t0 + t], stats[:, t0 + t]).then_inc(s["ln_agg"], 1)
                dve.wait_ge(s["ln_agg"], first + nt)
                dve.tensor_scalar(var_eps[:, t0:t0 + nt], agg[:, t0:t0 + nt, 1], EPS, None, ALU.add).then_inc(s["ln_eps"], 1)
                dve.wait_ge(s["ln_rstd"], n + 1)
                for t in range(t0, t0 + nt):
                    op = dve.tensor_scalar(XN[:, t, 0:C], X[:, t], agg[:, t, 0:1], rstd[:, t:t + 1], ALU.subtract, ALU.mult)
                op.then_inc(s["ln_done"], 1)

            def rec_project(h):
                dve.wait_ge(s["xt_f"], h + 1)
                dve.wait_ge(s["xt_hi"], h + 1)
                dve.tensor_tensor(ffn1.XTl[:], ffn1.XTf[:], ffn1.XTh[:].bitcast(F32), ALU.subtract).then_inc(s["xt_lo"], 1)
                if h:
                    dve.wait_ge(s["xc_hi"], h)
                    dve.wait_ge(s["xc_lo"], h)
                conv = (s["conv_m0"], s["conv_m1"])
                for shift in range(TAPS):
                    for m in range(KC):
                        tap = vecs[:, m, V_TAP + TAPS - 1 - shift:V_TAP + TAPS - shift]
                        src = ffn1.XTf[:, m].rearrange("p (b t) -> p b t", b=HB)[:, :, 0:T - shift]
                        dst = XCf[:, m].rearrange("p (b t) -> p b t", b=HB)[:, :, shift:T]
                        if shift == 0:
                            dve.tensor_scalar(XCf[:, m], ffn1.XTf[:, m], tap, None, ALU.mult).then_inc(conv[m], 1)
                        else:
                            dve.wait_ge(conv[m], TAPS * h + shift)
                            dve.scalar_tensor_tensor(out=dst, in0=src, scalar=tap, in1=dst, op0=ALU.mult,
                                                     op1=ALU.add).then_inc(conv[m], 1)
                dve.wait_ge(s["silu_done"], 2 * h + 2)
                dve.wait_ge(s["xc_hi"], h + 1)
                dve.tensor_tensor(XCl[:], XCf[:], XCh[:].bitcast(F32), ALU.subtract).then_inc(s["xc_lo"], 1)
                dve.wait_ge(s["tg_done"], 2 * h + 2)
                dve.tensor_scalar(t_ga[:, h], t_ga[:, h], 0.5, 0.5, ALU.mult, ALU.add).then_inc(s["gamma_done"], 1)

            def rec_norms(h):
                dve.wait_ge(s["nk_ps"], h + 1)
                dve.tensor_scalar(sq_k[:, h], bank_pair("nk", h), 1e-24, None, ALU.max).then_inc(s["nk_max"], 1)
                dve.wait_ge(s["nq_ps"], h + 1)
                dve.tensor_scalar(sq_q[:, h], bank_pair("nq", h), 1e-24, None, ALU.max).then_inc(s["nq_max"], 1)
                dve.wait_ge(s["v_cp"], h + 1)
                dve.wait_ge(s["rv_done"], h + 1)
                dve.tensor_tensor(v_t[:, h], v_t[:, h], sq_v[:, h], ALU.mult).then_inc(s["v_n"], 1)
                dve.wait_ge(s["v_n"], h + 1)
                dve.wait_ge(s["vec_half"], 1)
                for m, done in enumerate((s["v_a0"], s["v_a1"])):
                    dve.tensor_scalar(v_t[:, h, m], v_t[:, h, m], vecs[:, m, V_VN_G:V_VN_G + 1],
                                      vecs[:, m, V_VN_B:V_VN_B + 1], ALU.mult, ALU.add).then_inc(done, 1)
                dve.wait_ge(s["k_n"], h + 1)
                dve.wait_ge(s["ti_done"], 2 * h + 2)
                kf, tf, vf, gf, mf = (a[:, h].rearrange("p m t -> p (m t)") for a in (k_t, t_ig, v_t, t_ga, mem))
                dve.scalar_tensor_tensor(out=kf, in0=tf, scalar=1.0, in1=kf, op0=ALU.add,
                                         op1=ALU.mult).then_inc(s["k_g"], 1)
                dve.wait_ge(s["k_g"], h + 1)
                dve.wait_ge(s["v_a0"], h + 1)
                dve.wait_ge(s["v_a1"], h + 1)
                dve.tensor_tensor(kf, kf, vf, ALU.mult).then_inc(s["b_done"], 1)
                dve.wait_ge(s["b_done"], h + 1)
                dve.wait_ge(s["gamma_done"], h + 1)
                for n in range(KC * HB):
                    span = slice(n * T, (n + 1) * T)
                    dve.tensor_tensor_scan(mf[:, span], gf[:, span], kf[:, span], 0.0, ALU.mult, ALU.add).then_inc(s["mem_done"], 1)

            def rec_memory(h):
                dve.wait_ge(s["r1_done"], h + 1)
                dve.tensor_tensor(v_t[:, h], bank_pair("mc", h), sq_v[:, h], ALU.mult).then_inc(s["y_n"], 1)
                dve.wait_ge(s["y_n"], h + 1)
                for m, done in enumerate((s["y_a0"], s["y_a1"])):
                    dve.tensor_scalar(v_t[:, h, m], v_t[:, h, m], vecs[:, m, V_MN_G:V_MN_G + 1],
                                      vecs[:, m, V_MN_B:V_MN_B + 1], ALU.mult, ALU.add).then_inc(done, 1)
                dve.wait_ge(s["y_a0"], h + 1)
                dve.wait_ge(s["y_a1"], h + 1)
                dve.wait_ge(s["qn_done"], h + 1)
                dve.tensor_tensor(v_t[:, h], v_t[:, h], q_t[:, h], ALU.mult).then_inc(s["o_done"], 1)

            def rec_group(h):
                dve.wait_ge(s["r2_done"], h + 1)
                dve.tensor_tensor(k_t[:, h], bank_pair("oc", h), sq_q[:, h], ALU.mult).then_inc(s["z_n"], 1)
                dve.wait_ge(s["z_n"], h + 1)
                for m, done in enumerate((s["z_a0"], s["z_a1"])):
                    dve.tensor_scalar(k_t[:, h, m], k_t[:, h, m], vecs[:, m, V_GN_G:V_GN_G + 1],
                                      vecs[:, m, V_GN_B:V_GN_B + 1], ALU.mult, ALU.add).then_inc(done, 1)
                dve.wait_ge(s["z_a0"], h + 1)
                dve.wait_ge(s["z_a1"], h + 1)
                dve.wait_ge(s["to_done"], 2 * h + 2)
                kf, tf = (a[:, h].rearrange("p m t -> p (m t)") for a in (k_t, t_og))
                dve.scalar_tensor_tensor(out=kf, in0=tf, scalar=1.0, in1=kf, op0=ALU.add,
                                         op1=ALU.mult).then_inc(s["z_done"], 1)

            def add_to_x(dst, src, done):
                dve.tensor_tensor(dst, dst, src, ALU.add).then_inc(done, 1)

            def half_of_x(h):
                return X[:, h * HT:(h + 1) * HT].rearrange("p (a t) c -> p a (t c)", a=2)

            def ffn_half(f, h, psum):
                n, w = 2 * f + h, ffn[f]
                if f or h:
                    pass
                dve.wait_ge(s["ft_f"], n + 1)
                dve.wait_ge(s["ft_hi"], n + 1)
                dve.tensor_tensor(w.XTl[:], w.XTf[:], w.XTh[:].bitcast(F32), ALU.subtract).then_inc(s["ft_lo"], 1)
                for c in range(FCH):
                    rows = P if c < FULL else REST
                    up = psum(f"gu{c}")[0:P, 1] if c < FULL else psum(f"gu{c}")[REST:P, 0]
                    if c == 0 and n in (1, 3):
                        dve.wait_ge(s["dn_ps"], n)
                    dve.wait_ge(s["silu_g"], n * FCH + c + 1)
                    dve.tensor_tensor(w.HD[0:rows, c], up, w.SG[0:rows, c % 2], ALU.mult).then_inc(s["hd_done"], 1)
                dve.wait_ge(s["dn_ps"], n + 1)
                if f == 0:
                    dve.wait_ge(s["rec_added"], h + 1)
                else:
                    dve.wait_ge(s["a_added"], loop_value(STEPS - 1, 2, 2))
                add_to_x(half_of_x(h), psum("dn"), s["ffn_added"])

            dve.memset(XN[:, :, C:C + 2], 1.0).then_inc(s["consts_dve"], 1)
            dve.wait_ge(s["x_in"], 16)
            layer_norm(0, 0, NT)
            dve.wait_ge(s["consts_pool"], 7)
            dve.scalar_tensor_tensor(out=centre[:], in0=heads_ones[:], scalar=-1.0 / D, in1=ident[:],
                                     op0=ALU.mult, op1=ALU.add).then_inc(s["consts_dve"], 1)
            dve.wait_ge(s["vec_in"], 16)
            dve.tensor_scalar(vecs[:, :, V_IG_B:V_VN_B + 1], vecs[:, :, V_IG_B:V_VN_B + 1], 0.5, None, ALU.mult)
            dve.tensor_scalar(vecs[:, :, V_GN_G:V_GN_B + 1], vecs[:, :, V_GN_G:V_GN_B + 1], 0.5, None,
                              ALU.mult).then_inc(s["vec_half"], 1)
            dve.wait_ge(s["w_gamma_in"], 16)
            dve.wait_ge(s["w_rec_in"], 16)
            for k in range(KC):
                dve.tensor_copy(w_raw[:, k, W_GAMMA].rearrange("p (h d) -> p h d", d=D),
                                gam[:, k].unsqueeze(2).to_broadcast([P, H, D])).then_inc(s["consts_dve"], 1)
                dve.tensor_reduce(msum[:, k], w_raw[:, k, W_V].rearrange("p (h d) -> p h d", d=D), AX.X,
                                  ALU.add).then_inc(s["consts_dve"], 1)
            dve.wait_ge(s["consts_dve"], 6)
            for k in range(KC):
                v3 = w_raw[:, k, W_V].rearrange("p (h d) -> p h d", d=D)
                dve.scalar_tensor_tensor(out=v3, in0=msum[:, k].unsqueeze(2).to_broadcast([P, H, D]), scalar=-1.0 / D,
                                         in1=v3, op0=ALU.mult, op1=ALU.add).then_inc(s["consts_dve"], 1)
            dve.wait_ge(s["consts_dve"], 8)
            for k in range(KC):
                dve.tensor_copy(w_hi[:, k], w_raw[:, k]).then_inc(s["rec_split"], 1)
                dve.wait_ge(s["rec_split"], 2 * k + 1)
                dve.tensor_tensor(w_lo[:, k], w_raw[:, k], w_hi[:, k].bitcast(F32), ALU.subtract).then_inc(s["rec_split"], 1)
            for stage, h in ORDER:
                if stage == "project":
                    rec_project(h)
                    if h == 0:
                        dve.wait_ge(s["w_gu_in"], 16)
                        raw = ffn1.HD[:].rearrange("p a b -> p (a b)")[:, 0:KC * 2 * INTER].rearrange("p (k n) -> p k n", k=KC)
                        dve.tensor_copy(gu_hi[:], raw).then_inc(s["gu_split"], 1)
                        dve.wait_ge(s["gu_split"], 1)
                        dve.tensor_tensor(gu_lo[:], raw, gu_hi[:].bitcast(F32), ALU.subtract).then_inc(s["gu_split"], 1)
                        dve.wait_ge(s["w_dn_in"], 32)
                        dve.wait_ge(s["scale_in"], 16)
                        dve.wait_ge(s["down_s_in"], 16)
                        for c in range(FCH):
                            rows = P if c < FULL else REST
                            op = dve.scalar_tensor_tensor(
                                out=w_down[0:rows, c], in0=w_down[0:rows, c], scalar=f_scale[0:rows, FCH + c:FCH + c + 1],
                                in1=down_b[0:rows], op0=ALU.mult, op1=ALU.mult)
                            if c >= FULL - 1:
                                op.then_inc(s["dn_scaled"], 1)
                elif stage == "norms":
                    rec_norms(h)
                elif stage == "memory":
                    rec_memory(h)
                elif stage == "group":
                    rec_group(h)
                elif stage == "out":
                    dve.wait_ge(s["wo_ps"], h + 1)
                    add_to_x(half_of_x(h), bank_pair("wo", h), s["rec_added"])
                    dve.wait_ge(s["rec_added"], h + 1)
                    layer_norm(1 + h, h * HT, HT)
                elif stage == "ffn":
                    if h == 0:
                        dve.wait_ge(s["gu_split"], 2)
                    ffn_half(0, h, lambda name: bank_pair(name, h))

            dve.wait_ge(s["ffn_added"], 2)
            layer_norm(3, 0, NT)
            dve.memset(S_rep, 0.0).then_inc(s["s_rep"], 1)
            for q in range(3):
                dve.tensor_copy(mask[32 * q:32 * q + 32], ident[32 * q:32 * q + 32, 32 * q:32 * q + B])
            dve.tensor_scalar(ones_r[:], ident[:], 0.0, 1.0, ALU.mult, ALU.add).then_inc(s["ones_r_done"], 1)
            dve.wait_ge(s["bo_in"], 16)
            dve.wait_ge(s["ln_done"], 4)
            dve.tensor_tensor(X[:], X[:], bo_b[:].unsqueeze(1).to_broadcast([P, NT, C]), ALU.add).then_inc(s["bo_added"], 1)
            dve.tensor_copy(XH[:], XN[:, :, 0:C]).then_inc(s["x_hi"], 1)
            for b in range(B):
                dve.wait_ge(s["g_hi"], b + 1)
                dve.tensor_copy(S_col[:, :, b:b + 1], ps[:, b, :, C:C + 1]).then_inc(s["s_cp"], 1)
                dve.tensor_tensor(G_lo[:, b], ps[:, b, :, 0:C], G_hi[:, b].bitcast(F32), ALU.subtract).then_inc(s["g_lo"], 1)
            dve.wait_ge(s["s_cp"], B)
            dve.wait_ge(s["s_rep"], 1)
            for q in range(3):
                dve.tensor_copy(S_rep[:, :, 32 * q:32 * q + B], S_col[:]).then_inc(s["s_rep"], 1)
            dve.wait_ge(s["s_rep"], 4)
            dve.tensor_copy(S_hi[:], S_rep).then_inc(s["s_rep_hi"], 1)
            dve.wait_ge(s["s_rep_hi"], 1)
            dve.tensor_tensor(S_lo[:], S_rep, S_hi[:].bitcast(F32), ALU.subtract).then_inc(s["s_rep_lo"], 1)
            dve.wait_ge(s["x_hi"], 1)
            dve.tensor_tensor(XL[:], XN[:, :, 0:C], XH[:].bitcast(F32), ALU.subtract).then_inc(s["x_lo"], 1)
            dve.wait_ge(s["x_lo"], 1)
            dve.wait_ge(s["bv_in"], 16)
            dve.wait_ge(s["g_lo"], B)
            for sm, per in ((s["raw_k_free"], 1), (s["raw_o_free"], 1), (s["raw_v_free"], 1), (s["bq_raw_free"], 1),
                            (s["wk_split"], 2), (s["wo_split"], 2), (s["wv_split"], 2), (s["bq_split"], 2), (s["r_sum"], 1),
                            (s["z_added"], 2 * B), (s["negmax"], NG), (s["bias_done"], NG), (s["rsum"], NG), (s["e_norm"], NG),
                            (s["p_lo"], B), (s["u_added"], 2 * NG), (s["a_added"], 2)):
                dve.sem_inc(sm, per)
            with dve.Fori(0, STEPS) as i:
                def split(raw, hi, lo, done, free):
                    dve.tensor_copy(hi[:], raw[:]).then_inc(done, 1)
                    dve.wait_ge(done, loop_value(i, 2, 1))
                    dve.tensor_tensor(lo[:], raw[:], hi[:].bitcast(F32), ALU.subtract).then_inc(done, 1)
                    dve.wait_ge(done, loop_value(i, 2, 2))
                    dve.sem_inc(free, 1)

                def softmax_bias(g):
                    dve.wait_ge(s["s_ps"], loop_value(i, NG, g + 1))
                    dve.wait_ge(s["exp_done"], loop_value(i, NG * B, (g - 1) * B))
                    dve.tensor_reduce(neg[:, g % 2], ps[:, S_PAIR[g // 2], g % 2].rearrange("p (b n) -> p b n", b=B),
                                      AX.X, ALU.max, negate=True).then_inc(s["negmax"], 1)
                    dve.wait_ge(s["negmax"], loop_value(i, NG, g + 1))
                    dve.tensor_scalar(e_bias[:, g % 2], neg[:, g % 2], SCALE, None, ALU.mult).then_inc(s["bias_done"], 1)

                def softmax_norm(g):
                    j = g % 2
                    dve.wait_ge(s["exp_done"], loop_value(i, NG * B, (g + 1) * B))
                    dve.reciprocal(e_inv[:, j], e_sum[:, j]).then_inc(s["rsum"], 1)
                    dve.wait_ge(s["rsum"], loop_value(i, NG, g + 1))
                    dve.tensor_tensor(E[:, j], E[:, j], e_inv[:, j].unsqueeze(2).to_broadcast([P, B, NQ]),
                                      ALU.mult).then_inc(s["e_norm"], 1)

                def add_values_bias(g):
                    dve.wait_ge(s["u_ps"], loop_value(i, NG, g + 1))
                    if g < HL:
                        dve.wait_ge(s["a_ps"], loop_value(i - 1, 2, 2))
                    else:
                        dve.wait_ge(s["a_ps"], loop_value(i, 2, 1))
                    if g == 0:
                        dve.wait_ge(s["w_cp"], loop_value(i, 1, 1))
                    for j in range(2):
                        dve.scalar_tensor_tensor(
                            out=U[:, g % HL, 2 * j:2 * j + 2], in0=w_sum[:, g % HL].unsqueeze(1).to_broadcast([P, 2, C]),
                            scalar=bv_c[:, bass.ds(i * NG + g, 1)],
                            in1=ps[:, U_PAIR[g], j].rearrange("p (b c) -> p b c", b=2), op0=ALU.mult,
                            op1=ALU.add).then_inc(s["u_added"], 1)

                def add_out(j):
                    dve.wait_ge(s["a_ps"], loop_value(i, 2, j + 1))
                    dst = X[:].rearrange("p (b r) c -> p b r c", r=R)[:, :, j]
                    dve.tensor_tensor(dst, dst, ps[:, A_PAIR[j]].rearrange("p a (b c) -> p (a b) c", c=C),
                                      ALU.add).then_inc(s["a_added"], 1)

                dve.wait_ge(s["wk_in"], 16 * (i + 1))
                split(raw_k, wk_hi, wk_lo, s["wk_split"], s["raw_k_free"])
                dve.wait_ge(s["bk_in"], 16 * (i + 1))
                dve.wait_ge(s["r_ps"], loop_value(i, 1, 1))
                dve.wait_ge(s["r_mask"], loop_value(i - 1, 1, 1))
                dve.scalar_tensor_tensor(out=r_row[:], in0=bk_b[:], scalar=float(T), in1=ps[:, 0, 0], op0=ALU.mult,
                                         op1=ALU.add).then_inc(s["r_sum"], 1)
                dve.wait_ge(s["bq_in"], 16 * (i + 1))
                dve.tensor_copy(bq_s[:], bq_b[:]).then_inc(s["bq_split"], 1)
                dve.wait_ge(s["bq_split"], loop_value(i, 2, 1))
                dve.tensor_tensor(bq_s[64:96], bq_b[64:96], bq_s[64:96].bitcast(F32), ALU.subtract).then_inc(s["bq_split"], 1)
                dve.wait_ge(s["bq_split"], loop_value(i, 2, 2))
                dve.sem_inc(s["bq_raw_free"], 1)
                dve.wait_ge(s["wo_in"], 16 * (i + 1))
                split(raw_o, wo_hi, wo_lo, s["wo_split"], s["raw_o_free"])
                for b in range(B):
                    dve.wait_ge(s["z_ps"], loop_value(i, B, b + 1))
                    for m in range(KC):
                        dve.scalar_tensor_tensor(out=Z[:, m, b], in0=bk_b[:], scalar=S_col[:, m, b:b + 1],
                                                 in1=ps[:, Z_PAIR[b], m], op0=ALU.mult, op1=ALU.add).then_inc(s["z_added"], 1)
                dve.wait_ge(s["wv_in"], 16 * (i + 1))
                split(raw_v, wv_hi, wv_lo, s["wv_split"], s["raw_v_free"])
                softmax_bias(0)
                softmax_bias(1)
                softmax_norm(0)
                softmax_norm(1)
                for b in range(B):
                    dve.wait_ge(s["p_hi"], loop_value(i, B, b + 1))
                    dve.tensor_tensor(P_lo[:, :, b].rearrange("p m l c -> p m (l c)"), ps[:, P_PAIR[b]],
                                      P_hi[:, :, b].rearrange("p m l c -> p m (l c)").bitcast(F32),
                                      ALU.subtract).then_inc(s["p_lo"], 1)
                softmax_bias(2)
                softmax_bias(3)
                softmax_norm(2)
                softmax_norm(3)
                add_values_bias(0)
                add_values_bias(1)
                add_out(0)
                add_values_bias(2)
                add_values_bias(3)
                add_out(1)

            dve.wait_ge(s["a_added"], loop_value(STEPS - 1, 2, 2))
            for h in range(2):
                layer_norm(4 + h, h * HT, HT)
            for h in range(2):
                ffn_half(1, h, lambda name: ps[:, F2_PAIR[name, h]])


LN_RUNS = [(0, NT), (0, HT), (HT, HT), (0, NT), (0, HT), (HT, HT)]

Z_PAIR = [1, 2, 3, 0]
S_PAIR = [2, 0]
P_PAIR = [3, 0, 1, 2]
T_PAIR = [3, 0]
U_PAIR = [1, 2, 1, 2]
A_PAIR = [3, 3]
F2_PAIR = {(n, h): (h * len(STAGE_SLOTS["ffn"]) + k) % 4 for h in range(2) for k, n in enumerate(STAGE_SLOTS["ffn"])}


def kernel(**inputs):
    import numpy as np
    import concourse.bacc as bacc
    from concourse.bass_utils import run_bass_kernel_spmd as run

    a = {n: np.asarray(v) for n, v in inputs.items()}
    rec = {n[len("L0_attn_a_"):]: v for n, v in a.items() if n.startswith("L0_attn_a_")}
    att = {n[len("L0_attn_b_"):]: v for n, v in a.items() if n.startswith("L0_attn_b_")}
    ff = {n[len("L0_ffn_"):]: v for n, v in a.items() if n.startswith("L0_ffn_")}

    def col(v):
        return v.reshape(-1, 1)

    vec = np.concatenate(
        [rec["conv_w"].reshape(C, TAPS), col(rec["conv_b"]), col(rec["ig_b"]), col(np.repeat(rec["gamma_b"], D)),
         col(rec["og_b"]), col(np.tile(rec["vn_g"], H)), col(np.tile(rec["vn_b"], H)), col(np.tile(rec["mn_g"], H)),
         col(np.tile(rec["mn_b"], H)), col(rec["gn_g"]), col(rec["gn_b"])], axis=1)
    w_rec = np.stack([rec[n].T for n in ("Wq", "Wk", "Wv", "ig_w", "og_w")], axis=1)

    gate_up = [ff[n].T for n in ("gate_w", "up_w")]
    w_gu = np.concatenate([w[:, c * P:(c + 1) * P] for c in range(FCH) for w in gate_up], axis=1)

    def chunk_cols(v):
        return np.concatenate([v, np.zeros(FCH * P - INTER, v.dtype)]).reshape(FCH, P).T

    ffn_scale = np.concatenate([chunk_cols(ff["gate_s"]), chunk_cols(ff["up_s"])], axis=1)

    heads = np.array([[r * Y_BLOCKS + i * HL + l for r in range(2) for l in range(HL)] for i in range(STEPS)])

    def by_step(w):
        w = w.reshape(-1, NQ, NH)[:, :, heads]
        return w.transpose(2, 0, 3, 1).reshape(STEPS, -1, NG * NQ)

    wo = att["Wo"].reshape(STEPS, HL, T, C).transpose(0, 2, 1, 3).reshape(STEPS, T, HL * C)
    arrays = {
        "x": a["L0_attn_a_x"], "w_rec": w_rec, "w_gamma": rec["gamma_w"].T, "w_rec_out": rec["Wo"].T, "vec": vec,
        "w_gu": w_gu, "w_dn": ff["down_w"].T, "ffn_scale": ffn_scale, "down_s": ff["down_s"],
        "wk": by_step(att["Wk"]), "wv": by_step(att["Wv"]), "wq": by_step(att["Wq"]), "wo": wo,
        "bk": by_step(att["bk"][None])[:, 0], "bq": by_step(att["bq"][None])[:, 0],
        "bv": by_step(att["bv"][None])[:, 0].reshape(NH, NQ).T, "bo": att["bo"],
    }
    nc = bacc.Bacc("TRN2", target_bir_lowering=False, num_devices=1)
    arrays = {n: np.ascontiguousarray(v) for n, v in arrays.items()}
    args = [nc.dram_tensor(n, v.shape, mybir.dt.from_np(v.dtype), kind="ExternalInput").ap() for n, v in arrays.items()]
    args.append(nc.dram_tensor("y", (B, T, C), F32, kind="ExternalOutput").ap())
    hybrid_block(nc, *args)
    r = run(nc, [arrays], core_ids=[0])
    return r.results[0]["y"]
```

```python
from contextlib import ExitStack

import concourse.bass as bass
from concourse import mybir

F32 = mybir.dt.float32
F32R = mybir.dt.float32r
ACT = mybir.ActivationFunctionType
ALU = mybir.AluOpType
AX = mybir.AxisListType

P = 128
B, T, C = 4, 256, 256
H, D = 16, 16
TAPS = 4
NH, NQ = 16, 128
INTER = 704
R = T // P
NT = B * R
KC = C // P
HALF = B * T // 2
HT = NT // 2
HB = B // 2
EPS = 1e-5
FULL = INTER // P
REST = INTER - FULL * P
FCH = FULL + 1
NG = 4
STEPS = NH // NG
HL = NG // 2
Y_BLOCKS = NH // 2
SCALE = float(NQ) ** -0.5
BANK = 512

V_TAP, V_CONV_B, V_IG_B, V_GAMMA_B, V_OG_B, V_VN_G, V_VN_B, V_MN_G, V_MN_B, V_GN_G, V_GN_B = 0, 4, 5, 6, 7, 8, 9, 10, 11, 12, 13
N_VEC = 14
W_K, W_V, W_Q, W_IG, W_OG, W_GAMMA = range(6)

ORDER = [
    ("xt", 0), ("conv", 0), ("k", 0), ("v", 0), ("silu", 0), ("q", 0), ("lx", 1), ("nv", 0), ("nk", 0), ("nq", 0),
    ("xt", 1), ("rk", 0), ("ig", 0), ("gamma", 0), ("og", 0), ("scan", 0), ("k", 1), ("v", 1), ("conv", 1), ("mc", 0),
    ("q", 1), ("mv", 0), ("silu", 1), ("nv", 1), ("nk", 1), ("nq", 1), ("oc", 0), ("ov", 0), ("rk", 1), ("ig", 1),
    ("gamma", 1), ("wo", 0), ("ln", 0), ("og", 1), ("ft", 0), ("scan", 1), ("gu0", 0), ("gu1", 0), ("mc", 1),
    ("gu2", 0), ("mv", 1), ("gu3", 0), ("gu4", 0), ("oc", 1), ("gu5", 0), ("ov", 1), ("dna", 0), ("wo", 1), ("ln", 1),
    ("dnb", 0), ("ft", 1), ("lc", 0), ("gu0", 1), ("gu1", 1), ("gu2", 1), ("gu3", 1), ("gu4", 1), ("gu5", 1),
    ("dna", 1), ("lc", 2), ("dnb", 1), ("lc", 3), ("gm", 0), ("gm", 1), ("gm", 2), ("gm", 3)]
ORDER2 = [("ln", 0), ("ft", 0), ("ln", 1), ("gu0", 0), ("gu1", 0), ("ft", 1), ("gu2", 0), ("gu3", 0), ("gu4", 0),
          ("gu5", 0), ("dna", 0), ("dnb", 0), ("gu0", 1), ("gu1", 1), ("gu2", 1), ("gu3", 1), ("gu4", 1),
          ("gu5", 1), ("dna", 1), ("dnb", 1)]
NO_PSUM = ("conv", "silu", "scan", "rk", "ln", "lx", "lc", "dnb")
LOG_EXP, SILU_TANH = "natural_log_exp_and_others", "silu_and_others"
TABLES = {"rk": LOG_EXP, "nv": LOG_EXP, "mv": LOG_EXP, "ov": LOG_EXP,
          "silu": SILU_TANH, "ig": SILU_TANH, "gamma": SILU_TANH, "og": SILU_TANH}
LN_X, LN_FFN, LN_CHAN, LN_FFN2 = range(4)


def upto(h, m):
    return KC * h + m + 1


def pair_plan(order):
    pair, before, held = {}, {}, [None] * 4
    due = [-4, -3, -2, -1]
    for n, step in enumerate(s for s in order if s[0] not in NO_PSUM):
        q = due.index(min(due))
        pair[step], before[step] = q, held[q]
        held[q] = step
        due[q] = n + (2.5 if step[0] in ("mc", "oc") else 0)
    return pair, before


def tables_ahead(n):
    for name, _ in ORDER[n:]:
        if name in TABLES or name.startswith("gu"):
            return TABLES.get(name, SILU_TANH)
    return LOG_EXP


class FfnBuffers:

    def __init__(self, XTh, XTl, HD, SG):
        self.XTh, self.XTl, self.HD, self.SG = XTh, XTl, HD, SG


def loop_value(i, per_step, nth):
    return (i + 1) * per_step + nth


def hybrid_block(nc, x, w_rec, w_gamma, w_rec_out, vec, w_gu, w_dn, ffn_scale, down_s,
                 wk, wv, wq, wo, bk, bq, bv, bo, out):
    pair, before = pair_plan(ORDER)
    pair2, before2 = pair_plan(ORDER2)
    with ExitStack() as ctx:
        def sem(name):
            return ctx.enter_context(nc.semaphore(name))

        def sb(name, shape, dt=F32, scope=ctx):
            return scope.enter_context(nc.sbuf_tensor(name, shape, dt))

        s = {n: sem(n) for n in """
            x0_in x1_in x23_in w_kv_in w_rest_in w_gamma_in w_out_in vec_in w_gu_in w_dn_in gu_again_in scale_in down_s_in
            wk_in wv_in wq_in wo_in bk_in bq_in bv_in bo_in x_out
            consts_pool consts_dve centred gamma_rep vec_half rec_hi rec_split gu_split dn_scaled
            ln_stat ln_agg ln_eps ln_rstd ln_done
            xt_ps xt_f xt_hi xt_lo conv_m0 conv_m1 silu_done xc_hi xc_lo
            q_ps k_ps v_ps ig_ps og_ps gamma_ps q_cp k_cp v_cp q_sq k_sq v_sq ti_done to_done tg_done gamma_done
            nq_ps nk_ps nv_ps nq_max nk_max nq_ln nk_ln nv_ln rq_done rk_done rv_done
            qn_done k_n k_g v_n v_a b_done mem_done
            mc_ps mc_sq mv_ps mv_ln r1_done y_n y_a o_done
            oc_ps oc_sq ov_ps ov_ln r2_done z_n z_a z_done wo_ps rec_added
            ft_ps ft_hi ft_lo gu_ps silu_g hd_done dn_ps ffn_added
            bo_added x_hi x_lo g_ps g_hi g_lo s_cp s_zero s_hi s_lo mask_done ones_r_done
            raw_k_free raw_o_free raw_v_free wk_split wo_split wv_split bq_split bq_raw_free
            r_ps r_sum r_mask r_hi r_lo z_ps z_added w_ps w_cp s_ps negmax bias_done exp_done rsum
            e_norm p_ps p_hi p_lo t_ps t_cp u_ps u_added a_ps a_added""".split()}

        ps = ctx.enter_context(nc.psum_tensor("ps", [P, 4, 2, BANK], F32))

        X = sb("X", [P, NT, C])
        XN = sb("XN", [P, NT, C + 2])
        gu_hi = sb("gu_hi", [P, KC, 2 * INTER], F32R)
        gu_lo = sb("gu_lo", [P, KC, 2 * INTER], F32R)
        w_down = sb("w_down", [P, FCH, C])
        f_scale = sb("f_scale", [P, 2 * FCH])
        ident = sb("ident", [P, P])
        heads_ones = sb("heads_ones", [P, P])
        centre = sb("centre", [P, P])
        eps_col = sb("eps_col", [P, 1])
        minus_half = sb("minus_half", [P, NT])
        stats = sb("stats", [P, NT, 6])
        agg = sb("agg", [P, NT, 2])
        var_eps = sb("var_eps", [P, NT])
        rstd = sb("rstd", [P, NT])

        one = ctx.enter_context(ExitStack())
        w_hi = sb("w_hi", [P, KC, 6, C], F32R, one)
        w_lo = sb("w_lo", [P, KC, 6, C], F32R, one)
        q_t, k_t, v_t, sq_q, sq_k, sq_v, t_og, mem = (
            sb(n, [P, 2, KC, HALF], F32, one) for n in ("q_t", "k_t", "v_t", "sq_q", "sq_k", "sq_v", "t_og", "mem"))
        w_out = sb("w_out", [P, KC, C], F32, one)
        down_b = sb("down_b", [P, C], F32, one)
        vecs = sb("vecs", [P, KC, N_VEC], F32, one)
        gam = sb("gam", [P, KC, H], F32, one)
        msum = sb("msum", [P, KC, H], F32, one)
        XCf = sb("XCf", [P, KC, HALF], F32, one)
        XCh = sb("XCh", [P, KC, HALF], F32R, one)
        XCl = sb("XCl", [P, KC, HALF], F32R, one)
        gates = sb("gates", [P, 2, 2, KC, HALF], F32, one)
        t_ig, t_ga = gates[:, 0], gates[:, 1]
        XTf = sb("XTf", [P, KC, HALF], F32, one)
        XTh = sb("XTh", [P, KC, HALF], F32R, one)
        XTl = sb("XTl", [P, KC, HALF], F32R, one)
        HD = sb("HD", [P, FCH, HALF], F32, one)
        SG = sb("SG", [P, 2, HALF], F32, one)
        ffn1 = FfnBuffers(
            (XTh, XCh), (XTl, XCl),
            (HD, gates[:].rearrange("p a h m t -> p (a h m) t")[:, 0:FCH]), SG)
        HD_flat = HD[:].rearrange("p a b -> p (a b)")
        w_raw = HD_flat.rearrange("p (k w c) -> p k w c", k=KC, w=6)
        gu_raw = HD_flat[:, 0:KC * 2 * INTER].rearrange("p (k n) -> p k n", k=KC)
        one.close()

        two = ctx.enter_context(ExitStack())
        raw_k = sb("raw_k", [P, KC, NG * NQ], F32, two)
        raw_v = sb("raw_v", [P, KC, NG * NQ], F32, two)
        raw_o = sb("raw_o", [P, R, HL * C], F32, two)
        raw_q = sb("raw_q", [P, KC, NG * NQ], F32, two)
        wk_hi = sb("wk_hi", [P, KC, NG * NQ], F32R, two)
        wk_lo = sb("wk_lo", [P, KC, NG * NQ], F32R, two)
        wo_hi = sb("wo_hi", [P, R, HL * C], F32R, two)
        wo_lo = sb("wo_lo", [P, R, HL * C], F32R, two)
        bk_b = sb("bk_b", [P, NG * NQ], F32, two)
        bq_b = sb("bq_b", [96, NG * NQ], F32, two)
        bq_s = sb("bq_s", [96, NG * NQ], F32R, two)
        bv_c = sb("bv_c", [P, NH], F32, two)
        bo_b = sb("bo_b", [P, C], F32, two)
        XH = sb("XH", [P, NT, C], F32R, two)
        XL = sb("XL", [P, NT, C], F32R, two)
        G_hi = sb("G_hi", [P, B, KC, C], F32R, two)
        G_lo = sb("G_lo", [P, B, KC, C], F32R, two)
        S_col = sb("S_col", [P, KC, B], F32, two)
        S_hi = sb("S_hi", [P, KC, P], F32R, two)
        S_lo = sb("S_lo", [P, KC, P], F32R, two)
        ones_r = sb("ones_r", [P, P], F32R, two)
        mask = sb("mask", [96, B], F32, two)
        wv_hi = sb("wv_hi", [P, KC, NG * NQ], F32R, two)
        wv_lo = sb("wv_lo", [P, KC, NG * NQ], F32R, two)
        Z = sb("Z", [P, KC, B, NG * NQ], F32, two)
        r_row = sb("r_row", [P, NG * NQ], F32, two)
        r_s = sb("r_s", [96, NG, B, NQ], F32R, two)
        r_masked = XN[:].rearrange("p a b -> p (a b)")[0:96, 0:NG * B * NQ].rearrange(
            "p (g b n) -> p g b n", g=NG, b=B)
        w_sum = sb("w_sum", [P, HL, C], F32, two)
        E = sb("E", [P, 2, B, NQ], F32, two)
        neg = sb("neg", [P, 2, B], F32, two)
        e_bias = sb("e_bias", [P, 2, B], F32, two)
        e_sum = sb("e_sum", [P, 2, B], F32, two)
        e_inv = sb("e_inv", [P, 2, B], F32, two)
        ET = sb("ET", [P, NG, B, NQ], F32, two)
        P_hi = sb("P_hi", [P, KC, B, HL, C], F32R, two)
        P_lo = sb("P_lo", [P, KC, B, HL, C], F32R, two)
        U = sb("U", [P, HL, B, C], F32, two)
        two.close()

        ffn2 = FfnBuffers(
            [sb(f"XTh2{h}", [P, KC, HALF], F32R) for h in range(2)], [sb(f"XTl2{h}", [P, KC, HALF], F32R) for h in range(2)], [sb(f"HD2{h}", [P, FCH, HALF]) for h in range(2)],
            sb("SG2", [P, 2, HALF]))
        ffn = [ffn1, ffn2]

        freed, freed2 = {}, {}
        for h in range(2):
            freed["xt", h] = [(s["xt_f"], upto(h, 1))]
            for name, done in (("ig", "ti_done"), ("og", "to_done"), ("q", "q_cp"), ("k", "k_cp"), ("v", "v_cp"),
                               ("gamma", "tg_done"), ("nq", "nq_max"), ("nk", "nk_max"), ("nv", "nv_ln"), ("mc", "y_n"),
                               ("mv", "mv_ln"), ("oc", "z_n"), ("ov", "ov_ln")):
                freed[name, h] = [(s[done], upto(h, 1))]
            freed["wo", h] = [(s["rec_added"], HB * (h + 1))]
            for f, table in enumerate((freed, freed2)):
                n = 2 * f + h
                table["ft", h] = [(s["ft_lo"], upto(n, 1))]
                table["dna", h] = [(s["ffn_added"], HB * (n + 1))]
                for c in range(FCH):
                    table[f"gu{c}", h] = [(s["hd_done"], n * FCH + c + 1)]
        for b in range(B):
            freed["gm", b] = [(s["g_lo"], b + 1), (s["s_cp"], b + 1)]

        def bank_pair(name, h):
            return ps[:, pair[name, h]]

        def bank_pair2(name, h):
            return ps[:, pair2[name, h]]

        def gu_before(f, h):
            return (2 * f + h) * FCH

        def half_batches(h):
            return range(HB * h, HB * (h + 1))

        def batches_of_lc(b):
            return half_batches(0) if b == 0 else range(b, b + 1)

        def token_cols(t):
            b, r = t // R, t % R
            return slice(b * T + r, (b + 1) * T, R)

        def by_tile(bank):
            return bank.rearrange("p (b r n) -> p b r n", b=HB, r=R)

        def in_time(row):
            return row.rearrange("p (b n r) -> p b r n", b=HB, r=R)

        block = ctx.enter_context(nc.Block())

        @block.sync
        def _(sp):
            x_view = X[:].rearrange("p (b r) c -> p b (r c)", r=R)
            x_rows = x.rearrange("b (p r) c -> p b (r c)", r=R)
            w_rows = w_rec.rearrange("(k p) w c -> p k w c", p=P)
            sp.dma_start(x_view[:, 0:1], x_rows[:, 0:1]).then_inc(s["x0_in"], 16)
            sp.dma_start(x_view[:, 1:HB], x_rows[:, 1:HB]).then_inc(s["x1_in"], 16)
            sp.dma_start(w_raw[:, :, W_K:W_V + 1, :], w_rows[:, :, W_K:W_V + 1]).then_inc(s["w_kv_in"], 16)
            sp.dma_start(vecs[:], vec.rearrange("(k p) v -> p k v", p=P)).then_inc(s["vec_in"], 16)
            sp.dma_start(gam[:], w_gamma.rearrange("(k p) h -> p k h", p=P)).then_inc(s["w_gamma_in"], 16)
            sp.dma_start(w_raw[:, :, W_Q:W_OG + 1, :], w_rows[:, :, W_Q:W_OG + 1]).then_inc(s["w_rest_in"], 16)
            sp.dma_start(x_view[:, HB:B], x_rows[:, HB:B]).then_inc(s["x23_in"], 16)
            sp.dma_start(w_out[:], w_rec_out.rearrange("(k p) c -> p k c", p=P)).then_inc(s["w_out_in"], 16)
            sp.dma_start(f_scale[:], ffn_scale).then_inc(s["scale_in"], 16)
            sp.wait_ge(s["rec_split"], 6)
            sp.dma_start(gu_raw, w_gu.rearrange("(k p) n -> p k n", p=P)).then_inc(s["w_gu_in"], 16)
            sp.dma_start(w_down[:, 0:FULL, :], w_dn[0:FULL * P].rearrange("(n p) c -> p n c", p=P)).then_inc(s["w_dn_in"], 16)
            sp.dma_start(w_down[0:REST, FULL, :], w_dn[FULL * P:INTER]).then_inc(s["w_dn_in"], 16)
            sp.dma_start(down_b[:], down_s.partition_broadcast(P)).then_inc(s["down_s_in"], 16)

            def load_step(i):
                sp.dma_start(raw_k[:], wk[i].rearrange("(k p) n -> p k n", p=P)).then_inc(s["wk_in"], 16)
                sp.dma_start(bk_b[:], bk[i].partition_broadcast(P)).then_inc(s["bk_in"], 16)
                sp.dma_start(raw_o[:], wo[i].rearrange("(p r) n -> p r n", r=R)).then_inc(s["wo_in"], 16)
                sp.dma_start(raw_v[:], wv[i].rearrange("(k p) n -> p k n", p=P)).then_inc(s["wv_in"], 16)
                sp.dma_start(bq_b[:], bq[i].partition_broadcast(96)).then_inc(s["bq_in"], 16)
                sp.dma_start(raw_q[:], wq[i].rearrange("(k p) n -> p k n", p=P)).then_inc(s["wq_in"], 16)

            sp.wait_ge(s["wo_ps"], B)
            sp.dma_start(bv_c[:], bv).then_inc(s["bv_in"], 16)
            sp.dma_start(bo_b[:], bo.partition_broadcast(P)).then_inc(s["bo_in"], 16)
            load_step(0)
            with sp.Fori(1, STEPS) as i:
                sp.wait_ge(s["raw_k_free"], loop_value(i - 1, 1, 1))
                sp.dma_start(raw_k[:], wk[bass.ds(i, 1)].rearrange("o (k p) n -> p (o k) n", p=P)).then_inc(s["wk_in"], 16)
                sp.wait_ge(s["z_added"], loop_value(i - 1, 2 * B, 2 * B))
                sp.wait_ge(s["r_sum"], loop_value(i - 1, 1, 1))
                sp.dma_start(bk_b[:], bk[bass.ds(i, 1)].rearrange("o n -> (o n)").partition_broadcast(P)).then_inc(s["bk_in"], 16)
                sp.wait_ge(s["raw_o_free"], loop_value(i - 1, 1, 1))
                sp.dma_start(raw_o[:], wo[bass.ds(i, 1)].rearrange("o (p r) n -> p (o r) n", r=R)).then_inc(s["wo_in"], 16)
                sp.wait_ge(s["raw_v_free"], loop_value(i - 1, 1, 1))
                sp.dma_start(raw_v[:], wv[bass.ds(i, 1)].rearrange("o (k p) n -> p (o k) n", p=P)).then_inc(s["wv_in"], 16)
                sp.wait_ge(s["bq_raw_free"], loop_value(i - 1, 1, 1))
                sp.dma_start(bq_b[:], bq[bass.ds(i, 1)].rearrange("o n -> (o n)").partition_broadcast(96)).then_inc(s["bq_in"], 16)
                sp.wait_ge(s["s_ps"], loop_value(i - 1, NG, NG))
                sp.dma_start(raw_q[:], wq[bass.ds(i, 1)].rearrange("o (k p) n -> p (o k) n", p=P)).then_inc(s["wq_in"], 16)

            o_view = out.rearrange("b (p r) c -> p b (r c)", r=R)
            for b in range(B):
                sp.wait_ge(s["ffn_added"], B + b + 1)
                sp.dma_start(o_view[:, b], x_view[:, b]).then_inc(s["x_out"], 16)
            sp.wait_ge(s["x_out"], 16 * B)

        @block.gpsimd
        def _(pool):
            pool.memset(ident[:], 0.0).then_inc(s["consts_pool"], 1)
            pool.memset(heads_ones[:], 1.0).then_inc(s["consts_pool"], 1)
            pool.memset(eps_col[:], EPS).then_inc(s["consts_pool"], 1)
            pool.memset(minus_half[:], -0.5).then_inc(s["consts_pool"], 1)
            pool.wait_ge(s["consts_pool"], 4)
            pool.affine_select(out=ident[:], in_=ident[:], compare_op=ALU.not_equal, fill=1.0, base=0,
                               pattern=[[-1, P]], channel_multiplier=1).then_inc(s["consts_pool"], 1)
            blocks = heads_ones[:].rearrange("p (h d) -> p h d", d=D)
            pool.affine_select(out=blocks, in_=blocks, compare_op=ALU.is_ge, fill=0.0, base=0,
                               pattern=[[-D, P // D], [0, D]], channel_multiplier=1).then_inc(s["consts_pool"], 1)
            pool.wait_ge(s["consts_pool"], 6)
            pool.affine_select(out=blocks, in_=blocks, compare_op=ALU.is_ge, fill=0.0, base=D - 1,
                               pattern=[[D, P // D], [0, D]], channel_multiplier=-1).then_inc(s["consts_pool"], 1)

            def layer_norm(kind, batches):
                for b in batches:
                    tiles = slice(R * b, R * (b + 1))
                    pool.wait_ge(s["ln_eps"], B * kind + b + 1)
                    pool.tensor_tensor(rstd[:, tiles], var_eps[:, tiles], minus_half[:, 0:R],
                                       ALU.pow).then_inc(s["ln_rstd"], 1)

            def step_silu(h):
                if h:
                    pool.wait_ge(s["og_ps"], upto(0, 1))
                for m in range(KC):
                    pool.wait_ge(s["silu_done"], upto(h, m))
                    pool.tensor_scalar(XCh[:, m], XCf[:, m], 1.0, 0.0, ALU.mult, ALU.add).then_inc(s["xc_hi"], 1)

            def step_rk(h):
                for m in range(KC):
                    pool.wait_ge(s["rq_done"], upto(h, m))
                    pool.wait_ge(s["q_cp"], upto(h, m))
                    pool.tensor_tensor(q_t[:, h, m], q_t[:, h, m], sq_q[:, h, m], ALU.mult).then_inc(s["qn_done"], 1)

            def split_gate_up():
                pool.wait_ge(s["w_gu_in"], 16)
                pool.tensor_scalar(gu_hi[:], gu_raw, 1.0, 0.0, ALU.mult, ALU.add).then_inc(s["gu_split"], 1)
                pool.wait_ge(s["gu_split"], 1)
                pool.tensor_tensor(gu_lo[:], gu_raw, gu_hi[:].bitcast(F32), ALU.subtract).then_inc(s["gu_split"], 1)

            layer_norm(LN_X, half_batches(0))
            for step, h in ORDER:
                if step == "lx":
                    layer_norm(LN_X, half_batches(h))
                elif step == "silu":
                    step_silu(h)
                    if h == 1:
                        split_gate_up()
                elif step == "rk":
                    step_rk(h)
                elif step == "ln":
                    layer_norm(LN_FFN, half_batches(h))
                elif step == "lc":
                    layer_norm(LN_CHAN, batches_of_lc(h))

            pool.wait_ge(s["mask_done"], 3)
            pool.sem_inc(s["r_mask"], 1)
            pool.sem_inc(s["r_lo"], 1)
            with pool.Fori(0, STEPS) as i:
                pool.wait_ge(s["r_sum"], loop_value(i, 1, 1))
                pool.wait_ge(s["r_lo"], loop_value(i - 1, 1, 1))
                for g in range(NG):
                    rm = pool.tensor_tensor(
                        r_masked[:, g],
                        r_row[0:96, g * NQ:(g + 1) * NQ].unsqueeze(1).to_broadcast([96, B, NQ]),
                        mask[:].unsqueeze(2).to_broadcast([96, B, NQ]), ALU.mult)
                rm.then_inc(s["r_mask"], 1)
                pool.wait_ge(s["r_hi"], loop_value(i, 1, 1))
                pool.wait_ge(s["r_mask"], loop_value(i, 1, 1))
                pool.tensor_tensor(r_s[32:64], r_masked[32:64], r_s[32:64].bitcast(F32),
                                   ALU.subtract).then_inc(s["r_lo"], 1)
            for step, h in ORDER2:
                if step == "ln":
                    layer_norm(LN_FFN2, half_batches(h))

        @block.scalar
        def _(act):
            def rsqrt_of(src, dst, scale, bias, ln_sem, done_sem, h, ready):
                for m in range(KC):
                    act.wait_ge(ready, upto(h, m))
                    act.activation(dst[:, m], src[:, m], ACT.Ln, scale=scale, bias=bias).then_inc(ln_sem, 1)
                for m in range(KC):
                    act.wait_ge(ln_sem, upto(h, m))
                    act.activation(dst[:, m], dst[:, m], ACT.Exp, scale=-0.5).then_inc(done_sem, 1)

            def step_xt(h):
                for m in range(KC):
                    act.wait_ge(s["xt_ps"], upto(h, m))
                    if h:
                        act.wait_ge(s["q_ps"], upto(0, 1))
                    act.copy(in_time(XTh[:, m]), by_tile(bank_pair("xt", h)[:, m])).then_inc(s["xt_hi"], 1)
                for m in range(KC):
                    act.wait_ge(s["xt_lo"], upto(h, m))
                    if h:
                        act.wait_ge((s["conv_m0"], s["conv_m1"])[m], TAPS)
                    act.copy(in_time(XTf[:, m]), by_tile(bank_pair("xt", h)[:, m])).then_inc(s["xt_f"], 1)

            def step_silu(h):
                for m, conv in enumerate((s["conv_m0"], s["conv_m1"])):
                    act.wait_ge(conv, TAPS * (h + 1))
                    act.activation(XCf[:, m], XCf[:, m], ACT.Silu,
                                   bias=vecs[:, m, V_CONV_B:V_CONV_B + 1]).then_inc(s["silu_done"], 1)

            def square_and_copy(name, h, dst, sq):
                for m in range(KC):
                    act.wait_ge(s[name + "_ps"], upto(h, m))
                    act.activation(sq[:, h, m], bank_pair(name, h)[:, m], ACT.Square).then_inc(s[name + "_sq"], 1)
                for m in range(KC):
                    act.copy(dst[:, h, m], bank_pair(name, h)[:, m]).then_inc(s[name + "_cp"], 1)

            def gate(name, h, dst, done, col):
                act.wait_ge(s["vec_half"], 1)
                for m in range(KC):
                    act.wait_ge(s[name + "_ps"], upto(h, m))
                    act.activation(dst[:, h, m], bank_pair(name, h)[:, m], ACT.Tanh, scale=0.5,
                                   bias=vecs[:, m, col:col + 1]).then_inc(done, 1)

            def step_nv(h):
                rsqrt_of(bank_pair("nv", h), sq_v[:, h], 1.0 / D, eps_col[:], s["nv_ln"], s["rv_done"], h, s["nv_ps"])

            def step_rk(h):
                rsqrt_of(sq_k[:, h], sq_k[:, h], 1.0, 0.0, s["nk_ln"], s["rk_done"], h, s["nk_max"])
                rsqrt_of(sq_q[:, h], sq_q[:, h], 1.0, 0.0, s["nq_ln"], s["rq_done"], h, s["nq_max"])

            def step_mc(h):
                for m in range(KC):
                    act.wait_ge(s["mc_ps"], upto(h, m))
                    act.wait_ge(s["v_n"], upto(h, m))
                    act.activation(sq_v[:, h, m], bank_pair("mc", h)[:, m], ACT.Square).then_inc(s["mc_sq"], 1)

            def step_mv(h):
                rsqrt_of(bank_pair("mv", h), sq_v[:, h], 1.0 / D, eps_col[:], s["mv_ln"], s["r1_done"], h, s["mv_ps"])

            def step_oc(h):
                for m in range(KC):
                    act.wait_ge(s["oc_ps"], upto(h, m))
                    act.wait_ge(s["qn_done"], upto(h, m))
                    act.activation(sq_q[:, h, m], bank_pair("oc", h)[:, m], ACT.Square).then_inc(s["oc_sq"], 1)

            def step_ov(h):
                rsqrt_of(bank_pair("ov", h), sq_q[:, h], 1.0 / D, eps_col[:], s["ov_ln"], s["r2_done"], h, s["ov_ps"])

            def step_gm(b):
                act.wait_ge(s["g_ps"], b + 1)
                act.copy(G_hi[:, b], bank_pair("gm", b)[:, :, 0:C]).then_inc(s["g_hi"], 1)

            def round_weights(block_):
                act.copy(w_hi[:, :, block_], w_raw[:, :, block_]).then_inc(s["rec_hi"], 1)

            def step_ft(f, h, psum):
                if f == 0:
                    act.wait_ge(s["q_ps"], upto(1, 1))
                    act.wait_ge(s["og_ps"], upto(1, 1))
                for m in range(KC):
                    act.wait_ge(s["ft_ps"], upto(2 * f + h, m))
                    act.copy(in_time(ffn[f].XTh[h][:, m]), by_tile(psum[:, m])).then_inc(s["ft_hi"], 1)

            def step_gu(f, h, c, psum):
                w, at = ffn[f], gu_before(f, h) + c
                rows = P if c < FULL else REST
                act.wait_ge(s["scale_in"], 16)
                act.wait_ge(s["gu_ps"], at + 1)
                if at % (2 * FCH) >= 2:
                    act.wait_ge(s["hd_done"], at - 1)
                act.activation(w.SG[0:rows, at % 2], psum[0:rows, 0], ACT.Silu,
                               scale=f_scale[0:rows, c:c + 1]).then_inc(s["silu_g"], 1)

            act.wait_ge(s["w_kv_in"], 16)
            round_weights(W_K)
            act.wait_ge(s["consts_pool"], 7)
            act.wait_ge(s["vec_in"], 16)
            for n, (step, h) in enumerate(ORDER):
                if n == 0 or tables_ahead(n) != tables_ahead(n - 1):
                    act.preload_act_table_set(tables_ahead(n))
                if step == "xt":
                    step_xt(h)
                    if h == 0:
                        act.wait_ge(s["centred"], 4)
                        round_weights(W_V)
                        act.wait_ge(s["w_rest_in"], 16)
                        for block_ in (W_Q, W_IG, W_OG):
                            round_weights(block_)
                        act.wait_ge(s["gamma_rep"], 2)
                        round_weights(W_GAMMA)
                elif step == "silu":
                    step_silu(h)
                elif step == "k":
                    square_and_copy("k", h, k_t, sq_k)
                elif step == "v":
                    square_and_copy("v", h, v_t, sq_v)
                elif step == "q":
                    square_and_copy("q", h, q_t, sq_q)
                elif step == "ig":
                    gate("ig", h, t_ig, s["ti_done"], V_IG_B)
                elif step == "gamma":
                    gate("gamma", h, t_ga, s["tg_done"], V_GAMMA_B)
                elif step == "og":
                    gate("og", h, t_og, s["to_done"], V_OG_B)
                elif step == "nv":
                    step_nv(h)
                elif step == "rk":
                    step_rk(h)
                elif step == "mc":
                    step_mc(h)
                elif step == "mv":
                    step_mv(h)
                elif step == "oc":
                    step_oc(h)
                elif step == "ov":
                    step_ov(h)
                elif step == "ft":
                    step_ft(0, h, bank_pair("ft", h))
                elif step.startswith("gu"):
                    step_gu(0, h, int(step[2:]), bank_pair(step, h))
                elif step == "gm":
                    step_gm(h)

            for sm, per in ((s["r_hi"], 1), (s["w_cp"], 1), (s["exp_done"], NG * B), (s["p_hi"], B), (s["t_cp"], 2)):
                act.sem_inc(sm, per)
            act.preload_act_table_set(LOG_EXP)
            with act.Fori(0, STEPS) as i:
                act.wait_ge(s["r_mask"], loop_value(i, 1, 1))
                act.wait_ge(s["s_ps"], loop_value(i - 1, NG, NG))
                act.copy(r_s[:], r_masked).then_inc(s["r_hi"], 1)
                act.wait_ge(s["w_ps"], loop_value(i, 1, 1))
                act.wait_ge(s["u_added"], loop_value(i - 1, 2 * NG, 2 * NG))
                act.copy(w_sum[:].rearrange("p a c -> p (a c)"), ps[:, 1, 0, :]).then_inc(s["w_cp"], 1)

                def exps(g):
                    j = g % 2
                    act.wait_ge(s["bias_done"], loop_value(i, NG, g + 1))
                    act.wait_ge(s["t_ps"], loop_value(i, 2, g // 2))
                    act.wait_ge(s["e_norm"], loop_value(i, NG, g - 1))
                    for b in range(B):
                        act.activation(E[:, j, b], ps[:, S_PAIR[g // 2], j, b * NQ:(b + 1) * NQ], ACT.Exp,
                                       scale=SCALE, bias=e_bias[:, j, b:b + 1],
                                       accum_out=e_sum[:, j, b:b + 1]).then_inc(s["exp_done"], 1)

                def transposed(j):
                    act.wait_ge(s["t_ps"], loop_value(i, 2, j + 1))
                    act.wait_ge(s["a_ps"], loop_value(i - 1, 4, 2 * j + 2))
                    act.copy(ET[:, 2 * j:2 * j + 2].rearrange("p g b n -> p g (b n)"),
                             ps[:, T_PAIR[j]]).then_inc(s["t_cp"], 1)

                def round_p(b):
                    act.wait_ge(s["p_ps"], loop_value(i, B, b + 1))
                    act.wait_ge(s["u_ps"], loop_value(i - 1, 2 * NG, 2 * NG))
                    act.copy(P_hi[:, :, b].rearrange("p m l c -> p m (l c)"), ps[:, P_PAIR[b]]).then_inc(s["p_hi"], 1)

                round_p(0)
                exps(0)
                exps(1)
                for b in range(1, B):
                    round_p(b)
                transposed(0)
                exps(2)
                exps(3)
                transposed(1)
            act.preload_act_table_set(SILU_TANH)
            for step, h in ORDER2:
                if step == "ft":
                    step_ft(1, h, bank_pair2("ft", h))
                elif step.startswith("gu"):
                    step_gu(1, h, int(step[2:]), bank_pair2(step, h))

        @block.tensor
        def _(pe):
            def claim(name, h):
                if before[name, h] is not None:
                    for last_read in freed[before[name, h]]:
                        pe.wait_ge(*last_read)
                return bank_pair(name, h)

            def claim2(name, h):
                if before2[name, h] is None:
                    pe.wait_ge(s["a_added"], loop_value(STEPS - 1, 4, 2))
                    if pair2[name, h] == A_PAIR[1]:
                        pe.wait_ge(s["a_added"], loop_value(STEPS - 1, 4, 4))
                else:
                    for last_read in freed2[before2[name, h]]:
                        pe.wait_ge(*last_read)
                return bank_pair2(name, h)

            def split_product(outs, left, right, ready=None):
                for k, ((lh, ll), (rh, rl)) in enumerate(zip(left, right)):
                    if ready:
                        ready(k, 0)
                    pe.matmul(outs, lh, rh, start=(k == 0), stop=False)
                    pe.matmul(outs, ll, rh, start=False, stop=False)
                    if ready:
                        ready(k, 1)
                    mm = pe.matmul(outs, lh, rl, start=False, stop=(k == len(left) - 1))
                return mm

            def transposes(dst, kind, h, done):
                for j, b in enumerate(half_batches(h)):
                    pe.wait_ge(s["ln_done"], B * kind + b + 1)
                    for m in range(KC):
                        for t in range(R * j, R * (j + 1)):
                            tr = pe.transpose(dst[:, m, t * P:(t + 1) * P], XN[:, h * HT + t, m * P:(m + 1) * P], ident[:])
                        if j == HB - 1:
                            tr.then_inc(done, 1)

            def projection(name, block_, h, xh, xl, hi, lo):
                dst = claim(name, h)
                pe.wait_ge(s["rec_split"], block_ + 1)

                def ready(k, part):
                    pe.wait_ge((hi, lo)[part], upto(h, k))

                for m in range(KC):
                    mm = split_product(dst[:, m],
                                       [(w_hi[:, k, block_, m * P:(m + 1) * P], w_lo[:, k, block_, m * P:(m + 1) * P]) for k in range(KC)],
                                       [(xh[:, k], xl[:, k]) for k in range(KC)], ready if m == 0 else None)
                    mm.then_inc(s[name + "_ps"], 1)

            def of_x(name, block_, h):
                projection(name, block_, h, XTh, XTl, s["xt_hi"], s["xt_lo"])

            def of_conv(name, block_, h):
                projection(name, block_, h, XCh, XCl, s["xc_hi"], s["xc_lo"])

            def by_head(name, h, matrix, src, ready, each=1):
                dst = claim(name, h)
                for m in range(KC):
                    pe.wait_ge(ready, each * upto(h, m))
                    pe.matmul(dst[:, m], matrix[:], src[:, h, m], start=True, stop=True).then_inc(s[name + "_ps"], 1)

            def step_wo(h):
                dst = claim("wo", h).rearrange("p a (t c) -> p (a t) c", c=C)
                pe.wait_ge(s["w_out_in"], 16)
                pe.wait_ge(s["z_done"], upto(h, 1))
                for t in range(HT):
                    for k in range(KC):
                        mm = pe.matmul(dst[:, t], k_t[:, h, k, token_cols(t)], w_out[:, k], start=(k == 0), stop=(k == KC - 1))
                    if t % R == R - 1:
                        mm.then_inc(s["wo_ps"], 1)

            def step_gu(f, h, c, dst):
                w, n = ffn[f], 2 * f + h
                pe.wait_ge(s["gu_split"], 2)

                def ready(k, part):
                    pe.wait_ge((s["ft_hi"], s["ft_lo"])[part], upto(n, k))

                right = [(w.XTh[h][:, k], w.XTl[h][:, k]) for k in range(KC)]
                for j in range(2 if c < FULL else 1):
                    cols = slice((2 * c + j) * P, (2 * c + j + 1) * P)
                    mm = split_product(dst[:, j], [(gu_hi[:, k, cols], gu_lo[:, k, cols]) for k in range(KC)], right,
                                       ready if c == 0 and j == 0 else None)
                mm.then_inc(s["gu_ps"], 1)

            def step_dn(f, h, j, pair_):
                dst = pair_.rearrange("p a (t c) -> p (a t) c", c=C)
                pe.wait_ge(s["dn_scaled"], 2)
                pe.wait_ge(s["hd_done"], gu_before(f, h) + FULL)
                for t in range(R * j, R * (j + 1)):
                    for c in range(FCH):
                        rows = P if c < FULL else REST
                        if c == FULL:
                            pe.wait_ge(s["hd_done"], gu_before(f, h) + FCH)
                        mm = pe.matmul(dst[:, t], ffn[f].HD[h][0:rows, c, token_cols(t)], w_down[0:rows, c],
                                       start=(c == 0), stop=(c == FCH - 1))
                mm.then_inc(s["dn_ps"], 1)

            def step_gm(b):
                dst = claim("gm", b)
                pe.wait_ge(s["ln_done"], B * LN_CHAN + b + 1)
                for m in range(KC):
                    for k in range(R):
                        mm = pe.matmul(dst[:, m, 0:C + 1], XN[:, b * R + k, m * P:(m + 1) * P],
                                       XN[:, b * R + k, 0:C + 1], start=(k == 0), stop=(k == R - 1))
                mm.then_inc(s["g_ps"], 1)

            pe.wait_ge(s["consts_pool"], 7)
            for step, h in ORDER:
                if step == "xt":
                    transposes(claim("xt", h), LN_X, h, s["xt_ps"])
                elif step in ("q", "k", "v"):
                    of_x(step, {"q": W_Q, "k": W_K, "v": W_V}[step], h)
                elif step in ("ig", "og", "gamma"):
                    of_conv(step, {"ig": W_IG, "og": W_OG, "gamma": W_GAMMA}[step], h)
                elif step in ("nq", "nk", "nv"):
                    by_head(step, h, heads_ones, {"nq": sq_q, "nk": sq_k, "nv": sq_v}[step], s[step[1] + "_sq"])
                elif step == "mc":
                    pe.wait_ge(s["consts_dve"], 2)
                    by_head("mc", h, centre, mem, s["mem_done"], HB)
                elif step == "mv":
                    by_head("mv", h, heads_ones, sq_v, s["mc_sq"])
                elif step == "oc":
                    by_head("oc", h, centre, v_t, s["o_done"])
                elif step == "ov":
                    by_head("ov", h, heads_ones, sq_q, s["oc_sq"])
                elif step == "wo":
                    step_wo(h)
                elif step == "ft":
                    transposes(claim("ft", h), LN_FFN, h, s["ft_ps"])
                elif step.startswith("gu"):
                    step_gu(0, h, int(step[2:]), claim(step, h))
                elif step == "dna":
                    step_dn(0, h, 0, claim("dna", h))
                elif step == "dnb":
                    step_dn(0, h, 1, bank_pair("dna", h))
                elif step == "gm":
                    step_gm(h)

            pe.wait_ge(s["ffn_added"], B)
            for sm, per in ((s["r_ps"], 1), (s["z_ps"], B), (s["w_ps"], 1), (s["s_ps"], NG), (s["p_ps"], B), (s["t_ps"], 2),
                            (s["u_ps"], 2 * NG), (s["a_ps"], 4)):
                pe.sem_inc(sm, per)
            with pe.Fori(0, STEPS) as i:
                def scores(g):
                    dst = ps[:, S_PAIR[g // 2], g % 2]
                    cols = slice(g * NQ, (g + 1) * NQ)
                    if g == 0:
                        pe.wait_ge(s["wq_in"], 16 * (i + 1))
                        pe.wait_ge(s["z_added"], loop_value(i, 2 * B, 2 * B))
                    for k in range(KC):
                        pe.matmul(dst, raw_q[:, k, cols], Z[:, k, :, cols], start=(k == 0), stop=False)
                    if g == 0:
                        pe.wait_ge(s["bq_split"], loop_value(i, 2, 2))
                        pe.wait_ge(s["r_lo"], loop_value(i, 1, 1))
                    pe.matmul(dst, bq_s[:, cols], r_s[:, g].rearrange("p b n -> p (b n)"), start=False,
                              stop=True).then_inc(s["s_ps"], 1)

                def transpose_pair(j):
                    pe.wait_ge(s["e_norm"], loop_value(i, NG, 2 * j + 2))
                    for g in range(2):
                        for b in range(B):
                            tr = pe.transpose(ps[:, T_PAIR[j], g, b * NQ:(b + 1) * NQ], E[:, g, b], ident[:])
                    tr.then_inc(s["t_ps"], 1)

                def project_wo(b):
                    for m in range(KC):
                        mm = split_product(ps[:, P_PAIR[b], m],
                                           [(XH[:, b * R + k, m * P:(m + 1) * P], XL[:, b * R + k, m * P:(m + 1) * P]) for k in range(R)],
                                           [(wo_hi[:, k], wo_lo[:, k]) for k in range(R)])
                    mm.then_inc(s["p_ps"], 1)

                def values(g):
                    cols = slice(g * NQ, (g + 1) * NQ)
                    for j in range(2):
                        right = [(P_hi[:, k, 2 * j:2 * j + 2, g % HL], P_lo[:, k, 2 * j:2 * j + 2, g % HL]) for k in range(KC)]
                        mm = split_product(ps[:, U_PAIR[g], j], [(wv_hi[:, k, cols], wv_lo[:, k, cols]) for k in range(KC)], right)
                        mm.then_inc(s["u_ps"], 1)

                def attend(j):
                    dst = ps[:, A_PAIR[j]].rearrange("p a (b c) -> p (a b) c", c=C)
                    for b in range(B):
                        if b == HB:
                            pe.wait_ge(s["u_added"], loop_value(i, 2 * NG, 2 * HL * (j + 1)))
                        for l in range(HL):
                            mm = pe.matmul(dst[:, b], ET[:, 2 * j + l, b], U[:, l, b], start=(l == 0), stop=(l == HL - 1))
                        if b % HB == HB - 1:
                            mm.then_inc(s["a_ps"], 1)

                pe.wait_ge(s["wk_split"], loop_value(i, 2, 2))
                for b in range(B):
                    pe.wait_ge(s["g_lo"], max(b, GM_IN_PAIR[Z_PAIR[b]]) + 1)
                    if b == 2:
                        pe.wait_ge(s["a_added"], loop_value(i - 1, 4, 4))
                    if b == 3:
                        pe.wait_ge(s["r_sum"], loop_value(i, 1, 1))
                    for m in range(KC):
                        mm = split_product(ps[:, Z_PAIR[b], m],
                                           [(G_hi[:, b, k, m * P:(m + 1) * P], G_lo[:, b, k, m * P:(m + 1) * P]) for k in range(KC)],
                                           [(wk_hi[:, k], wk_lo[:, k]) for k in range(KC)])
                    mm.then_inc(s["z_ps"], 1)
                    if b == 0:
                        pe.wait_ge(s["s_hi"], 3)
                        pe.wait_ge(s["s_lo"], 3)
                        pe.wait_ge(s["g_lo"], GM_IN_PAIR[0] + 1)
                        split_product(ps[:, 0, 0], [(S_hi[:, k], S_lo[:, k]) for k in range(KC)],
                                      [(wk_hi[:, k], wk_lo[:, k]) for k in range(KC)]).then_inc(s["r_ps"], 1)
                pe.wait_ge(s["ones_r_done"], 1)
                pe.wait_ge(s["wo_split"], loop_value(i, 2, 2))
                pe.wait_ge(s["z_added"], loop_value(i, 2 * B, 2))
                for k in range(R):
                    for part, w in enumerate((wo_hi, wo_lo)):
                        mm = pe.matmul(ps[:, 1, 0], ones_r[:], w[:, k], start=(k == 0 and part == 0),
                                       stop=(k == R - 1 and part == 1))
                mm.then_inc(s["w_ps"], 1)
                pe.wait_ge(s["z_added"], loop_value(i, 2 * B, 4))
                pe.wait_ge(s["x_lo"], 2)
                project_wo(0)
                scores(0)
                scores(1)
                project_wo(1)
                pe.wait_ge(s["w_cp"], loop_value(i, 1, 1))
                project_wo(2)
                pe.wait_ge(s["p_lo"], loop_value(i, B, 1))
                project_wo(3)
                transpose_pair(0)
                pe.wait_ge(s["p_lo"], loop_value(i, B, 2))
                scores(2)
                pe.wait_ge(s["wv_split"], loop_value(i, 2, 2))
                pe.wait_ge(s["p_lo"], loop_value(i, B, B))
                values(0)
                values(1)
                scores(3)
                pe.wait_ge(s["t_cp"], loop_value(i, 2, 1))
                pe.wait_ge(s["u_added"], loop_value(i, 2 * NG, 3))
                attend(0)
                values(2)
                transpose_pair(1)
                values(3)
                pe.wait_ge(s["t_cp"], loop_value(i, 2, 2))
                pe.wait_ge(s["u_added"], loop_value(i, 2 * NG, 7))
                pe.wait_ge(s["a_added"], loop_value(i, 4, 2))
                attend(1)

            for step, h in ORDER2:
                if step == "ft":
                    transposes(claim2("ft", h), LN_FFN2, h, s["ft_ps"])
                elif step.startswith("gu"):
                    step_gu(1, h, int(step[2:]), claim2(step, h))
                elif step == "dna":
                    step_dn(1, h, 0, claim2("dna", h))
                elif step == "dnb":
                    step_dn(1, h, 1, bank_pair2("dna", h))

        @block.vector
        def _(dve):
            def layer_norm(kind, batches, arrive):
                for b in batches:
                    arrive(b)
                    tiles = slice(R * b, R * (b + 1))
                    for t in range(R):
                        dve.bn_stats(stats[:, R * b + t], X[:, R * b + t]).then_inc(s["ln_stat"], 1)
                    for t in range(R):
                        dve.wait_ge(s["ln_stat"], NT * kind + R * b + t + 1)
                        dve.bn_aggr(agg[:, R * b + t], stats[:, R * b + t]).then_inc(s["ln_agg"], 1)
                    dve.wait_ge(s["ln_agg"], NT * kind + R * (b + 1))
                    dve.tensor_scalar(var_eps[:, tiles], agg[:, tiles, 1], EPS, None, ALU.add).then_inc(s["ln_eps"], 1)
                for b in batches:
                    dve.wait_ge(s["ln_rstd"], B * kind + b + 1)
                    for t in range(R * b, R * (b + 1)):
                        op = dve.tensor_scalar(XN[:, t, 0:C], X[:, t], agg[:, t, 0:1], rstd[:, t:t + 1], ALU.subtract, ALU.mult)
                    op.then_inc(s["ln_done"], 1)

            def loaded(b):
                dve.wait_ge(s[("x0_in", "x1_in", "x23_in", "x23_in")[b]], 16)

            def add_recurrence(b):
                dve.wait_ge(s["wo_ps"], b + 1)
                x_b = X[:, R * b:R * (b + 1)]
                dve.tensor_tensor(x_b, x_b, bank_pair("wo", b // HB)[:, b % HB].rearrange("p (t c) -> p t c", c=C),
                                  ALU.add).then_inc(s["rec_added"], 1)
                dve.wait_ge(s["rec_added"], b + 1)

            def step_xt(h):
                for m in range(KC):
                    dve.wait_ge(s["xt_hi"], upto(h, m))
                    if h:
                        dve.wait_ge(s["q_ps"], upto(0, 1))
                    dve.tensor_tensor(in_time(XTl[:, m]), by_tile(bank_pair("xt", h)[:, m]), in_time(XTh[:, m]).bitcast(F32),
                                      ALU.subtract).then_inc(s["xt_lo"], 1)

            def step_conv(h):
                if h:
                    dve.wait_ge(s["xc_hi"], upto(0, 1))
                    dve.wait_ge(s["xc_lo"], upto(0, 1))
                conv = (s["conv_m0"], s["conv_m1"])
                for shift in range(TAPS):
                    for m in range(KC):
                        if shift == 0:
                            dve.wait_ge(s["xt_f"], upto(h, m))
                        tap = vecs[:, m, V_TAP + TAPS - 1 - shift:V_TAP + TAPS - shift]
                        src = XTf[:, m].rearrange("p (b t) -> p b t", b=HB)[:, :, 0:T - shift]
                        dst = XCf[:, m].rearrange("p (b t) -> p b t", b=HB)[:, :, shift:T]
                        if shift == 0:
                            dve.tensor_scalar(XCf[:, m], XTf[:, m], tap, None, ALU.mult).then_inc(conv[m], 1)
                        else:
                            dve.wait_ge(conv[m], TAPS * h + shift)
                            dve.scalar_tensor_tensor(out=dst, in0=src, scalar=tap, in1=dst, op0=ALU.mult,
                                                     op1=ALU.add).then_inc(conv[m], 1)

            def step_silu(h):
                if h:
                    dve.wait_ge(s["og_ps"], upto(0, 1))
                for m in range(KC):
                    dve.wait_ge(s["silu_done"], upto(h, m))
                    dve.wait_ge(s["xc_hi"], upto(h, m))
                    dve.tensor_tensor(XCl[:, m], XCf[:, m], XCh[:, m].bitcast(F32), ALU.subtract).then_inc(s["xc_lo"], 1)

            def norm_guard(name, h, sq, done):
                for m in range(KC):
                    dve.wait_ge(s[name + "_ps"], upto(h, m))
                    dve.tensor_scalar(sq[:, h, m], bank_pair(name, h)[:, m], 1e-24, None, ALU.max).then_inc(done, 1)

            def times(out, a, b, h, done, *ready):
                for m in range(KC):
                    for r in ready:
                        dve.wait_ge(r, upto(h, m))
                    dve.tensor_tensor(out[:, m], a[:, m], b[:, m], ALU.mult).then_inc(done, 1)

            def affine(t, h, gain, bias, done, ready):
                for m in range(KC):
                    dve.wait_ge(ready, upto(h, m))
                    dve.tensor_scalar(t[:, h, m], t[:, h, m], vecs[:, m, gain:gain + 1], vecs[:, m, bias:bias + 1],
                                      ALU.mult, ALU.add).then_inc(done, 1)

            def one_plus_times(t, g, h, done, *ready):
                for m in range(KC):
                    for r in ready:
                        dve.wait_ge(r, upto(h, m))
                    dve.scalar_tensor_tensor(out=t[:, h, m], in0=g[:, h, m], scalar=1.0, in1=t[:, h, m], op0=ALU.add,
                                             op1=ALU.mult).then_inc(done, 1)

            def step_rk(h):
                times(k_t[:, h], k_t[:, h], sq_k[:, h], h, s["k_n"], s["k_cp"], s["rk_done"])
                times(v_t[:, h], v_t[:, h], sq_v[:, h], h, s["v_n"], s["v_cp"], s["rv_done"])
                dve.wait_ge(s["vec_half"], 1)
                affine(v_t, h, V_VN_G, V_VN_B, s["v_a"], s["v_n"])

            def step_scan(h):
                one_plus_times(k_t, t_ig, h, s["k_g"], s["ti_done"], s["k_n"])
                times(k_t[:, h], k_t[:, h], v_t[:, h], h, s["b_done"], s["k_g"], s["v_a"])
                for m in range(KC):
                    dve.wait_ge(s["tg_done"], upto(h, m))
                    dve.tensor_scalar(t_ga[:, h, m], t_ga[:, h, m], 0.5, 0.5, ALU.mult, ALU.add).then_inc(s["gamma_done"], 1)
                for m in range(KC):
                    dve.wait_ge(s["b_done"], upto(h, m))
                    dve.wait_ge(s["gamma_done"], upto(h, m))
                    for b in range(HB):
                        span = slice(b * T, (b + 1) * T)
                        dve.tensor_tensor_scan(mem[:, h, m, span], t_ga[:, h, m, span], k_t[:, h, m, span], 0.0,
                                               ALU.mult, ALU.add).then_inc(s["mem_done"], 1)

            def step_mv(h):
                times(v_t[:, h], bank_pair("mc", h), sq_v[:, h], h, s["y_n"], s["r1_done"])
                affine(v_t, h, V_MN_G, V_MN_B, s["y_a"], s["y_n"])
                times(v_t[:, h], v_t[:, h], q_t[:, h], h, s["o_done"], s["y_a"], s["qn_done"])

            def step_ov(h):
                times(k_t[:, h], bank_pair("oc", h), sq_q[:, h], h, s["z_n"], s["r2_done"])
                affine(k_t, h, V_GN_G, V_GN_B, s["z_a"], s["z_n"])
                one_plus_times(k_t, t_og, h, s["z_done"], s["z_a"], s["to_done"])

            def step_ft(f, h, psum):
                w, n = ffn[f], 2 * f + h
                for m in range(KC):
                    dve.wait_ge(s["ft_hi"], upto(n, m))
                    dve.tensor_tensor(in_time(w.XTl[h][:, m]), by_tile(psum[:, m]), in_time(w.XTh[h][:, m]).bitcast(F32),
                                      ALU.subtract).then_inc(s["ft_lo"], 1)

            def step_gu(f, h, c, psum):
                w, at = ffn[f], gu_before(f, h) + c
                rows = P if c < FULL else REST
                up = psum[0:P, 1] if c < FULL else psum[REST:P, 0]
                dve.wait_ge(s["silu_g"], at + 1)
                dve.tensor_tensor(w.HD[h][0:rows, c], up, w.SG[0:rows, at % 2], ALU.mult).then_inc(s["hd_done"], 1)

            def step_dn(f, h, j, pair_):
                b = HB * h + j
                dve.wait_ge(s["dn_ps"], B * f + b + 1)
                dve.tensor_tensor(X[:, R * b:R * (b + 1)], X[:, R * b:R * (b + 1)],
                                  pair_[:, j].rearrange("p (t c) -> p t c", c=C), ALU.add).then_inc(s["ffn_added"], 1)

            def ffn_added(b):
                dve.wait_ge(s["ffn_added"], b + 1)

            def step_lc(n):
                layer_norm(LN_CHAN, batches_of_lc(n), ffn_added)
                dve.wait_ge(s["bo_in"], 16)
                for b in batches_of_lc(n):
                    dve.wait_ge(s["ln_done"], B * LN_CHAN + b + 1)
                    x_b = X[:, R * b:R * (b + 1)]
                    dve.tensor_tensor(x_b, x_b, bo_b[:].unsqueeze(1).to_broadcast([P, R, C]), ALU.add).then_inc(s["bo_added"], 1)

            def split_xn(h):
                tiles = slice(HT * h, HT * (h + 1))
                dve.tensor_copy(XH[:, tiles], XN[:, tiles, 0:C]).then_inc(s["x_hi"], 1)
                dve.wait_ge(s["x_hi"], h + 1)
                dve.tensor_tensor(XL[:, tiles], XN[:, tiles, 0:C], XH[:, tiles].bitcast(F32), ALU.subtract).then_inc(s["x_lo"], 1)

            def step_gm(b):
                dve.wait_ge(s["g_hi"], b + 1)
                dve.tensor_copy(S_col[:, :, b:b + 1], bank_pair("gm", b)[:, :, C:C + 1]).then_inc(s["s_cp"], 1)
                if b == B - 1:
                    split_sums()
                dve.tensor_tensor(G_lo[:, b], bank_pair("gm", b)[:, :, 0:C], G_hi[:, b].bitcast(F32), ALU.subtract).then_inc(s["g_lo"], 1)

            def constants():
                for part in (S_hi, S_lo):
                    for k in range(KC):
                        dve.tensor_scalar(part[:, k], ident[:], 0.0, 0.0, ALU.mult, ALU.add).then_inc(s["s_zero"], 1)
                for q in range(3):
                    dve.tensor_copy(mask[32 * q:32 * q + 32], ident[32 * q:32 * q + 32, 32 * q:32 * q + B]).then_inc(s["mask_done"], 1)
                dve.tensor_scalar(ones_r[:], ident[:], 0.0, 1.0, ALU.mult, ALU.add).then_inc(s["ones_r_done"], 1)

            def split_sums():
                dve.wait_ge(s["s_cp"], B)
                dve.wait_ge(s["s_zero"], 2 * KC)
                for q in range(3):
                    dve.tensor_copy(S_hi[:, :, 32 * q:32 * q + B], S_col[:]).then_inc(s["s_hi"], 1)
                for q in range(3):
                    cols = slice(32 * q, 32 * q + B)
                    dve.wait_ge(s["s_hi"], q + 1)
                    dve.tensor_tensor(S_lo[:, :, cols], S_col[:], S_hi[:, :, cols].bitcast(F32), ALU.subtract).then_inc(s["s_lo"], 1)

            def split(raw, hi, lo, got, done, free, step):
                dve.wait_ge(got, 16 * (step + 1))
                dve.tensor_copy(hi[:], raw[:]).then_inc(done, 1)
                dve.wait_ge(done, loop_value(step, 2, 1))
                dve.tensor_tensor(lo[:], raw[:], hi[:].bitcast(F32), ALU.subtract).then_inc(done, 1)
                dve.wait_ge(done, loop_value(step, 2, 2))
                dve.sem_inc(free, 1)

            def split_wk(step):
                split(raw_k, wk_hi, wk_lo, s["wk_in"], s["wk_split"], s["raw_k_free"], step)

            def split_wo(step):
                split(raw_o, wo_hi, wo_lo, s["wo_in"], s["wo_split"], s["raw_o_free"], step)

            def split_wv(step):
                split(raw_v, wv_hi, wv_lo, s["wv_in"], s["wv_split"], s["raw_v_free"], step)

            for sm, per in ((s["raw_k_free"], 1), (s["raw_o_free"], 1), (s["raw_v_free"], 1), (s["bq_raw_free"], 1),
                            (s["wk_split"], 2), (s["wo_split"], 2), (s["wv_split"], 2), (s["bq_split"], 2), (s["r_sum"], 1),
                            (s["z_added"], 2 * B), (s["negmax"], NG), (s["bias_done"], NG), (s["rsum"], NG), (s["e_norm"], NG),
                            (s["p_lo"], B), (s["u_added"], 2 * NG), (s["a_added"], 4)):
                dve.sem_inc(sm, per)
            def split_weights(block_, nth):
                dve.wait_ge(s["rec_hi"], nth + 1)
                dve.tensor_tensor(w_lo[:, :, block_], w_raw[:, :, block_], w_hi[:, :, block_].bitcast(F32),
                                  ALU.subtract).then_inc(s["rec_split"], 1)

            def scale_down_weights():
                dve.wait_ge(s["w_dn_in"], 32)
                dve.wait_ge(s["scale_in"], 16)
                dve.wait_ge(s["down_s_in"], 16)
                for c in range(FCH):
                    rows = P if c < FULL else REST
                    op = dve.scalar_tensor_tensor(
                        out=w_down[0:rows, c], in0=w_down[0:rows, c], scalar=f_scale[0:rows, FCH + c:FCH + c + 1],
                        in1=down_b[0:rows], op0=ALU.mult, op1=ALU.mult)
                    if c >= FULL - 1:
                        op.then_inc(s["dn_scaled"], 1)

            dve.memset(XN[:, :, C:C + 2], 1.0).then_inc(s["consts_dve"], 1)
            layer_norm(LN_X, half_batches(0), loaded)
            dve.wait_ge(s["w_kv_in"], 16)
            for k in range(KC):
                dve.tensor_reduce(msum[:, k], w_raw[:, k, W_V].rearrange("p (h d) -> p h d", d=D), AX.X,
                                  ALU.add).then_inc(s["centred"], 1)
            dve.wait_ge(s["w_gamma_in"], 16)
            for k in range(KC):
                dve.tensor_copy(w_raw[:, k, W_GAMMA].rearrange("p (h d) -> p h d", d=D),
                                gam[:, k].unsqueeze(2).to_broadcast([P, H, D])).then_inc(s["gamma_rep"], 1)
            dve.wait_ge(s["centred"], 2)
            for k in range(KC):
                v3 = w_raw[:, k, W_V].rearrange("p (h d) -> p h d", d=D)
                dve.scalar_tensor_tensor(out=v3, in0=msum[:, k].unsqueeze(2).to_broadcast([P, H, D]), scalar=-1.0 / D,
                                         in1=v3, op0=ALU.mult, op1=ALU.add).then_inc(s["centred"], 1)
            split_weights(W_K, 0)
            for step, h in ORDER:
                if step == "xt":
                    step_xt(h)
                    if h == 0:
                        dve.wait_ge(s["vec_in"], 16)
                        dve.tensor_scalar(vecs[:, :, V_IG_B:V_VN_B + 1], vecs[:, :, V_IG_B:V_VN_B + 1], 0.5, None, ALU.mult)
                        dve.tensor_scalar(vecs[:, :, V_GN_G:V_GN_B + 1], vecs[:, :, V_GN_G:V_GN_B + 1], 0.5, None,
                                          ALU.mult).then_inc(s["vec_half"], 1)
                elif step == "conv":
                    if h == 0:
                        split_weights(W_V, 1)
                        split_weights(W_Q, 2)
                    step_conv(h)
                    if h == 0:
                        for nth, block_ in ((3, W_IG), (4, W_OG), (5, W_GAMMA)):
                            split_weights(block_, nth)
                        dve.wait_ge(s["consts_pool"], 7)
                        dve.scalar_tensor_tensor(out=centre[:], in0=heads_ones[:], scalar=-1.0 / D, in1=ident[:],
                                                 op0=ALU.mult, op1=ALU.add).then_inc(s["consts_dve"], 1)
                elif step == "lx":
                    layer_norm(LN_X, half_batches(h), loaded)
                elif step == "silu":
                    step_silu(h)
                elif step == "nk":
                    norm_guard("nk", h, sq_k, s["nk_max"])
                elif step == "nq":
                    norm_guard("nq", h, sq_q, s["nq_max"])
                elif step == "rk":
                    step_rk(h)
                elif step == "scan":
                    step_scan(h)
                elif step == "mv":
                    step_mv(h)
                elif step == "ov":
                    step_ov(h)
                elif step == "ln":
                    layer_norm(LN_FFN, half_batches(h), add_recurrence)
                elif step == "ft":
                    step_ft(0, h, bank_pair("ft", h))
                elif step.startswith("gu"):
                    step_gu(0, h, int(step[2:]), bank_pair(step, h))
                    if (step, h) == ("gu1", 0):
                        scale_down_weights()
                    elif (step, h) == ("gu0", 1):
                        split_wk(0)
                    elif (step, h) == ("gu1", 1):
                        constants()
                    elif (step, h) == ("gu2", 1):
                        split_wo(0)
                elif step in ("dna", "dnb"):
                    step_dn(0, h, int(step == "dnb"), bank_pair("dna", h))
                elif step == "lc":
                    step_lc(h)
                    if h == 0:
                        split_xn(0)
                elif step == "gm":
                    step_gm(h)

            split_xn(1)
            dve.wait_ge(s["bv_in"], 16)

            def add_out(i, j, half):
                dve.wait_ge(s["a_ps"], loop_value(i, 4, 2 * j + half + 1))
                dst = X[:].rearrange("p (b r) c -> p b r c", r=R)[:, HB * half:HB * (half + 1), j]
                dve.tensor_tensor(dst, dst, ps[:, A_PAIR[j], half].rearrange("p (b c) -> p b c", c=C),
                                  ALU.add).then_inc(s["a_added"], 1)

            def attention_step(i, last):
                def softmax_bias(g):
                    dve.wait_ge(s["s_ps"], loop_value(i, NG, g + 1))
                    dve.wait_ge(s["exp_done"], loop_value(i, NG * B, (g - 1) * B))
                    dve.tensor_reduce(neg[:, g % 2], ps[:, S_PAIR[g // 2], g % 2].rearrange("p (b n) -> p b n", b=B),
                                      AX.X, ALU.max, negate=True).then_inc(s["negmax"], 1)
                    dve.wait_ge(s["negmax"], loop_value(i, NG, g + 1))
                    dve.tensor_scalar(e_bias[:, g % 2], neg[:, g % 2], SCALE, None, ALU.mult).then_inc(s["bias_done"], 1)

                def softmax_norm(g):
                    j = g % 2
                    dve.wait_ge(s["exp_done"], loop_value(i, NG * B, (g + 1) * B))
                    dve.reciprocal(e_inv[:, j], e_sum[:, j]).then_inc(s["rsum"], 1)
                    dve.wait_ge(s["rsum"], loop_value(i, NG, g + 1))
                    dve.tensor_tensor(E[:, j], E[:, j], e_inv[:, j].unsqueeze(2).to_broadcast([P, B, NQ]),
                                      ALU.mult).then_inc(s["e_norm"], 1)

                def add_values_bias(g):
                    if g < HL:
                        dve.wait_ge(s["a_ps"], loop_value(i - 1, 4, 4))
                    else:
                        dve.wait_ge(s["a_ps"], loop_value(i, 4, 2))
                    if g == 0:
                        dve.wait_ge(s["w_cp"], loop_value(i, 1, 1))
                    for j in range(2):
                        dve.wait_ge(s["u_ps"], loop_value(i, 2 * NG, 2 * g + j + 1))
                        dve.scalar_tensor_tensor(
                            out=U[:, g % HL, 2 * j:2 * j + 2], in0=w_sum[:, g % HL].unsqueeze(1).to_broadcast([P, 2, C]),
                            scalar=bv_c[:, bass.ds(i * NG + g, 1)],
                            in1=ps[:, U_PAIR[g], j].rearrange("p (b c) -> p b c", b=2), op0=ALU.mult,
                            op1=ALU.add).then_inc(s["u_added"], 1)

                dve.wait_ge(s["bk_in"], 16 * (i + 1))
                dve.wait_ge(s["r_ps"], loop_value(i, 1, 1))
                dve.wait_ge(s["r_mask"], loop_value(i - 1, 1, 1))
                dve.scalar_tensor_tensor(out=r_row[:], in0=bk_b[:], scalar=float(T), in1=ps[:, 0, 0], op0=ALU.mult,
                                         op1=ALU.add).then_inc(s["r_sum"], 1)
                dve.wait_ge(s["bq_in"], 16 * (i + 1))
                dve.tensor_copy(bq_s[:], bq_b[:]).then_inc(s["bq_split"], 1)
                dve.wait_ge(s["bq_split"], loop_value(i, 2, 1))
                dve.tensor_tensor(bq_s[64:96], bq_b[64:96], bq_s[64:96].bitcast(F32), ALU.subtract).then_inc(s["bq_split"], 1)
                dve.wait_ge(s["bq_split"], loop_value(i, 2, 2))
                dve.sem_inc(s["bq_raw_free"], 1)
                for b in range(B):
                    dve.wait_ge(s["z_ps"], loop_value(i, B, b + 1))
                    for m in range(KC):
                        dve.scalar_tensor_tensor(out=Z[:, m, b], in0=bk_b[:], scalar=S_col[:, m, b:b + 1],
                                                 in1=ps[:, Z_PAIR[b], m], op0=ALU.mult, op1=ALU.add).then_inc(s["z_added"], 1)
                def split_p(b):
                    dve.wait_ge(s["p_hi"], loop_value(i, B, b + 1))
                    dve.tensor_tensor(P_lo[:, :, b].rearrange("p m l c -> p m (l c)"), ps[:, P_PAIR[b]],
                                      P_hi[:, :, b].rearrange("p m l c -> p m (l c)").bitcast(F32),
                                      ALU.subtract).then_inc(s["p_lo"], 1)

                split_wv(i)
                split_p(0)
                softmax_bias(0)
                softmax_bias(1)
                softmax_norm(0)
                softmax_norm(1)
                for b in range(1, B):
                    split_p(b)
                softmax_bias(2)
                if not last:
                    split_wk(i + 1)
                add_values_bias(0)
                softmax_norm(2)
                add_values_bias(1)
                softmax_bias(3)
                if not last:
                    split_wo(i + 1)
                softmax_norm(3)
                add_out(i, 0, 0)
                add_out(i, 0, 1)
                add_values_bias(2)
                add_values_bias(3)
                if not last:
                    add_out(i, 1, 0)
                    add_out(i, 1, 1)

            with dve.Fori(0, STEPS - 1) as i:
                attention_step(i, False)
            attention_step(STEPS - 1, True)

            def add_last_out(b):
                half = b // HB
                if b % HB == 0:
                    add_out(STEPS - 1, 1, half)
                    dve.wait_ge(s["a_added"], loop_value(STEPS - 1, 4, 2 + half + 1))

            for step, h in ORDER2:
                if step == "ln":
                    layer_norm(LN_FFN2, half_batches(h), add_last_out)
                elif step == "ft":
                    step_ft(1, h, bank_pair2("ft", h))
                elif step.startswith("gu"):
                    step_gu(1, h, int(step[2:]), bank_pair2(step, h))
                elif step in ("dna", "dnb"):
                    step_dn(1, h, int(step == "dnb"), bank_pair2("dna", h))


Z_PAIR = [1, 2, 3, 0]
P_PAIR = [2, 0, 1, 2]
S_PAIR = [3, 0]
T_PAIR = [3, 0]
U_PAIR = [1, 2, 1, 2]
A_PAIR = [3, 3]
GM_IN_PAIR = {pair_plan(ORDER)[0]["gm", b]: b for b in range(B)}


def kernel(**inputs):
    import numpy as np
    import concourse.bacc as bacc
    from concourse.bass_utils import run_bass_kernel_spmd as run

    a = {n: np.asarray(v) for n, v in inputs.items()}
    rec = {n[len("L0_attn_a_"):]: v for n, v in a.items() if n.startswith("L0_attn_a_")}
    att = {n[len("L0_attn_b_"):]: v for n, v in a.items() if n.startswith("L0_attn_b_")}
    ff = {n[len("L0_ffn_"):]: v for n, v in a.items() if n.startswith("L0_ffn_")}

    def col(v):
        return v.reshape(-1, 1)

    vec = np.concatenate(
        [rec["conv_w"].reshape(C, TAPS), col(rec["conv_b"]), col(rec["ig_b"]), col(np.repeat(rec["gamma_b"], D)),
         col(rec["og_b"]), col(np.tile(rec["vn_g"], H)), col(np.tile(rec["vn_b"], H)), col(np.tile(rec["mn_g"], H)),
         col(np.tile(rec["mn_b"], H)), col(rec["gn_g"]), col(rec["gn_b"])], axis=1)
    w_rec = np.stack([rec[n].T for n in ("Wk", "Wv", "Wq", "ig_w", "og_w")], axis=1)

    gate_up = [ff[n].T for n in ("gate_w", "up_w")]
    w_gu = np.concatenate([w[:, c * P:(c + 1) * P] for c in range(FCH) for w in gate_up], axis=1)

    def chunk_cols(v):
        return np.concatenate([v, np.zeros(FCH * P - INTER, v.dtype)]).reshape(FCH, P).T

    ffn_scale = np.concatenate([chunk_cols(ff["gate_s"]), chunk_cols(ff["up_s"])], axis=1)

    heads = np.array([[r * Y_BLOCKS + i * HL + l for r in range(2) for l in range(HL)] for i in range(STEPS)])

    def by_step(w):
        w = w.reshape(-1, NQ, NH)[:, :, heads]
        return w.transpose(2, 0, 3, 1).reshape(STEPS, -1, NG * NQ)

    wo = att["Wo"].reshape(STEPS, HL, T, C).transpose(0, 2, 1, 3).reshape(STEPS, T, HL * C)
    arrays = {
        "x": a["L0_attn_a_x"], "w_rec": w_rec, "w_gamma": rec["gamma_w"].T, "w_rec_out": rec["Wo"].T, "vec": vec,
        "w_gu": w_gu, "w_dn": ff["down_w"].T, "ffn_scale": ffn_scale, "down_s": ff["down_s"],
        "wk": by_step(att["Wk"]), "wv": by_step(att["Wv"]), "wq": by_step(att["Wq"]), "wo": wo,
        "bk": by_step(att["bk"][None])[:, 0], "bq": by_step(att["bq"][None])[:, 0],
        "bv": by_step(att["bv"][None])[:, 0].reshape(NH, NQ).T, "bo": att["bo"],
    }
    nc = bacc.Bacc("TRN2", target_bir_lowering=False, num_devices=1)
    arrays = {n: np.ascontiguousarray(v) for n, v in arrays.items()}
    args = [nc.dram_tensor(n, v.shape, mybir.dt.from_np(v.dtype), kind="ExternalInput").ap() for n, v in arrays.items()]
    args.append(nc.dram_tensor("y", (B, T, C), F32, kind="ExternalOutput").ap())
    hybrid_block(nc, *args)
    r = run(nc, [arrays], core_ids=[0])
    return r.results[0]["y"]
```

```python
from contextlib import ExitStack

import concourse.bass as bass
from concourse import mybir

F32 = mybir.dt.float32
F32R = mybir.dt.float32r
ACT = mybir.ActivationFunctionType
ALU = mybir.AluOpType
AX = mybir.AxisListType

P = 128
B, T, C = 4, 256, 256
H, D = 16, 16
TAPS = 4
NH, NQ = 16, 128
INTER = 704
R = T // P
NT = B * R
KC = C // P
HALF = B * T // 2
HT = NT // 2
HB = B // 2
EPS = 1e-5
FULL = INTER // P
REST = INTER - FULL * P
FCH = FULL + 1
NG = 4
STEPS = NH // NG
HL = NG // 2
Y_BLOCKS = NH // 2
SCALE = float(NQ) ** -0.5
BANK = 512

V_TAP, V_CONV_B, V_IG_B, V_GAMMA_B, V_OG_B, V_VN_G, V_VN_B, V_MN_G, V_MN_B, V_GN_G, V_GN_B = 0, 4, 5, 6, 7, 8, 9, 10, 11, 12, 13
N_VEC = 14
W_K, W_V, W_Q, W_IG, W_OG, W_GAMMA = range(6)

ORDER = [
    ("xt", 0), ("conv", 0), ("k", 0), ("v", 0), ("silu", 0), ("q", 0), ("lx", 1), ("nv", 0), ("nk", 0), ("nq", 0),
    ("xt", 1), ("rk", 0), ("ig", 0), ("gamma", 0), ("og", 0), ("scan", 0), ("k", 1), ("v", 1), ("conv", 1), ("mc", 0),
    ("q", 1), ("mv", 0), ("silu", 1), ("nv", 1), ("nk", 1), ("nq", 1), ("oc", 0), ("ov", 0), ("rk", 1), ("ig", 1),
    ("gamma", 1), ("wo", 0), ("ln", 0), ("og", 1), ("ft", 0), ("scan", 1), ("gu0", 0), ("mc", 1), ("gu1", 0),
    ("mv", 1), ("gu2", 0), ("gu3", 0), ("gu4", 0), ("oc", 1), ("gu5", 0), ("ov", 1), ("dna", 0), ("dnb", 0),
    ("wo", 1), ("ln", 1), ("ft", 1), ("lc", 0), ("gu0", 1), ("gu1", 1), ("gu2", 1), ("gu3", 1), ("gu4", 1),
    ("gu5", 1), ("dna", 1), ("lc", 2), ("dnb", 1), ("lc", 3), ("gm", 0), ("gm", 1), ("gm", 2), ("gm", 3)]
ORDER2 = [("ln", 0), ("ft", 0), ("ln", 1), ("gu0", 0), ("gu1", 0), ("ft", 1), ("gu2", 0), ("gu3", 0), ("gu4", 0),
          ("gu5", 0), ("dna", 0), ("dnb", 0), ("gu0", 1), ("gu1", 1), ("gu2", 1), ("gu3", 1), ("gu4", 1),
          ("gu5", 1), ("dna", 1), ("dnb", 1)]
NO_PSUM = ("conv", "silu", "scan", "rk", "ln", "lx", "lc", "dnb")
LOG_EXP, SILU_TANH = "natural_log_exp_and_others", "silu_and_others"
TABLES = {"rk": LOG_EXP, "nv": LOG_EXP, "mv": LOG_EXP, "ov": LOG_EXP,
          "silu": SILU_TANH, "ig": SILU_TANH, "gamma": SILU_TANH, "og": SILU_TANH}
LN_X, LN_FFN, LN_CHAN, LN_FFN2 = range(4)


def upto(h, m):
    return KC * h + m + 1


def pair_plan(order, first=0):
    pair, before, held = {}, {}, [None] * 4
    due = [(q - first) % 4 - 4 for q in range(4)]
    for n, step in enumerate(s for s in order if s[0] not in NO_PSUM):
        q = due.index(min(due))
        pair[step], before[step] = q, held[q]
        held[q] = step
        due[q] = n + (2.5 if step[0] in ("mc", "oc") else 0)
    return pair, before


def tables_ahead(n):
    for name, _ in ORDER[n:]:
        if name in TABLES or name.startswith("gu"):
            return TABLES.get(name, SILU_TANH)
    return LOG_EXP


class FfnBuffers:

    def __init__(self, XTh, XTl, SG, HD, HDh, HDl, down_hi, down_lo):
        self.XTh, self.XTl, self.SG, self.HD, self.HDh, self.HDl = XTh, XTl, SG, HD, HDh, HDl
        self.down_hi, self.down_lo = down_hi, down_lo


def loop_value(i, per_step, nth):
    return (i + 1) * per_step + nth


def hybrid_block(nc, x, w_rec, w_gamma, w_rec_out, vec, w_gu, w_dn, ffn_scale, down_s,
                 wk, wv, wq, wo, bk, bq, bv, bo, out):
    pair, before = pair_plan(ORDER)
    pair2, before2 = pair_plan(ORDER2, (A_PAIR[1] + 1) % 4)
    with ExitStack() as ctx:
        def sem(name):
            return ctx.enter_context(nc.semaphore(name))

        def sb(name, shape, dt=F32, scope=ctx):
            return scope.enter_context(nc.sbuf_tensor(name, shape, dt))

        s = {n: sem(n) for n in """
            x0_in x1_in x23_in w_kv_in w_rest_in w_gamma_in w_out_in vec_in w_gu_in w_dn_in scale_in down_s_in
            wk_in wv_in wq_in wo_in bk_in bq_in bv_in bo_in x_out
            consts_pool consts_dve centred gamma_rep vec_half rec_hi rec_split gu_split dn_scaled
            ln_stat ln_agg ln_eps ln_rstd ln_done
            xt_ps xt_f xt_hi xt_lo conv_m0 conv_m1 silu_done xc_hi xc_lo
            q_ps k_ps v_ps ig_ps og_ps gamma_ps q_cp k_cp v_cp q_sq k_sq v_sq ti_done to_done tg_done gamma_done
            nq_ps nk_ps nv_ps nq_max nk_max nq_ln nk_ln nv_ln rq_done rk_done rv_done
            qn_done k_n k_g v_n v_a b_done mem_done
            mc_ps mc_sq mv_ps mv_ln r1_done y_n y_a o_done
            oc_ps oc_sq ov_ps ov_ln r2_done z_n z_a z_done wo_ps rec_added
            ft_ps ft_hi ft_lo gu_ps silu_g hd_done hd_hi hd_lo hd_lo_last dn_hi dn_lo dn_ps ffn_added
            bo_added x_hi x_lo g_ps g_hi g_lo s_cp s_zero s_hi s_lo mask_done ones_r_done
            raw_k_free raw_o_free raw_v_free wk_split wo_split wv_split bq_split bq_raw_free
            r_ps r_sum r_mask r_hi r_lo z_ps z_added w_ps w_cp s_ps negmax bias_done exp_done rsum
            e_norm p_ps p_hi p_lo t_ps t_hi t_lo u_ps u_added u_hi u_lo a_ps a_added""".split()}

        ps = ctx.enter_context(nc.psum_tensor("ps", [P, 4, 2, BANK], F32))

        X = sb("X", [P, NT, C])
        XN = sb("XN", [P, NT, C + 2])
        gu_hi = sb("gu_hi", [P, KC, 2 * INTER], F32R)
        gu_lo = sb("gu_lo", [P, KC, 2 * INTER], F32R)
        w_down = sb("w_down", [P, FCH, C])
        f_scale = sb("f_scale", [P, 2 * FCH])
        ident = sb("ident", [P, P])
        heads_ones = sb("heads_ones", [P, P])
        centre = sb("centre", [P, P])
        eps_col = sb("eps_col", [P, 1])
        minus_half = sb("minus_half", [P, NT])
        stats = sb("stats", [P, NT, 6])
        agg = sb("agg", [P, NT, 2])
        var_eps = sb("var_eps", [P, NT])
        rstd = sb("rstd", [P, NT])

        one = ctx.enter_context(ExitStack())
        w_hi = sb("w_hi", [P, KC, 6, C], F32R, one)
        w_lo = sb("w_lo", [P, KC, 6, C], F32R, one)
        q_t, k_t, v_t, sq_q, sq_k, sq_v, t_og, mem = (
            sb(n, [P, 2, KC, HALF], F32, one) for n in ("q_t", "k_t", "v_t", "sq_q", "sq_k", "sq_v", "t_og", "mem"))
        w_out = sb("w_out", [P, KC, C], F32, one)
        down_b = sb("down_b", [P, C], F32, one)
        vecs = sb("vecs", [P, KC, N_VEC], F32, one)
        gam = sb("gam", [P, KC, H], F32, one)
        msum = sb("msum", [P, KC, H], F32, one)
        XCf = sb("XCf", [P, KC, HALF], F32, one)
        XCh = sb("XCh", [P, KC, HALF], F32R, one)
        XCl = sb("XCl", [P, KC, HALF], F32R, one)
        XTf = sb("XTf", [P, KC, HALF], F32, one)
        XTh = sb("XTh", [P, KC, HALF], F32R, one)
        XTl = sb("XTl", [P, KC, HALF], F32R, one)
        SG = sb("SG", [P, 2, HALF], F32, one)
        with ExitStack() as early:
            gates = sb("gates", [P, 2, 2, KC, HALF], F32, early)
            raw = sb("raw", [P, KC * 6 * C], F32, early)
        t_ig, t_ga = gates[:, 0], gates[:, 1]
        down_hi = sb("down_hi", [P, FCH, C], F32R, one)
        down_lo = sb("down_lo", [P, FCH, C], F32R, one)
        HDh = sb("HDh", [P, FCH, HALF], F32R, one)
        HDl = sb("HDl", [P, FCH, HALF], F32R, one)
        ffn1 = FfnBuffers((XTh, XCh), (XTl, XCl), SG, (XTf[:, 0], XTf[:, 1], XCf[:, 0], XCf[:, 1]),
                          HDh, HDl, down_hi, down_lo)
        w_raw = raw[:].rearrange("p (k w c) -> p k w c", k=KC, w=6)
        gu_raw = raw[:, 0:KC * 2 * INTER].rearrange("p (k n) -> p k n", k=KC)
        one.close()

        two = ctx.enter_context(ExitStack())
        raw_k = sb("raw_k", [P, KC, NG * NQ], F32, two)
        raw_v = sb("raw_v", [P, KC, NG * NQ], F32, two)
        raw_o = sb("raw_o", [P, R, HL * C], F32, two)
        raw_q = sb("raw_q", [P, KC, NG * NQ], F32, two)
        wk_hi = sb("wk_hi", [P, KC, NG * NQ], F32R, two)
        wk_lo = sb("wk_lo", [P, KC, NG * NQ], F32R, two)
        wo_hi = sb("wo_hi", [P, R, HL * C], F32R, two)
        wo_lo = sb("wo_lo", [P, R, HL * C], F32R, two)
        bk_b = sb("bk_b", [P, NG * NQ], F32, two)
        bq_b = sb("bq_b", [96, NG * NQ], F32, two)
        bq_s = sb("bq_s", [96, NG * NQ], F32R, two)
        bv_c = sb("bv_c", [P, NH], F32, two)
        bo_b = sb("bo_b", [P, C], F32, two)
        XH = sb("XH", [P, NT, C], F32R, two)
        XL = sb("XL", [P, NT, C], F32R, two)
        G_hi = sb("G_hi", [P, B, KC, C], F32R, two)
        G_lo = sb("G_lo", [P, B, KC, C], F32R, two)
        S_col = sb("S_col", [P, KC, B], F32, two)
        S_hi = sb("S_hi", [P, KC, P], F32R, two)
        S_lo = sb("S_lo", [P, KC, P], F32R, two)
        ones_r = sb("ones_r", [P, P], F32R, two)
        mask = sb("mask", [96, B], F32, two)
        wv_hi = sb("wv_hi", [P, KC, NG * NQ], F32R, two)
        wv_lo = sb("wv_lo", [P, KC, NG * NQ], F32R, two)
        r_row = sb("r_row", [P, NG * NQ], F32, two)
        r_masked = XN[:].rearrange("p a b -> p (a b)")[0:96, 0:NG * B * NQ].rearrange(
            "p (g b n) -> p g b n", g=NG, b=B)
        w_sum = sb("w_sum", [P, HL, C], F32, two)
        E = sb("E", [P, 2, B, NQ], F32, two)
        neg = sb("neg", [P, 2, B], F32, two)
        e_bias = sb("e_bias", [P, 2, B], F32, two)
        e_sum = sb("e_sum", [P, 2, B], F32, two)
        e_inv = sb("e_inv", [P, 2, B], F32, two)
        ET_hi = sb("ET_hi", [P, NG, B, NQ], F32R, two)
        P_hi = sb("P_hi", [P, KC, B, HL, C], F32R, two)
        P_lo = sb("P_lo", [P, KC, B, HL, C], F32R, two)
        U_hi = sb("U_hi", [P, HL, B, C], F32R, two)
        with ExitStack() as scored:
            Z = sb("Z", [P, KC, B, NG * NQ], F32, scored)
            r_s = sb("r_s", [96, NG, B, NQ], F32R, scored)
        ET_lo = sb("ET_lo", [P, NG, B, NQ], F32R, two)
        U_lo = sb("U_lo", [P, HL, B, C], F32R, two)
        U = sb("U", [P, 2, B, C], F32, two)
        two.close()

        ffn2 = FfnBuffers(
            [sb(f"XTh2{h}", [P, KC, HALF], F32R) for h in range(2)], [sb(f"XTl2{h}", [P, KC, HALF], F32R) for h in range(2)],
            sb("SG2", [P, 2, HALF]), [sb(f"HD2{n}", [P, HALF]) for n in range(4)],
            sb("HDh2", [P, FCH, HALF], F32R), sb("HDl2", [P, FCH, HALF], F32R),
            sb("down_hi2", [P, FCH, C], F32R), sb("down_lo2", [P, FCH, C], F32R))
        ffn = [ffn1, ffn2]

        freed, freed2 = {}, {}
        for h in range(2):
            freed["xt", h] = [(s["xt_f"], upto(h, 1))]
            for name, done in (("ig", "ti_done"), ("og", "to_done"), ("q", "q_cp"), ("k", "k_cp"), ("v", "v_cp"),
                               ("gamma", "tg_done"), ("nq", "nq_max"), ("nk", "nk_max"), ("nv", "nv_ln"), ("mc", "y_n"),
                               ("mv", "mv_ln"), ("oc", "z_n"), ("ov", "ov_ln")):
                freed[name, h] = [(s[done], upto(h, 1))]
            freed["wo", h] = [(s["rec_added"], HB * (h + 1))]
            for f, table in enumerate((freed, freed2)):
                n = 2 * f + h
                table["ft", h] = [(s["ft_lo"], upto(n, 1))]
                table["dna", h] = [(s["ffn_added"], HB * (n + 1))]
                for c in range(FCH):
                    table[f"gu{c}", h] = [(s["hd_done"], n * FCH + c + 1)]
        for b in range(B):
            freed["gm", b] = [(s["g_lo"], b + 1), (s["s_cp"], b + 1)]

        def bank_pair(name, h):
            return ps[:, pair[name, h]]

        def bank_pair2(name, h):
            return ps[:, pair2[name, h]]

        def gu_before(f, h):
            return (2 * f + h) * FCH

        def rows_of(c):
            return P if c < FULL else REST

        def down_blocks(t):
            return t[:, 0:FULL], t[0:REST, FULL:FCH]

        def half_batches(h):
            return range(HB * h, HB * (h + 1))

        def batches_of_lc(b):
            return half_batches(0) if b == 0 else range(b, b + 1)

        def token_cols(t):
            b, r = t // R, t % R
            return slice(b * T + r, (b + 1) * T, R)

        def by_tile(bank):
            return bank.rearrange("p (b r n) -> p b r n", b=HB, r=R)

        def in_time(row):
            return row.rearrange("p (b n r) -> p b r n", b=HB, r=R)

        block = ctx.enter_context(nc.Block())

        @block.sync
        def _(sp):
            x_view = X[:].rearrange("p (b r) c -> p b (r c)", r=R)
            x_rows = x.rearrange("b (p r) c -> p b (r c)", r=R)
            w_rows = w_rec.rearrange("(k p) w c -> p k w c", p=P)
            sp.dma_start(x_view[:, 0:1], x_rows[:, 0:1]).then_inc(s["x0_in"], 16)
            sp.dma_start(x_view[:, 1:HB], x_rows[:, 1:HB]).then_inc(s["x1_in"], 16)
            sp.dma_start(w_raw[:, :, W_K:W_V + 1, :], w_rows[:, :, W_K:W_V + 1]).then_inc(s["w_kv_in"], 16)
            sp.dma_start(vecs[:], vec.rearrange("(k p) v -> p k v", p=P)).then_inc(s["vec_in"], 16)
            sp.dma_start(gam[:], w_gamma.rearrange("(k p) h -> p k h", p=P)).then_inc(s["w_gamma_in"], 16)
            sp.dma_start(w_raw[:, :, W_Q:W_OG + 1, :], w_rows[:, :, W_Q:W_OG + 1]).then_inc(s["w_rest_in"], 16)
            sp.dma_start(x_view[:, HB:B], x_rows[:, HB:B]).then_inc(s["x23_in"], 16)
            sp.dma_start(w_out[:], w_rec_out.rearrange("(k p) c -> p k c", p=P)).then_inc(s["w_out_in"], 16)
            sp.dma_start(f_scale[:], ffn_scale).then_inc(s["scale_in"], 16)
            sp.wait_ge(s["rec_split"], 6)
            sp.dma_start(gu_raw, w_gu.rearrange("(k p) n -> p k n", p=P)).then_inc(s["w_gu_in"], 16)
            sp.dma_start(w_down[:, 0:FULL, :], w_dn[0:FULL * P].rearrange("(n p) c -> p n c", p=P)).then_inc(s["w_dn_in"], 16)
            sp.dma_start(w_down[0:REST, FULL, :], w_dn[FULL * P:INTER]).then_inc(s["w_dn_in"], 16)
            sp.dma_start(down_b[:], down_s.partition_broadcast(P)).then_inc(s["down_s_in"], 16)

            def load_step(i):
                sp.dma_start(raw_k[:], wk[i].rearrange("(k p) n -> p k n", p=P)).then_inc(s["wk_in"], 16)
                sp.dma_start(bk_b[:], bk[i].partition_broadcast(P)).then_inc(s["bk_in"], 16)
                sp.dma_start(raw_o[:], wo[i].rearrange("(p r) n -> p r n", r=R)).then_inc(s["wo_in"], 16)
                sp.dma_start(raw_v[:], wv[i].rearrange("(k p) n -> p k n", p=P)).then_inc(s["wv_in"], 16)
                sp.dma_start(bq_b[:], bq[i].partition_broadcast(96)).then_inc(s["bq_in"], 16)
                sp.dma_start(raw_q[:], wq[i].rearrange("(k p) n -> p k n", p=P)).then_inc(s["wq_in"], 16)

            sp.wait_ge(s["wo_ps"], B)
            sp.dma_start(bv_c[:], bv).then_inc(s["bv_in"], 16)
            sp.dma_start(bo_b[:], bo.partition_broadcast(P)).then_inc(s["bo_in"], 16)
            load_step(0)
            with sp.Fori(1, STEPS) as i:
                sp.wait_ge(s["raw_k_free"], loop_value(i - 1, 1, 1))
                sp.dma_start(raw_k[:], wk[bass.ds(i, 1)].rearrange("o (k p) n -> p (o k) n", p=P)).then_inc(s["wk_in"], 16)
                sp.wait_ge(s["z_added"], loop_value(i - 1, 2 * B, 2 * B))
                sp.wait_ge(s["r_sum"], loop_value(i - 1, 1, 1))
                sp.dma_start(bk_b[:], bk[bass.ds(i, 1)].rearrange("o n -> (o n)").partition_broadcast(P)).then_inc(s["bk_in"], 16)
                sp.wait_ge(s["raw_o_free"], loop_value(i - 1, 1, 1))
                sp.dma_start(raw_o[:], wo[bass.ds(i, 1)].rearrange("o (p r) n -> p (o r) n", r=R)).then_inc(s["wo_in"], 16)
                sp.wait_ge(s["raw_v_free"], loop_value(i - 1, 1, 1))
                sp.dma_start(raw_v[:], wv[bass.ds(i, 1)].rearrange("o (k p) n -> p (o k) n", p=P)).then_inc(s["wv_in"], 16)
                sp.wait_ge(s["bq_raw_free"], loop_value(i - 1, 1, 1))
                sp.dma_start(bq_b[:], bq[bass.ds(i, 1)].rearrange("o n -> (o n)").partition_broadcast(96)).then_inc(s["bq_in"], 16)
                sp.wait_ge(s["s_ps"], loop_value(i - 1, NG, NG))
                sp.dma_start(raw_q[:], wq[bass.ds(i, 1)].rearrange("o (k p) n -> p (o k) n", p=P)).then_inc(s["wq_in"], 16)

            o_view = out.rearrange("b (p r) c -> p b (r c)", r=R)
            for b in range(B):
                sp.wait_ge(s["ffn_added"], B + b + 1)
                sp.dma_start(o_view[:, b], x_view[:, b]).then_inc(s["x_out"], 16)
            sp.wait_ge(s["x_out"], 16 * B)

        @block.gpsimd
        def _(pool):
            pool.memset(ident[:], 0.0).then_inc(s["consts_pool"], 1)
            pool.memset(heads_ones[:], 1.0).then_inc(s["consts_pool"], 1)
            pool.memset(eps_col[:], EPS).then_inc(s["consts_pool"], 1)
            pool.memset(minus_half[:], -0.5).then_inc(s["consts_pool"], 1)
            pool.wait_ge(s["consts_pool"], 4)
            pool.affine_select(out=ident[:], in_=ident[:], compare_op=ALU.not_equal, fill=1.0, base=0,
                               pattern=[[-1, P]], channel_multiplier=1).then_inc(s["consts_pool"], 1)
            blocks = heads_ones[:].rearrange("p (h d) -> p h d", d=D)
            pool.affine_select(out=blocks, in_=blocks, compare_op=ALU.is_ge, fill=0.0, base=0,
                               pattern=[[-D, P // D], [0, D]], channel_multiplier=1).then_inc(s["consts_pool"], 1)
            pool.wait_ge(s["consts_pool"], 6)
            pool.affine_select(out=blocks, in_=blocks, compare_op=ALU.is_ge, fill=0.0, base=D - 1,
                               pattern=[[D, P // D], [0, D]], channel_multiplier=-1).then_inc(s["consts_pool"], 1)

            def layer_norm(kind, batches):
                for b in batches:
                    tiles = slice(R * b, R * (b + 1))
                    pool.wait_ge(s["ln_eps"], B * kind + b + 1)
                    pool.tensor_tensor(rstd[:, tiles], var_eps[:, tiles], minus_half[:, 0:R],
                                       ALU.pow).then_inc(s["ln_rstd"], 1)

            def step_silu(h):
                if h:
                    pool.wait_ge(s["og_ps"], upto(0, 1))
                for m in range(KC):
                    pool.wait_ge(s["silu_done"], upto(h, m))
                    pool.tensor_scalar(XCh[:, m], XCf[:, m], 1.0, 0.0, ALU.mult, ALU.add).then_inc(s["xc_hi"], 1)

            def step_rk(h):
                for m in range(KC):
                    pool.wait_ge(s["rq_done"], upto(h, m))
                    pool.wait_ge(s["q_cp"], upto(h, m))
                    pool.tensor_tensor(q_t[:, h, m], q_t[:, h, m], sq_q[:, h, m], ALU.mult).then_inc(s["qn_done"], 1)

            def split_gate_up():
                pool.wait_ge(s["w_gu_in"], 16)
                pool.tensor_scalar(gu_hi[:], gu_raw, 1.0, 0.0, ALU.mult, ALU.add).then_inc(s["gu_split"], 1)
                pool.wait_ge(s["gu_split"], 1)
                pool.tensor_tensor(gu_lo[:], gu_raw, gu_hi[:].bitcast(F32), ALU.subtract).then_inc(s["gu_split"], 1)

            def step_gu(f, h, c):
                w, n, at = ffn[f], 2 * f + h, gu_before(f, h) + c
                if c:
                    pool.wait_ge(s["hd_hi"], FCH * n + c)
                    pool.tensor_tensor(w.HDl[:, c - 1], w.HD[(at - 1) % 4][:], w.HDh[:, c - 1].bitcast(F32),
                                       ALU.subtract).then_inc(s["hd_lo"], 1)

            def down_low(f):
                for n, (raw, hi, lo) in enumerate(zip(down_blocks(w_down), down_blocks(ffn[f].down_hi), down_blocks(ffn[f].down_lo))):
                    pool.wait_ge(s["dn_hi"], 2 * f + n + 1)
                    pool.tensor_tensor(lo, raw, hi.bitcast(F32), ALU.subtract).then_inc(s["dn_lo"], 1)

            layer_norm(LN_X, half_batches(0))
            for step, h in ORDER:
                if step.startswith("gu"):
                    step_gu(0, h, int(step[2:]))
                    if (step, h) == ("gu1", 0):
                        down_low(0)
                elif step == "lx":
                    layer_norm(LN_X, half_batches(h))
                elif step == "silu":
                    step_silu(h)
                    if h == 1:
                        split_gate_up()
                elif step == "rk":
                    step_rk(h)
                elif step == "ln":
                    layer_norm(LN_FFN, half_batches(h))
                elif step == "lc":
                    layer_norm(LN_CHAN, batches_of_lc(h))

            pool.wait_ge(s["mask_done"], 3)
            pool.sem_inc(s["r_mask"], 1)
            pool.sem_inc(s["r_lo"], 1)
            def split_next(raw, hi, lo, done, free, i):
                pool.wait_ge(done, loop_value(i + 1, 2, 1))
                pool.tensor_tensor(lo[:], raw[:], hi[:].bitcast(F32), ALU.subtract).then_inc(done, 1)
                pool.wait_ge(done, loop_value(i + 1, 2, 2))
                pool.sem_inc(free, 1)

            def attention_step(i, last):
                pool.wait_ge(s["r_sum"], loop_value(i, 1, 1))
                pool.wait_ge(s["r_lo"], loop_value(i - 1, 1, 1))
                for g in range(NG):
                    rm = pool.tensor_tensor(
                        r_masked[:, g],
                        r_row[0:96, g * NQ:(g + 1) * NQ].unsqueeze(1).to_broadcast([96, B, NQ]),
                        mask[:].unsqueeze(2).to_broadcast([96, B, NQ]), ALU.mult)
                rm.then_inc(s["r_mask"], 1)
                pool.wait_ge(s["r_hi"], loop_value(i, 1, 1))
                pool.wait_ge(s["r_mask"], loop_value(i, 1, 1))
                pool.tensor_tensor(r_s[32:64], r_masked[32:64], r_s[32:64].bitcast(F32),
                                   ALU.subtract).then_inc(s["r_lo"], 1)
                if not last:
                    pool.wait_ge(s["r_lo"], loop_value(i, 1, 1))
                    split_next(raw_k, wk_hi, wk_lo, s["wk_split"], s["raw_k_free"], i)
                    split_next(raw_o, wo_hi, wo_lo, s["wo_split"], s["raw_o_free"], i)

            with pool.Fori(0, STEPS - 1) as i:
                attention_step(i, False)
            attention_step(STEPS - 1, True)
            for step, h in ORDER2:
                if step == "ln":
                    layer_norm(LN_FFN2, half_batches(h))
                elif step.startswith("gu"):
                    step_gu(1, h, int(step[2:]))
                    if (step, h) == ("gu0", 0):
                        down_low(1)

        @block.scalar
        def _(act):
            def rsqrt_of(src, dst, scale, bias, ln_sem, done_sem, h, ready):
                for m in range(KC):
                    act.wait_ge(ready, upto(h, m))
                    act.activation(dst[:, m], src[:, m], ACT.Ln, scale=scale, bias=bias).then_inc(ln_sem, 1)
                for m in range(KC):
                    act.wait_ge(ln_sem, upto(h, m))
                    act.activation(dst[:, m], dst[:, m], ACT.Exp, scale=-0.5).then_inc(done_sem, 1)

            def step_xt(h):
                for m in range(KC):
                    act.wait_ge(s["xt_ps"], upto(h, m))
                    if h:
                        act.wait_ge(s["q_ps"], upto(0, 1))
                    act.copy(in_time(XTh[:, m]), by_tile(bank_pair("xt", h)[:, m])).then_inc(s["xt_hi"], 1)
                for m in range(KC):
                    act.wait_ge(s["xt_lo"], upto(h, m))
                    if h:
                        act.wait_ge((s["conv_m0"], s["conv_m1"])[m], TAPS)
                    act.copy(in_time(XTf[:, m]), by_tile(bank_pair("xt", h)[:, m])).then_inc(s["xt_f"], 1)

            def step_silu(h):
                for m, conv in enumerate((s["conv_m0"], s["conv_m1"])):
                    act.wait_ge(conv, TAPS * (h + 1))
                    act.activation(XCf[:, m], XCf[:, m], ACT.Silu,
                                   bias=vecs[:, m, V_CONV_B:V_CONV_B + 1]).then_inc(s["silu_done"], 1)

            def square_and_copy(name, h, dst, sq):
                for m in range(KC):
                    act.wait_ge(s[name + "_ps"], upto(h, m))
                    act.activation(sq[:, h, m], bank_pair(name, h)[:, m], ACT.Square).then_inc(s[name + "_sq"], 1)
                for m in range(KC):
                    act.copy(dst[:, h, m], bank_pair(name, h)[:, m]).then_inc(s[name + "_cp"], 1)

            def gate(name, h, dst, done, col):
                act.wait_ge(s["vec_half"], 1)
                for m in range(KC):
                    act.wait_ge(s[name + "_ps"], upto(h, m))
                    act.activation(dst[:, h, m], bank_pair(name, h)[:, m], ACT.Tanh, scale=0.5,
                                   bias=vecs[:, m, col:col + 1]).then_inc(done, 1)

            def step_nv(h):
                rsqrt_of(bank_pair("nv", h), sq_v[:, h], 1.0 / D, eps_col[:], s["nv_ln"], s["rv_done"], h, s["nv_ps"])

            def step_rk(h):
                rsqrt_of(sq_k[:, h], sq_k[:, h], 1.0, 0.0, s["nk_ln"], s["rk_done"], h, s["nk_max"])
                rsqrt_of(sq_q[:, h], sq_q[:, h], 1.0, 0.0, s["nq_ln"], s["rq_done"], h, s["nq_max"])

            def step_mc(h):
                for m in range(KC):
                    act.wait_ge(s["mc_ps"], upto(h, m))
                    act.wait_ge(s["v_n"], upto(h, m))
                    act.activation(sq_v[:, h, m], bank_pair("mc", h)[:, m], ACT.Square).then_inc(s["mc_sq"], 1)

            def step_mv(h):
                rsqrt_of(bank_pair("mv", h), sq_v[:, h], 1.0 / D, eps_col[:], s["mv_ln"], s["r1_done"], h, s["mv_ps"])

            def step_oc(h):
                for m in range(KC):
                    act.wait_ge(s["oc_ps"], upto(h, m))
                    act.wait_ge(s["qn_done"], upto(h, m))
                    act.activation(sq_q[:, h, m], bank_pair("oc", h)[:, m], ACT.Square).then_inc(s["oc_sq"], 1)

            def step_ov(h):
                rsqrt_of(bank_pair("ov", h), sq_q[:, h], 1.0 / D, eps_col[:], s["ov_ln"], s["r2_done"], h, s["ov_ps"])

            def step_gm(b):
                act.wait_ge(s["g_ps"], b + 1)
                act.copy(G_hi[:, b], bank_pair("gm", b)[:, :, 0:C]).then_inc(s["g_hi"], 1)

            def round_weights(block_):
                act.copy(w_hi[:, :, block_], w_raw[:, :, block_]).then_inc(s["rec_hi"], 1)

            def step_ft(f, h, psum):
                if f == 0:
                    act.wait_ge(s["q_ps"], upto(1, 1))
                    act.wait_ge(s["og_ps"], upto(1, 1))
                for m in range(KC):
                    act.wait_ge(s["ft_ps"], upto(2 * f + h, m))
                    act.copy(in_time(ffn[f].XTh[h][:, m]), by_tile(psum[:, m])).then_inc(s["ft_hi"], 1)

            def round_hidden(f, h, c):
                rows = rows_of(c)
                act.wait_ge(s["hd_done"], gu_before(f, h) + c + 1)
                if h:
                    act.wait_ge(s["dn_ps"], B * f + HB)
                act.copy(ffn[f].HDh[0:rows, c], ffn[f].HD[(gu_before(f, h) + c) % 4][0:rows]).then_inc(s["hd_hi"], 1)

            def down_high(f):
                act.wait_ge(s["dn_scaled"], 2)
                act.wait_ge(s["mem_done"], 2 * KC * HB)
                for raw, hi in zip(down_blocks(w_down), down_blocks(ffn[f].down_hi)):
                    act.copy(hi, raw).then_inc(s["dn_hi"], 1)

            def step_gu(f, h, c, psum):
                w, at = ffn[f], gu_before(f, h) + c
                rows = rows_of(c)
                act.wait_ge(s["scale_in"], 16)
                act.wait_ge(s["gu_ps"], at + 1)
                if at % (2 * FCH) >= 2:
                    act.wait_ge(s["hd_done"], at - 1)
                act.activation(w.SG[0:rows, at % 2], psum[0:rows, 0], ACT.Silu,
                               scale=f_scale[0:rows, c:c + 1]).then_inc(s["silu_g"], 1)
                if c:
                    round_hidden(f, h, c - 1)
                if c == FULL:
                    round_hidden(f, h, c)

            act.wait_ge(s["w_kv_in"], 16)
            round_weights(W_K)
            act.wait_ge(s["consts_pool"], 7)
            act.wait_ge(s["vec_in"], 16)
            for n, (step, h) in enumerate(ORDER):
                if n == 0 or tables_ahead(n) != tables_ahead(n - 1):
                    act.preload_act_table_set(tables_ahead(n))
                if step == "xt":
                    step_xt(h)
                    if h == 0:
                        act.wait_ge(s["centred"], 4)
                        round_weights(W_V)
                        act.wait_ge(s["w_rest_in"], 16)
                        for block_ in (W_Q, W_IG, W_OG):
                            round_weights(block_)
                        act.wait_ge(s["gamma_rep"], 2)
                        round_weights(W_GAMMA)
                elif step == "silu":
                    step_silu(h)
                elif step == "k":
                    square_and_copy("k", h, k_t, sq_k)
                elif step == "v":
                    square_and_copy("v", h, v_t, sq_v)
                elif step == "q":
                    square_and_copy("q", h, q_t, sq_q)
                elif step == "ig":
                    gate("ig", h, t_ig, s["ti_done"], V_IG_B)
                elif step == "gamma":
                    gate("gamma", h, t_ga, s["tg_done"], V_GAMMA_B)
                elif step == "og":
                    gate("og", h, t_og, s["to_done"], V_OG_B)
                elif step == "nv":
                    step_nv(h)
                elif step == "rk":
                    step_rk(h)
                elif step == "mc":
                    step_mc(h)
                elif step == "mv":
                    step_mv(h)
                elif step == "oc":
                    step_oc(h)
                elif step == "ov":
                    step_ov(h)
                elif step == "ft":
                    step_ft(0, h, bank_pair("ft", h))
                elif step.startswith("gu"):
                    step_gu(0, h, int(step[2:]), bank_pair(step, h))
                    if (step, h) == ("gu1", 0):
                        down_high(0)
                elif step == "gm":
                    step_gm(h)

            for sm, per in ((s["r_hi"], 1), (s["w_cp"], 1), (s["exp_done"], NG * B), (s["p_hi"], B), (s["t_hi"], 2),
                            (s["u_hi"], 2 * NG)):
                act.sem_inc(sm, per)
            act.preload_act_table_set(LOG_EXP)
            def attention_step(i, last):
                act.wait_ge(s["r_mask"], loop_value(i, 1, 1))
                act.wait_ge(s["s_ps"], loop_value(i - 1, NG, NG))
                act.wait_ge(s["u_lo"], loop_value(i - 1, 2 * NG, 2 * NG))
                act.copy(r_s[:], r_masked).then_inc(s["r_hi"], 1)
                act.wait_ge(s["w_ps"], loop_value(i, 1, 1))
                act.wait_ge(s["u_added"], loop_value(i - 1, 2 * NG, 2 * NG))
                act.copy(w_sum[:].rearrange("p a c -> p (a c)"), ps[:, 1, 0, :]).then_inc(s["w_cp"], 1)

                def exps(g):
                    j = g % 2
                    act.wait_ge(s["bias_done"], loop_value(i, NG, g + 1))
                    act.wait_ge(s["t_ps"], loop_value(i, 2, g // 2))
                    act.wait_ge(s["e_norm"], loop_value(i, NG, g - 1))
                    for b in range(B):
                        act.activation(E[:, j, b], ps[:, S_PAIR[g // 2], j, b * NQ:(b + 1) * NQ], ACT.Exp,
                                       scale=SCALE, bias=e_bias[:, j, b:b + 1],
                                       accum_out=e_sum[:, j, b:b + 1]).then_inc(s["exp_done"], 1)

                def transposed(j):
                    act.wait_ge(s["t_ps"], loop_value(i, 2, j + 1))
                    act.wait_ge(s["a_ps"], loop_value(i - 1, 4, 2 * j + 2))
                    act.copy(ET_hi[:, 2 * j:2 * j + 2].rearrange("p g b n -> p g (b n)"),
                             ps[:, T_PAIR[j]]).then_inc(s["t_hi"], 1)

                def round_values(n):
                    for j in range(2):
                        if n == 0:
                            act.wait_ge(s["a_ps"], loop_value(i - 1, 4, j + 3))
                        else:
                            act.wait_ge(s["a_ps"], loop_value(i, 4, j + 1))
                        for g in (2 * n, 2 * n + 1):
                            act.wait_ge(s["u_added"], loop_value(i, 2 * NG, 2 * g + j + 1))
                            act.copy(U_hi[:, g % HL, 2 * j:2 * j + 2], U[:, g % 2, 2 * j:2 * j + 2]).then_inc(s["u_hi"], 1)

                def round_next(raw, hi, got, used, used_count, done):
                    act.wait_ge(got, 16 * (i + 2))
                    act.wait_ge(used, loop_value(i, used_count, used_count))
                    act.copy(hi[:], raw[:]).then_inc(done, 1)

                def round_p(b):
                    act.wait_ge(s["p_ps"], loop_value(i, B, b + 1))
                    act.wait_ge(s["u_ps"], loop_value(i - 1, 2 * NG, 2 * NG))
                    act.copy(P_hi[:, :, b].rearrange("p m l c -> p m (l c)"), ps[:, P_PAIR[b]]).then_inc(s["p_hi"], 1)

                round_p(0)
                exps(0)
                exps(1)
                for b in range(1, B):
                    round_p(b)
                if not last:
                    round_next(raw_k, wk_hi, s["wk_in"], s["z_ps"], B, s["wk_split"])
                transposed(0)
                exps(2)
                exps(3)
                if not last:
                    round_next(raw_o, wo_hi, s["wo_in"], s["p_ps"], B, s["wo_split"])
                round_values(0)
                transposed(1)
                round_values(1)

            with act.Fori(0, STEPS - 1) as i:
                attention_step(i, False)
            attention_step(STEPS - 1, True)
            act.preload_act_table_set(SILU_TANH)
            for step, h in ORDER2:
                if step == "ft":
                    step_ft(1, h, bank_pair2("ft", h))
                elif step.startswith("gu"):
                    step_gu(1, h, int(step[2:]), bank_pair2(step, h))
                    if (step, h) == ("gu0", 0):
                        down_high(1)

        @block.tensor
        def _(pe):
            def claim(name, h):
                if before[name, h] is not None:
                    for last_read in freed[before[name, h]]:
                        pe.wait_ge(*last_read)
                return bank_pair(name, h)

            def claim2(name, h):
                if before2[name, h] is None:
                    pe.wait_ge(s["a_added"], loop_value(STEPS - 1, 4, 2))
                    if pair2[name, h] == A_PAIR[1]:
                        pe.wait_ge(s["a_added"], loop_value(STEPS - 1, 4, 4))
                else:
                    for last_read in freed2[before2[name, h]]:
                        pe.wait_ge(*last_read)
                return bank_pair2(name, h)

            def split_product(outs, left, right, ready=None):
                for k, ((lh, ll), (rh, rl)) in enumerate(zip(left, right)):
                    if ready:
                        ready(k, 0)
                    pe.matmul(outs, lh, rh, start=(k == 0), stop=False)
                    pe.matmul(outs, ll, rh, start=False, stop=False)
                    if ready:
                        ready(k, 1)
                    mm = pe.matmul(outs, lh, rl, start=False, stop=(k == len(left) - 1))
                return mm

            def transposes(dst, kind, h, done):
                for j, b in enumerate(half_batches(h)):
                    pe.wait_ge(s["ln_done"], B * kind + b + 1)
                    for m in range(KC):
                        for t in range(R * j, R * (j + 1)):
                            tr = pe.transpose(dst[:, m, t * P:(t + 1) * P], XN[:, h * HT + t, m * P:(m + 1) * P], ident[:])
                        if j == HB - 1:
                            tr.then_inc(done, 1)

            def projection(name, block_, h, xh, xl, hi, lo):
                dst = claim(name, h)
                pe.wait_ge(s["rec_split"], block_ + 1)

                def ready(k, part):
                    pe.wait_ge((hi, lo)[part], upto(h, k))

                for m in range(KC):
                    mm = split_product(dst[:, m],
                                       [(w_hi[:, k, block_, m * P:(m + 1) * P], w_lo[:, k, block_, m * P:(m + 1) * P]) for k in range(KC)],
                                       [(xh[:, k], xl[:, k]) for k in range(KC)], ready if m == 0 else None)
                    mm.then_inc(s[name + "_ps"], 1)

            def of_x(name, block_, h):
                projection(name, block_, h, XTh, XTl, s["xt_hi"], s["xt_lo"])

            def of_conv(name, block_, h):
                projection(name, block_, h, XCh, XCl, s["xc_hi"], s["xc_lo"])

            def by_head(name, h, matrix, src, ready, each=1):
                dst = claim(name, h)
                for m in range(KC):
                    pe.wait_ge(ready, each * upto(h, m))
                    pe.matmul(dst[:, m], matrix[:], src[:, h, m], start=True, stop=True).then_inc(s[name + "_ps"], 1)

            def step_wo(h):
                dst = claim("wo", h).rearrange("p a (t c) -> p (a t) c", c=C)
                pe.wait_ge(s["w_out_in"], 16)
                pe.wait_ge(s["z_done"], upto(h, 1))
                for t in range(HT):
                    for k in range(KC):
                        mm = pe.matmul(dst[:, t], k_t[:, h, k, token_cols(t)], w_out[:, k], start=(k == 0), stop=(k == KC - 1))
                    if t % R == R - 1:
                        mm.then_inc(s["wo_ps"], 1)

            def step_gu(f, h, c, dst):
                w, n = ffn[f], 2 * f + h
                pe.wait_ge(s["gu_split"], 2)

                def ready(k, part):
                    pe.wait_ge((s["ft_hi"], s["ft_lo"])[part], upto(n, k))

                right = [(w.XTh[h][:, k], w.XTl[h][:, k]) for k in range(KC)]
                for j in range(2 if c < FULL else 1):
                    cols = slice((2 * c + j) * P, (2 * c + j + 1) * P)
                    mm = split_product(dst[:, j], [(gu_hi[:, k, cols], gu_lo[:, k, cols]) for k in range(KC)], right,
                                       ready if c == 0 and j == 0 else None)
                mm.then_inc(s["gu_ps"], 1)

            def step_dn(f, h, pair_):
                dst = pair_.rearrange("p a (t c) -> p (a t) c", c=C)
                w, n = ffn[f], 2 * f + h
                pe.wait_ge(s["dn_lo"], 2 * (f + 1))

                def chunks(t, first, end):
                    for c in range(first, end):
                        rows = rows_of(c)
                        hi, lo = w.HDh[0:rows, c, token_cols(t)], w.HDl[0:rows, c, token_cols(t)]
                        pe.wait_ge(s["hd_hi"], FCH * n + c + 1)
                        pe.matmul(dst[:, t], hi, w.down_hi[0:rows, c], start=(c == 0), stop=False)
                        pe.matmul(dst[:, t], hi, w.down_lo[0:rows, c], start=False, stop=False)
                        if c < FULL:
                            pe.wait_ge(s["hd_lo"], FULL * n + c + 1)
                        else:
                            pe.wait_ge(s["hd_lo_last"], n + 1)
                        mm = pe.matmul(dst[:, t], lo, w.down_hi[0:rows, c], start=False, stop=(c == FCH - 1))
                    return mm

                for j in range(HB):
                    chunks(R * j, 0, FCH - 2)
                for j in range(HB):
                    chunks(R * j, FCH - 2, FCH)
                    for t in range(R * j + 1, R * (j + 1)):
                        mm = chunks(t, 0, FCH)
                    mm.then_inc(s["dn_ps"], 1)

            def step_gm(b):
                dst = claim("gm", b)
                pe.wait_ge(s["ln_done"], B * LN_CHAN + b + 1)
                for m in range(KC):
                    for k in range(R):
                        mm = pe.matmul(dst[:, m, 0:C + 1], XN[:, b * R + k, m * P:(m + 1) * P],
                                       XN[:, b * R + k, 0:C + 1], start=(k == 0), stop=(k == R - 1))
                mm.then_inc(s["g_ps"], 1)

            pe.wait_ge(s["consts_pool"], 7)
            for step, h in ORDER:
                if step == "xt":
                    transposes(claim("xt", h), LN_X, h, s["xt_ps"])
                elif step in ("q", "k", "v"):
                    of_x(step, {"q": W_Q, "k": W_K, "v": W_V}[step], h)
                elif step in ("ig", "og", "gamma"):
                    of_conv(step, {"ig": W_IG, "og": W_OG, "gamma": W_GAMMA}[step], h)
                elif step in ("nq", "nk", "nv"):
                    by_head(step, h, heads_ones, {"nq": sq_q, "nk": sq_k, "nv": sq_v}[step], s[step[1] + "_sq"])
                elif step == "mc":
                    pe.wait_ge(s["consts_dve"], 2)
                    by_head("mc", h, centre, mem, s["mem_done"], HB)
                elif step == "mv":
                    by_head("mv", h, heads_ones, sq_v, s["mc_sq"])
                elif step == "oc":
                    by_head("oc", h, centre, v_t, s["o_done"])
                elif step == "ov":
                    by_head("ov", h, heads_ones, sq_q, s["oc_sq"])
                elif step == "wo":
                    step_wo(h)
                elif step == "ft":
                    transposes(claim("ft", h), LN_FFN, h, s["ft_ps"])
                elif step.startswith("gu"):
                    step_gu(0, h, int(step[2:]), claim(step, h))
                elif step == "dna":
                    step_dn(0, h, claim("dna", h))
                elif step == "gm":
                    step_gm(h)

            pe.wait_ge(s["ffn_added"], B)
            for sm, per in ((s["r_ps"], 1), (s["z_ps"], B), (s["w_ps"], 1), (s["s_ps"], NG), (s["p_ps"], B), (s["t_ps"], 2),
                            (s["u_ps"], 2 * NG), (s["a_ps"], 4)):
                pe.sem_inc(sm, per)
            def attention_step(i, first, last):
                def scores(g):
                    dst = ps[:, S_PAIR[g // 2], g % 2]
                    cols = slice(g * NQ, (g + 1) * NQ)
                    if g == 0:
                        pe.wait_ge(s["wq_in"], 16 * (i + 1))
                        pe.wait_ge(s["z_added"], loop_value(i, 2 * B, 2 * B))
                    for k in range(KC):
                        pe.matmul(dst, raw_q[:, k, cols], Z[:, k, :, cols], start=(k == 0), stop=False)
                    if g == 0:
                        pe.wait_ge(s["bq_split"], loop_value(i, 2, 2))
                        pe.wait_ge(s["r_lo"], loop_value(i, 1, 1))
                    pe.matmul(dst, bq_s[:, cols], r_s[:, g].rearrange("p b n -> p (b n)"), start=False,
                              stop=True).then_inc(s["s_ps"], 1)

                def transpose_pair(j):
                    pe.wait_ge(s["e_norm"], loop_value(i, NG, 2 * j + 2))
                    for g in range(2):
                        for b in range(B):
                            tr = pe.transpose(ps[:, T_PAIR[j], g, b * NQ:(b + 1) * NQ], E[:, g, b], ident[:])
                    tr.then_inc(s["t_ps"], 1)

                def project_wo(b):
                    for m in range(KC):
                        mm = split_product(ps[:, P_PAIR[b], m],
                                           [(XH[:, b * R + k, m * P:(m + 1) * P], XL[:, b * R + k, m * P:(m + 1) * P]) for k in range(R)],
                                           [(wo_hi[:, k], wo_lo[:, k]) for k in range(R)])
                    mm.then_inc(s["p_ps"], 1)

                def values(g):
                    cols = slice(g * NQ, (g + 1) * NQ)
                    for j in range(2):
                        right = [(P_hi[:, k, 2 * j:2 * j + 2, g % HL], P_lo[:, k, 2 * j:2 * j + 2, g % HL]) for k in range(KC)]
                        mm = split_product(ps[:, U_PAIR[g], j], [(wv_hi[:, k, cols], wv_lo[:, k, cols]) for k in range(KC)], right)
                        mm.then_inc(s["u_ps"], 1)

                def attend(j):
                    dst = ps[:, A_PAIR[j]].rearrange("p a (b c) -> p (a b) c", c=C)
                    for b in range(B):
                        if b == HB:
                            pe.wait_ge(s["u_lo"], loop_value(i, 2 * NG, 2 * HL * (j + 1)))
                        for l in range(HL):
                            e_hi, e_lo = ET_hi[:, 2 * j + l, b], ET_lo[:, 2 * j + l, b]
                            pe.matmul(dst[:, b], e_hi, U_hi[:, l, b], start=(l == 0), stop=False)
                            pe.matmul(dst[:, b], e_hi, U_lo[:, l, b], start=False, stop=False)
                            mm = pe.matmul(dst[:, b], e_lo, U_hi[:, l, b], start=False, stop=(l == HL - 1))
                        if b % HB == HB - 1:
                            mm.then_inc(s["a_ps"], 1)

                def rows(step):
                    pe.wait_ge(s["wk_split"], loop_value(step, 2, 2))
                    split_product(ps[:, ROWS_PAIR, 0], [(S_hi[:, k], S_lo[:, k]) for k in range(KC)],
                                  [(wk_hi[:, k], wk_lo[:, k]) for k in range(KC)]).then_inc(s["r_ps"], 1)

                pe.wait_ge(s["wk_split"], loop_value(i, 2, 2))
                for b in range(B):
                    if first:
                        pe.wait_ge(s["g_lo"], max(b, GM_IN_PAIR[Z_PAIR[b]]) + 1)
                    if b == 1:
                        pe.wait_ge(s["r_sum"], loop_value(i, 1, 1))
                    if b == 2:
                        pe.wait_ge(s["a_added"], loop_value(i - 1, 4, 2))
                    if b == 3:
                        pe.wait_ge(s["a_added"], loop_value(i - 1, 4, 4))
                    for m in range(KC):
                        mm = split_product(ps[:, Z_PAIR[b], m],
                                           [(G_hi[:, b, k, m * P:(m + 1) * P], G_lo[:, b, k, m * P:(m + 1) * P]) for k in range(KC)],
                                           [(wk_hi[:, k], wk_lo[:, k]) for k in range(KC)])
                    mm.then_inc(s["z_ps"], 1)
                    if first and b == 0:
                        pe.wait_ge(s["s_hi"], 3)
                        pe.wait_ge(s["s_lo"], 3)
                        pe.wait_ge(s["g_lo"], GM_IN_PAIR[ROWS_PAIR] + 1)
                        rows(i)
                pe.wait_ge(s["ones_r_done"], 1)
                pe.wait_ge(s["wo_split"], loop_value(i, 2, 2))
                pe.wait_ge(s["z_added"], loop_value(i, 2 * B, 2))
                for k in range(R):
                    for part, w in enumerate((wo_hi, wo_lo)):
                        mm = pe.matmul(ps[:, 1, 0], ones_r[:], w[:, k], start=(k == 0 and part == 0),
                                       stop=(k == R - 1 and part == 1))
                mm.then_inc(s["w_ps"], 1)
                pe.wait_ge(s["z_added"], loop_value(i, 2 * B, 4))
                pe.wait_ge(s["x_lo"], 2)
                project_wo(0)
                scores(0)
                scores(1)
                project_wo(1)
                pe.wait_ge(s["w_cp"], loop_value(i, 1, 1))
                project_wo(2)
                pe.wait_ge(s["p_lo"], loop_value(i, B, 1))
                project_wo(3)
                transpose_pair(0)
                pe.wait_ge(s["p_lo"], loop_value(i, B, 2))
                scores(2)
                scores(3)
                pe.wait_ge(s["wv_split"], loop_value(i, 2, 2))
                pe.wait_ge(s["p_lo"], loop_value(i, B, B))
                values(0)
                values(1)
                transpose_pair(1)
                pe.wait_ge(s["u_added"], loop_value(i, 2 * NG, 2))
                values(2)
                pe.wait_ge(s["u_added"], loop_value(i, 2 * NG, 4))
                values(3)
                pe.wait_ge(s["t_lo"], loop_value(i, 2, 1))
                pe.wait_ge(s["u_lo"], loop_value(i, 2 * NG, 2))
                attend(0)
                if not last:
                    pe.wait_ge(s["u_added"], loop_value(i, 2 * NG, 2 * NG))
                    rows(i + 1)
                pe.wait_ge(s["t_lo"], loop_value(i, 2, 2))
                pe.wait_ge(s["u_lo"], loop_value(i, 2 * NG, 6))
                attend(1)

            attention_step(0, True, False)
            with pe.Fori(1, STEPS - 1) as i:
                attention_step(i, False, False)
            attention_step(STEPS - 1, False, True)

            for step, h in ORDER2:
                if step == "ft":
                    transposes(claim2("ft", h), LN_FFN2, h, s["ft_ps"])
                elif step.startswith("gu"):
                    step_gu(1, h, int(step[2:]), claim2(step, h))
                elif step == "dna":
                    step_dn(1, h, claim2("dna", h))

        @block.vector
        def _(dve):
            def layer_norm(kind, batches, arrive):
                for b in batches:
                    arrive(b)
                    tiles = slice(R * b, R * (b + 1))
                    for t in range(R):
                        dve.bn_stats(stats[:, R * b + t], X[:, R * b + t]).then_inc(s["ln_stat"], 1)
                    for t in range(R):
                        dve.wait_ge(s["ln_stat"], NT * kind + R * b + t + 1)
                        dve.bn_aggr(agg[:, R * b + t], stats[:, R * b + t]).then_inc(s["ln_agg"], 1)
                    dve.wait_ge(s["ln_agg"], NT * kind + R * (b + 1))
                    dve.tensor_scalar(var_eps[:, tiles], agg[:, tiles, 1], EPS, None, ALU.add).then_inc(s["ln_eps"], 1)
                for b in batches:
                    dve.wait_ge(s["ln_rstd"], B * kind + b + 1)
                    for t in range(R * b, R * (b + 1)):
                        op = dve.tensor_scalar(XN[:, t, 0:C], X[:, t], agg[:, t, 0:1], rstd[:, t:t + 1], ALU.subtract, ALU.mult)
                    op.then_inc(s["ln_done"], 1)

            def loaded(b):
                dve.wait_ge(s[("x0_in", "x1_in", "x23_in", "x23_in")[b]], 16)

            def add_recurrence(b):
                dve.wait_ge(s["wo_ps"], b + 1)
                x_b = X[:, R * b:R * (b + 1)]
                dve.tensor_tensor(x_b, x_b, bank_pair("wo", b // HB)[:, b % HB].rearrange("p (t c) -> p t c", c=C),
                                  ALU.add).then_inc(s["rec_added"], 1)
                dve.wait_ge(s["rec_added"], b + 1)

            def step_xt(h):
                for m in range(KC):
                    dve.wait_ge(s["xt_hi"], upto(h, m))
                    if h:
                        dve.wait_ge(s["q_ps"], upto(0, 1))
                    dve.tensor_tensor(in_time(XTl[:, m]), by_tile(bank_pair("xt", h)[:, m]), in_time(XTh[:, m]).bitcast(F32),
                                      ALU.subtract).then_inc(s["xt_lo"], 1)

            def step_conv(h):
                if h:
                    dve.wait_ge(s["xc_hi"], upto(0, 1))
                    dve.wait_ge(s["xc_lo"], upto(0, 1))
                conv = (s["conv_m0"], s["conv_m1"])
                for shift in range(TAPS):
                    for m in range(KC):
                        if shift == 0:
                            dve.wait_ge(s["xt_f"], upto(h, m))
                        tap = vecs[:, m, V_TAP + TAPS - 1 - shift:V_TAP + TAPS - shift]
                        src = XTf[:, m].rearrange("p (b t) -> p b t", b=HB)[:, :, 0:T - shift]
                        dst = XCf[:, m].rearrange("p (b t) -> p b t", b=HB)[:, :, shift:T]
                        if shift == 0:
                            dve.tensor_scalar(XCf[:, m], XTf[:, m], tap, None, ALU.mult).then_inc(conv[m], 1)
                        else:
                            dve.wait_ge(conv[m], TAPS * h + shift)
                            dve.scalar_tensor_tensor(out=dst, in0=src, scalar=tap, in1=dst, op0=ALU.mult,
                                                     op1=ALU.add).then_inc(conv[m], 1)

            def step_silu(h):
                if h:
                    dve.wait_ge(s["og_ps"], upto(0, 1))
                for m in range(KC):
                    dve.wait_ge(s["silu_done"], upto(h, m))
                    dve.wait_ge(s["xc_hi"], upto(h, m))
                    dve.tensor_tensor(XCl[:, m], XCf[:, m], XCh[:, m].bitcast(F32), ALU.subtract).then_inc(s["xc_lo"], 1)

            def norm_guard(name, h, sq, done):
                for m in range(KC):
                    dve.wait_ge(s[name + "_ps"], upto(h, m))
                    dve.tensor_scalar(sq[:, h, m], bank_pair(name, h)[:, m], 1e-24, None, ALU.max).then_inc(done, 1)

            def times(out, a, b, h, done, *ready):
                for m in range(KC):
                    for r in ready:
                        dve.wait_ge(r, upto(h, m))
                    dve.tensor_tensor(out[:, m], a[:, m], b[:, m], ALU.mult).then_inc(done, 1)

            def affine(t, h, gain, bias, done, ready):
                for m in range(KC):
                    dve.wait_ge(ready, upto(h, m))
                    dve.tensor_scalar(t[:, h, m], t[:, h, m], vecs[:, m, gain:gain + 1], vecs[:, m, bias:bias + 1],
                                      ALU.mult, ALU.add).then_inc(done, 1)

            def one_plus_times(t, g, h, done, *ready):
                for m in range(KC):
                    for r in ready:
                        dve.wait_ge(r, upto(h, m))
                    dve.scalar_tensor_tensor(out=t[:, h, m], in0=g[:, h, m], scalar=1.0, in1=t[:, h, m], op0=ALU.add,
                                             op1=ALU.mult).then_inc(done, 1)

            def step_rk(h):
                times(k_t[:, h], k_t[:, h], sq_k[:, h], h, s["k_n"], s["k_cp"], s["rk_done"])
                times(v_t[:, h], v_t[:, h], sq_v[:, h], h, s["v_n"], s["v_cp"], s["rv_done"])
                dve.wait_ge(s["vec_half"], 1)
                affine(v_t, h, V_VN_G, V_VN_B, s["v_a"], s["v_n"])

            def step_scan(h):
                one_plus_times(k_t, t_ig, h, s["k_g"], s["ti_done"], s["k_n"])
                times(k_t[:, h], k_t[:, h], v_t[:, h], h, s["b_done"], s["k_g"], s["v_a"])
                for m in range(KC):
                    dve.wait_ge(s["tg_done"], upto(h, m))
                    dve.tensor_scalar(t_ga[:, h, m], t_ga[:, h, m], 0.5, 0.5, ALU.mult, ALU.add).then_inc(s["gamma_done"], 1)
                for m in range(KC):
                    dve.wait_ge(s["b_done"], upto(h, m))
                    dve.wait_ge(s["gamma_done"], upto(h, m))
                    for b in range(HB):
                        span = slice(b * T, (b + 1) * T)
                        dve.tensor_tensor_scan(mem[:, h, m, span], t_ga[:, h, m, span], k_t[:, h, m, span], 0.0,
                                               ALU.mult, ALU.add).then_inc(s["mem_done"], 1)

            def step_mv(h):
                times(v_t[:, h], bank_pair("mc", h), sq_v[:, h], h, s["y_n"], s["r1_done"])
                affine(v_t, h, V_MN_G, V_MN_B, s["y_a"], s["y_n"])
                times(v_t[:, h], v_t[:, h], q_t[:, h], h, s["o_done"], s["y_a"], s["qn_done"])

            def step_ov(h):
                times(k_t[:, h], bank_pair("oc", h), sq_q[:, h], h, s["z_n"], s["r2_done"])
                affine(k_t, h, V_GN_G, V_GN_B, s["z_a"], s["z_n"])
                one_plus_times(k_t, t_og, h, s["z_done"], s["z_a"], s["to_done"])

            def step_ft(f, h, psum):
                w, n = ffn[f], 2 * f + h
                for m in range(KC):
                    dve.wait_ge(s["ft_hi"], upto(n, m))
                    dve.tensor_tensor(in_time(w.XTl[h][:, m]), by_tile(psum[:, m]), in_time(w.XTh[h][:, m]).bitcast(F32),
                                      ALU.subtract).then_inc(s["ft_lo"], 1)

            def step_gu(f, h, c, psum):
                w, n, at = ffn[f], 2 * f + h, gu_before(f, h) + c
                rows = rows_of(c)
                up = psum[0:P, 1] if c < FULL else psum[REST:P, 0]
                dve.wait_ge(s["silu_g"], at + 1)
                if c >= 4:
                    dve.wait_ge(s["hd_lo"], FULL * n + c - 3)
                elif h:
                    if c == 3:
                        dve.wait_ge(s["hd_lo_last"], n)
                    else:
                        dve.wait_ge(s["hd_lo"], FULL * (n - 1) + c + 3)
                dve.tensor_tensor(w.HD[at % 4][0:rows], up, w.SG[0:rows, at % 2], ALU.mult).then_inc(s["hd_done"], 1)
                if c == FULL:
                    dve.wait_ge(s["hd_hi"], FCH * (n + 1))
                    dve.tensor_tensor(w.HDl[0:rows, c], w.HD[at % 4][0:rows], w.HDh[0:rows, c].bitcast(F32),
                                      ALU.subtract).then_inc(s["hd_lo_last"], 1)

            def step_dn(f, h, j, pair_):
                b = HB * h + j
                dve.wait_ge(s["dn_ps"], B * f + b + 1)
                dve.tensor_tensor(X[:, R * b:R * (b + 1)], X[:, R * b:R * (b + 1)],
                                  pair_[:, j].rearrange("p (t c) -> p t c", c=C), ALU.add).then_inc(s["ffn_added"], 1)

            def ffn_added(b):
                dve.wait_ge(s["ffn_added"], b + 1)

            def step_lc(n):
                layer_norm(LN_CHAN, batches_of_lc(n), ffn_added)
                dve.wait_ge(s["bo_in"], 16)
                for b in batches_of_lc(n):
                    dve.wait_ge(s["ln_done"], B * LN_CHAN + b + 1)
                    x_b = X[:, R * b:R * (b + 1)]
                    dve.tensor_tensor(x_b, x_b, bo_b[:].unsqueeze(1).to_broadcast([P, R, C]), ALU.add).then_inc(s["bo_added"], 1)

            def split_xn(h):
                tiles = slice(HT * h, HT * (h + 1))
                dve.tensor_copy(XH[:, tiles], XN[:, tiles, 0:C]).then_inc(s["x_hi"], 1)
                dve.wait_ge(s["x_hi"], h + 1)
                dve.tensor_tensor(XL[:, tiles], XN[:, tiles, 0:C], XH[:, tiles].bitcast(F32), ALU.subtract).then_inc(s["x_lo"], 1)

            def step_gm(b):
                dve.wait_ge(s["g_hi"], b + 1)
                dve.tensor_copy(S_col[:, :, b:b + 1], bank_pair("gm", b)[:, :, C:C + 1]).then_inc(s["s_cp"], 1)
                if b == B - 1:
                    split_sums()
                dve.tensor_tensor(G_lo[:, b], bank_pair("gm", b)[:, :, 0:C], G_hi[:, b].bitcast(F32), ALU.subtract).then_inc(s["g_lo"], 1)

            def constants():
                for part in (S_hi, S_lo):
                    for k in range(KC):
                        dve.tensor_scalar(part[:, k], ident[:], 0.0, 0.0, ALU.mult, ALU.add).then_inc(s["s_zero"], 1)
                for q in range(3):
                    dve.tensor_copy(mask[32 * q:32 * q + 32], ident[32 * q:32 * q + 32, 32 * q:32 * q + B]).then_inc(s["mask_done"], 1)
                dve.tensor_scalar(ones_r[:], ident[:], 0.0, 1.0, ALU.mult, ALU.add).then_inc(s["ones_r_done"], 1)

            def split_sums():
                dve.wait_ge(s["s_cp"], B)
                dve.wait_ge(s["s_zero"], 2 * KC)
                for q in range(3):
                    dve.tensor_copy(S_hi[:, :, 32 * q:32 * q + B], S_col[:]).then_inc(s["s_hi"], 1)
                for q in range(3):
                    cols = slice(32 * q, 32 * q + B)
                    dve.wait_ge(s["s_hi"], q + 1)
                    dve.tensor_tensor(S_lo[:, :, cols], S_col[:], S_hi[:, :, cols].bitcast(F32), ALU.subtract).then_inc(s["s_lo"], 1)

            def split(raw, hi, lo, got, done, free, step):
                dve.wait_ge(got, 16 * (step + 1))
                dve.tensor_copy(hi[:], raw[:]).then_inc(done, 1)
                dve.wait_ge(done, loop_value(step, 2, 1))
                dve.tensor_tensor(lo[:], raw[:], hi[:].bitcast(F32), ALU.subtract).then_inc(done, 1)
                dve.wait_ge(done, loop_value(step, 2, 2))
                dve.sem_inc(free, 1)

            def split_wk(step):
                split(raw_k, wk_hi, wk_lo, s["wk_in"], s["wk_split"], s["raw_k_free"], step)

            def split_wo(step):
                split(raw_o, wo_hi, wo_lo, s["wo_in"], s["wo_split"], s["raw_o_free"], step)

            def split_wv(step):
                split(raw_v, wv_hi, wv_lo, s["wv_in"], s["wv_split"], s["raw_v_free"], step)

            for sm, per in ((s["raw_k_free"], 1), (s["raw_o_free"], 1), (s["raw_v_free"], 1), (s["bq_raw_free"], 1),
                            (s["wk_split"], 2), (s["wo_split"], 2), (s["wv_split"], 2), (s["bq_split"], 2), (s["r_sum"], 1),
                            (s["z_added"], 2 * B), (s["negmax"], NG), (s["bias_done"], NG), (s["rsum"], NG), (s["e_norm"], NG),
                            (s["p_lo"], B), (s["t_lo"], 2), (s["u_added"], 2 * NG), (s["u_lo"], 2 * NG), (s["a_added"], 4)):
                dve.sem_inc(sm, per)
            def split_weights(block_, nth):
                dve.wait_ge(s["rec_hi"], nth + 1)
                dve.tensor_tensor(w_lo[:, :, block_], w_raw[:, :, block_], w_hi[:, :, block_].bitcast(F32),
                                  ALU.subtract).then_inc(s["rec_split"], 1)

            def scale_down_weights():
                dve.wait_ge(s["w_dn_in"], 32)
                dve.wait_ge(s["scale_in"], 16)
                dve.wait_ge(s["down_s_in"], 16)
                for c in range(FCH):
                    rows = rows_of(c)
                    op = dve.scalar_tensor_tensor(
                        out=w_down[0:rows, c], in0=w_down[0:rows, c], scalar=f_scale[0:rows, FCH + c:FCH + c + 1],
                        in1=down_b[0:rows], op0=ALU.mult, op1=ALU.mult)
                    if c >= FULL - 1:
                        op.then_inc(s["dn_scaled"], 1)

            dve.memset(XN[:, :, C:C + 2], 1.0).then_inc(s["consts_dve"], 1)
            layer_norm(LN_X, half_batches(0), loaded)
            dve.wait_ge(s["w_kv_in"], 16)
            for k in range(KC):
                dve.tensor_reduce(msum[:, k], w_raw[:, k, W_V].rearrange("p (h d) -> p h d", d=D), AX.X,
                                  ALU.add).then_inc(s["centred"], 1)
            dve.wait_ge(s["w_gamma_in"], 16)
            for k in range(KC):
                dve.tensor_copy(w_raw[:, k, W_GAMMA].rearrange("p (h d) -> p h d", d=D),
                                gam[:, k].unsqueeze(2).to_broadcast([P, H, D])).then_inc(s["gamma_rep"], 1)
            dve.wait_ge(s["centred"], 2)
            for k in range(KC):
                v3 = w_raw[:, k, W_V].rearrange("p (h d) -> p h d", d=D)
                dve.scalar_tensor_tensor(out=v3, in0=msum[:, k].unsqueeze(2).to_broadcast([P, H, D]), scalar=-1.0 / D,
                                         in1=v3, op0=ALU.mult, op1=ALU.add).then_inc(s["centred"], 1)
            split_weights(W_K, 0)
            for step, h in ORDER:
                if step == "xt":
                    step_xt(h)
                    if h == 0:
                        dve.wait_ge(s["vec_in"], 16)
                        dve.tensor_scalar(vecs[:, :, V_IG_B:V_VN_B + 1], vecs[:, :, V_IG_B:V_VN_B + 1], 0.5, None, ALU.mult)
                        dve.tensor_scalar(vecs[:, :, V_GN_G:V_GN_B + 1], vecs[:, :, V_GN_G:V_GN_B + 1], 0.5, None,
                                          ALU.mult).then_inc(s["vec_half"], 1)
                elif step == "conv":
                    if h == 0:
                        split_weights(W_V, 1)
                        split_weights(W_Q, 2)
                    step_conv(h)
                    if h == 0:
                        for nth, block_ in ((3, W_IG), (4, W_OG), (5, W_GAMMA)):
                            split_weights(block_, nth)
                        dve.wait_ge(s["consts_pool"], 7)
                        dve.scalar_tensor_tensor(out=centre[:], in0=heads_ones[:], scalar=-1.0 / D, in1=ident[:],
                                                 op0=ALU.mult, op1=ALU.add).then_inc(s["consts_dve"], 1)
                elif step == "lx":
                    layer_norm(LN_X, half_batches(h), loaded)
                elif step == "silu":
                    step_silu(h)
                elif step == "nk":
                    norm_guard("nk", h, sq_k, s["nk_max"])
                elif step == "nq":
                    norm_guard("nq", h, sq_q, s["nq_max"])
                elif step == "rk":
                    step_rk(h)
                elif step == "scan":
                    step_scan(h)
                elif step == "mv":
                    step_mv(h)
                elif step == "ov":
                    step_ov(h)
                elif step == "ln":
                    layer_norm(LN_FFN, half_batches(h), add_recurrence)
                elif step == "ft":
                    step_ft(0, h, bank_pair("ft", h))
                elif step.startswith("gu"):
                    step_gu(0, h, int(step[2:]), bank_pair(step, h))
                    if (step, h) == ("gu0", 0):
                        scale_down_weights()
                    elif (step, h) == ("gu2", 1):
                        split_xn(0)
                    elif (step, h) == ("gu3", 1):
                        split_wk(0)
                    elif (step, h) == ("gu1", 1):
                        constants()
                    elif (step, h) == ("gu5", 1):
                        split_wo(0)
                elif step in ("dna", "dnb"):
                    step_dn(0, h, int(step == "dnb"), bank_pair("dna", h))
                elif step == "lc":
                    step_lc(h)
                elif step == "gm":
                    step_gm(h)

            split_xn(1)
            dve.wait_ge(s["bv_in"], 16)

            def add_out(i, j, half):
                dve.wait_ge(s["a_ps"], loop_value(i, 4, 2 * j + half + 1))
                dst = X[:].rearrange("p (b r) c -> p b r c", r=R)[:, HB * half:HB * (half + 1), j]
                dve.tensor_tensor(dst, dst, ps[:, A_PAIR[j], half].rearrange("p (b c) -> p b c", c=C),
                                  ALU.add).then_inc(s["a_added"], 1)

            def attention_step(i, last):
                def softmax_bias(g):
                    dve.wait_ge(s["s_ps"], loop_value(i, NG, g + 1))
                    dve.wait_ge(s["exp_done"], loop_value(i, NG * B, (g - 1) * B))
                    dve.tensor_reduce(neg[:, g % 2], ps[:, S_PAIR[g // 2], g % 2].rearrange("p (b n) -> p b n", b=B),
                                      AX.X, ALU.max, negate=True).then_inc(s["negmax"], 1)
                    dve.wait_ge(s["negmax"], loop_value(i, NG, g + 1))
                    dve.tensor_scalar(e_bias[:, g % 2], neg[:, g % 2], SCALE, None, ALU.mult).then_inc(s["bias_done"], 1)

                def softmax_norm(g):
                    j = g % 2
                    dve.wait_ge(s["exp_done"], loop_value(i, NG * B, (g + 1) * B))
                    dve.reciprocal(e_inv[:, j], e_sum[:, j]).then_inc(s["rsum"], 1)
                    dve.wait_ge(s["rsum"], loop_value(i, NG, g + 1))
                    dve.tensor_tensor(E[:, j], E[:, j], e_inv[:, j].unsqueeze(2).to_broadcast([P, B, NQ]),
                                      ALU.mult).then_inc(s["e_norm"], 1)

                def add_values_bias(g):
                    dve.wait_ge(s["s_ps"], loop_value(i, NG, NG))
                    dve.wait_ge(s["u_lo"], loop_value(i, 2 * NG, 4 * (g // 2)))
                    if g == 0:
                        dve.wait_ge(s["w_cp"], loop_value(i, 1, 1))
                    for j in range(2):
                        dve.wait_ge(s["u_ps"], loop_value(i, 2 * NG, 2 * g + j + 1))
                        dve.scalar_tensor_tensor(
                            out=U[:, g % 2, 2 * j:2 * j + 2], in0=w_sum[:, g % HL].unsqueeze(1).to_broadcast([P, 2, C]),
                            scalar=bv_c[:, bass.ds(i * NG + g, 1)],
                            in1=ps[:, U_PAIR[g], j].rearrange("p (b c) -> p b c", b=2), op0=ALU.mult,
                            op1=ALU.add).then_inc(s["u_added"], 1)

                def split_values(n):
                    for j in range(2):
                        part = slice(2 * j, 2 * j + 2)
                        for l in range(2):
                            dve.wait_ge(s["u_hi"], loop_value(i, 2 * NG, 4 * n + 2 * j + l + 1))
                            dve.tensor_tensor(U_lo[:, l, part], U[:, l, part], U_hi[:, l, part].bitcast(F32),
                                              ALU.subtract).then_inc(s["u_lo"], 1)

                def split_transposed(j):
                    dve.wait_ge(s["s_ps"], loop_value(i, NG, NG))
                    dve.wait_ge(s["t_hi"], loop_value(i, 2, j + 1))
                    heads = slice(2 * j, 2 * j + 2)
                    dve.tensor_tensor(ET_lo[:, heads].rearrange("p g b n -> p g (b n)"), ps[:, T_PAIR[j]],
                                      ET_hi[:, heads].rearrange("p g b n -> p g (b n)").bitcast(F32),
                                      ALU.subtract).then_inc(s["t_lo"], 1)

                dve.wait_ge(s["bk_in"], 16 * (i + 1))
                dve.wait_ge(s["r_ps"], loop_value(i, 1, 1))
                dve.wait_ge(s["r_mask"], loop_value(i - 1, 1, 1))
                dve.scalar_tensor_tensor(out=r_row[:], in0=bk_b[:], scalar=float(T), in1=ps[:, ROWS_PAIR, 0], op0=ALU.mult,
                                         op1=ALU.add).then_inc(s["r_sum"], 1)
                dve.wait_ge(s["bq_in"], 16 * (i + 1))
                dve.tensor_copy(bq_s[:], bq_b[:]).then_inc(s["bq_split"], 1)
                dve.wait_ge(s["bq_split"], loop_value(i, 2, 1))
                dve.tensor_tensor(bq_s[64:96], bq_b[64:96], bq_s[64:96].bitcast(F32), ALU.subtract).then_inc(s["bq_split"], 1)
                dve.wait_ge(s["bq_split"], loop_value(i, 2, 2))
                dve.sem_inc(s["bq_raw_free"], 1)
                for b in range(B):
                    dve.wait_ge(s["z_ps"], loop_value(i, B, b + 1))
                    for m in range(KC):
                        dve.scalar_tensor_tensor(out=Z[:, m, b], in0=bk_b[:], scalar=S_col[:, m, b:b + 1],
                                                 in1=ps[:, Z_PAIR[b], m], op0=ALU.mult, op1=ALU.add).then_inc(s["z_added"], 1)
                def split_p(b):
                    dve.wait_ge(s["p_hi"], loop_value(i, B, b + 1))
                    dve.tensor_tensor(P_lo[:, :, b].rearrange("p m l c -> p m (l c)"), ps[:, P_PAIR[b]],
                                      P_hi[:, :, b].rearrange("p m l c -> p m (l c)").bitcast(F32),
                                      ALU.subtract).then_inc(s["p_lo"], 1)

                split_wv(i)
                split_p(0)
                softmax_bias(0)
                softmax_bias(1)
                softmax_norm(0)
                softmax_norm(1)
                for b in range(1, B):
                    split_p(b)
                softmax_bias(2)
                softmax_bias(3)
                split_transposed(0)
                softmax_norm(2)
                softmax_norm(3)
                add_values_bias(0)
                add_values_bias(1)
                split_values(0)
                split_transposed(1)
                add_values_bias(2)
                add_values_bias(3)
                add_out(i, 0, 0)
                split_values(1)
                add_out(i, 0, 1)
                if not last:
                    add_out(i, 1, 0)
                    add_out(i, 1, 1)

            with dve.Fori(0, STEPS - 1) as i:
                attention_step(i, False)
            attention_step(STEPS - 1, True)

            def add_last_out(b):
                half = b // HB
                if b % HB == 0:
                    add_out(STEPS - 1, 1, half)
                    dve.wait_ge(s["a_added"], loop_value(STEPS - 1, 4, 2 + half + 1))

            for step, h in ORDER2:
                if step == "ln":
                    layer_norm(LN_FFN2, half_batches(h), add_last_out)
                elif step == "ft":
                    step_ft(1, h, bank_pair2("ft", h))
                elif step.startswith("gu"):
                    step_gu(1, h, int(step[2:]), bank_pair2(step, h))
                elif step in ("dna", "dnb"):
                    step_dn(1, h, int(step == "dnb"), bank_pair2("dna", h))


ROWS_PAIR = 2
Z_PAIR = [1, 2, 3, 0]
P_PAIR = [2, 0, 1, 2]
S_PAIR = [3, 0]
T_PAIR = [3, 0]
U_PAIR = [1, 2, 1, 2]
A_PAIR = [3, 0]
GM_IN_PAIR = {pair_plan(ORDER)[0]["gm", b]: b for b in range(B)}


def kernel(**inputs):
    import numpy as np
    import concourse.bacc as bacc
    from concourse.bass_utils import run_bass_kernel_spmd as run

    a = {n: np.asarray(v) for n, v in inputs.items()}
    rec = {n[len("L0_attn_a_"):]: v for n, v in a.items() if n.startswith("L0_attn_a_")}
    att = {n[len("L0_attn_b_"):]: v for n, v in a.items() if n.startswith("L0_attn_b_")}
    ff = {n[len("L0_ffn_"):]: v for n, v in a.items() if n.startswith("L0_ffn_")}

    def col(v):
        return v.reshape(-1, 1)

    vec = np.concatenate(
        [rec["conv_w"].reshape(C, TAPS), col(rec["conv_b"]), col(rec["ig_b"]), col(np.repeat(rec["gamma_b"], D)),
         col(rec["og_b"]), col(np.tile(rec["vn_g"], H)), col(np.tile(rec["vn_b"], H)), col(np.tile(rec["mn_g"], H)),
         col(np.tile(rec["mn_b"], H)), col(rec["gn_g"]), col(rec["gn_b"])], axis=1)
    w_rec = np.stack([rec[n].T for n in ("Wk", "Wv", "Wq", "ig_w", "og_w")], axis=1)

    gate_up = [ff[n].T for n in ("gate_w", "up_w")]
    w_gu = np.concatenate([w[:, c * P:(c + 1) * P] for c in range(FCH) for w in gate_up], axis=1)

    def chunk_cols(v):
        return np.concatenate([v, np.zeros(FCH * P - INTER, v.dtype)]).reshape(FCH, P).T

    ffn_scale = np.concatenate([chunk_cols(ff["gate_s"]), chunk_cols(ff["up_s"])], axis=1)

    heads = np.array([[r * Y_BLOCKS + i * HL + l for r in range(2) for l in range(HL)] for i in range(STEPS)])

    def by_step(w):
        w = w.reshape(-1, NQ, NH)[:, :, heads]
        return w.transpose(2, 0, 3, 1).reshape(STEPS, -1, NG * NQ)

    wo = att["Wo"].reshape(STEPS, HL, T, C).transpose(0, 2, 1, 3).reshape(STEPS, T, HL * C)
    arrays = {
        "x": a["L0_attn_a_x"], "w_rec": w_rec, "w_gamma": rec["gamma_w"].T, "w_rec_out": rec["Wo"].T, "vec": vec,
        "w_gu": w_gu, "w_dn": ff["down_w"].T, "ffn_scale": ffn_scale, "down_s": ff["down_s"],
        "wk": by_step(att["Wk"]), "wv": by_step(att["Wv"]), "wq": by_step(att["Wq"]), "wo": wo,
        "bk": by_step(att["bk"][None])[:, 0], "bq": by_step(att["bq"][None])[:, 0],
        "bv": by_step(att["bv"][None])[:, 0].reshape(NH, NQ).T, "bo": att["bo"],
    }
    nc = bacc.Bacc("TRN2", target_bir_lowering=False, num_devices=1)
    arrays = {n: np.ascontiguousarray(v) for n, v in arrays.items()}
    args = [nc.dram_tensor(n, v.shape, mybir.dt.from_np(v.dtype), kind="ExternalInput").ap() for n, v in arrays.items()]
    args.append(nc.dram_tensor("y", (B, T, C), F32, kind="ExternalOutput").ap())
    hybrid_block(nc, *args)
    r = run(nc, [arrays], core_ids=[0])
    return r.results[0]["y"]
```
